# Optimizing a Trainium2 kernel written in Bass

```python
import numpy as np
import jax
import jax.numpy as jnp

def _softmax(x, axis=-1):
    return jax.nn.softmax(x, axis=axis)

def _gelu(x):
    return jax.nn.gelu(x, approximate=True)

def _silu(x):
    return jax.nn.silu(x)

def _sigmoid(x):
    return jax.nn.sigmoid(x)

def _layernorm(x, axis=-1, eps=1e-05):
    m = jnp.mean(x, axis=axis, keepdims=True)
    v = jnp.var(x, axis=axis, keepdims=True)
    return (x - m) / jnp.sqrt(v + eps)

def _scatter_add(tgt, idx, src, axis=0):
    return tgt.at[idx].add(src)

def _segment_sum(src, seg, n):
    return jax.ops.segment_sum(src, seg, n)
kernel_name = 'mk_decoder_preln_d1_seqx_r4_34b5cd'

def setup_inputs(seed: int=0):
    np.random.seed(seed)
    _w = jnp.asarray

    def _rec_inputs():
        import jax
        import jax.numpy as jnp
        _rk = jax.random.key(seed)
        x = 7.22e-05 + 1 * jax.random.normal(jax.random.fold_in(_rk, 1), (8, 512, 256), jnp.float32)
        _lenS = 512 - jax.random.randint(jax.random.fold_in(_rk, 7), (8,), 0, max(1, 512 // 4) + 1, jnp.int32)
        _lenS2 = 512 - jax.random.randint(jax.random.fold_in(_rk, 8), (8,), 0, max(1, 512 // 4) + 1, jnp.int32)
        _ctx_768P = jax.random.normal(jax.random.fold_in(_rk, 11), (8, 16, 192), jnp.float32)
        _ctx_768c = jax.random.dirichlet(jax.random.fold_in(_rk, 511), 0.3 * jnp.ones((16,), jnp.float32), (8, 512))
        _ctx_768t = jnp.einsum('bsk,bkd->bsd', _ctx_768c, _ctx_768P)
        _ctx_768t = _ctx_768t * jax.lax.rsqrt(jnp.mean(jnp.square(_ctx_768t)) + 1e-12) * 0.953939
        ctx_768 = -0.000191848 + 0.999787 * (_ctx_768t + 0.3 * jax.random.normal(jax.random.fold_in(_rk, 611), (8, 512, 192), jnp.float32))
        return (x, ctx_768)
    x, ctx_768 = _rec_inputs()

    def _L0_attn_setup():
        import jax, jax.numpy as jnp
        import numpy as np
        NUM_HEADS = 16
        key = jax.random.key(seed)
        ks = jax.random.split(key, 5)
        B, N, C = (2, 512, 256)
        x = jax.random.normal(ks[0], (B, N, C), dtype=jnp.float32)
        s_in = 1.0 / np.sqrt(C)
        Wq = jax.random.normal(ks[1], (C, 2 * C), dtype=jnp.float32) * s_in
        Wk = jax.random.normal(ks[2], (C, 2 * C), dtype=jnp.float32) * s_in
        Wv = jax.random.normal(ks[3], (C, 2 * C), dtype=jnp.float32) * s_in
        Wo = jax.random.normal(ks[4], (2 * C, C), dtype=jnp.float32) * (1.0 / np.sqrt(2 * C))
        return {'x': x, 'Wq': Wq, 'Wk': Wk, 'Wv': Wv, 'Wo': Wo}
    _L0_attn_all = _L0_attn_setup()
    _L0_attn_in = {k: v for k, v in _L0_attn_all.items() if k in ('Wq', 'Wk', 'Wv', 'Wo')}
    del _L0_attn_all

    def _L0_xattn_setup():
        import jax, jax.numpy as jnp
        import numpy as np
        NUM_HEADS = 16
        CLAMP = 10000.0
        key = jax.random.key(seed)
        ks = jax.random.split(key, 8)
        B, Nq, Nkv, Cq, Ckv = (4, 512, 512, 256, 192)
        s_q = 1.0 / np.sqrt(Cq)
        s_kv = 1.0 / np.sqrt(Ckv)
        return {'query': jax.random.normal(ks[0], (B, Nq, Cq), jnp.float32), 'key_value': jax.random.normal(ks[1], (B, Nkv, Ckv), jnp.float32), 'Wq': jax.random.normal(ks[2], (Cq, Cq), jnp.float32) * s_q, 'bq': jnp.zeros((Cq,), jnp.float32), 'Wk': jax.random.normal(ks[3], (Ckv, Cq), jnp.float32) * s_kv, 'bk': jnp.zeros((Cq,), jnp.float32), 'Wv': jax.random.normal(ks[4], (Ckv, Cq), jnp.float32) * s_kv, 'bv': jnp.zeros((Cq,), jnp.float32), 'Wo': jax.random.normal(ks[5], (Cq, Cq), jnp.float32) * s_q, 'bo': jnp.zeros((Cq,), jnp.float32)}
    _L0_xattn_all = _L0_xattn_setup()
    _L0_xattn_in = {k: v for k, v in _L0_xattn_all.items() if k in ('Wq', 'bq', 'Wk', 'bk', 'Wv', 'bv', 'Wo', 'bo')}
    del _L0_xattn_all

    def _L0_ffn_setup():
        import jax, jax.numpy as jnp
        import numpy as np
        B, S, H = (4, 512, 256)
        E = 8
        GS = 2
        NG = E // GS
        F = int(H * 4 * (2.0 / 3.0))
        key = jax.random.key(seed)
        ks = jax.random.split(key, 7)
        sc_h = 1.0 / np.sqrt(H)
        sc_f = 1.0 / np.sqrt(F)
        return {'x': jax.random.normal(ks[0], (B, S, H), dtype=jnp.float32), 'Wr': jax.random.normal(ks[1], (H, E), dtype=jnp.float32) * sc_h, 'br': jnp.zeros((E,), dtype=jnp.float32), 'W_up': jax.random.normal(ks[2], (NG, H, F), dtype=jnp.float32) * sc_h, 'b_up': jax.random.normal(ks[3], (NG, F), dtype=jnp.float32) * 0.01, 'W_down': jax.random.normal(ks[4], (E, F, H), dtype=jnp.float32) * sc_f, 'b_down': jax.random.normal(ks[5], (E, H), dtype=jnp.float32) * 0.01}
    _L0_ffn_all = _L0_ffn_setup()
    _L0_ffn_in = {k: v for k, v in _L0_ffn_all.items() if k in ('Wr', 'br', 'W_up', 'b_up', 'W_down', 'b_down')}
    del _L0_ffn_all
    return {'x': x, 'ctx_768': ctx_768, 'L0_attn_Wq': _L0_attn_in['Wq'], 'L0_attn_Wk': _L0_attn_in['Wk'], 'L0_attn_Wv': _L0_attn_in['Wv'], 'L0_attn_Wo': _L0_attn_in['Wo'], 'L0_xattn_Wq': _L0_xattn_in['Wq'], 'L0_xattn_bq': _L0_xattn_in['bq'], 'L0_xattn_Wk': _L0_xattn_in['Wk'], 'L0_xattn_bk': _L0_xattn_in['bk'], 'L0_xattn_Wv': _L0_xattn_in['Wv'], 'L0_xattn_bv': _L0_xattn_in['bv'], 'L0_xattn_Wo': _L0_xattn_in['Wo'], 'L0_xattn_bo': _L0_xattn_in['bo'], 'L0_ffn_Wr': _L0_ffn_in['Wr'], 'L0_ffn_br': _L0_ffn_in['br'], 'L0_ffn_W_up': _L0_ffn_in['W_up'], 'L0_ffn_b_up': _L0_ffn_in['b_up'], 'L0_ffn_W_down': _L0_ffn_in['W_down'], 'L0_ffn_b_down': _L0_ffn_in['b_down']}

def reference(x, ctx_768, L0_attn_Wq, L0_attn_Wk, L0_attn_Wv, L0_attn_Wo, L0_xattn_Wq, L0_xattn_bq, L0_xattn_Wk, L0_xattn_bk, L0_xattn_Wv, L0_xattn_bv, L0_xattn_Wo, L0_xattn_bo, L0_ffn_Wr, L0_ffn_br, L0_ffn_W_up, L0_ffn_b_up, L0_ffn_W_down, L0_ffn_b_down):
    import jax
    import jax.numpy as jnp

    def _L0_attn_ref(x, Wq, Wk, Wv, Wo):
        import jax, jax.numpy as jnp
        import numpy as np
        NUM_HEADS = 16
        B, N, C = x.shape
        H = NUM_HEADS
        hd = C // H

        def proj(W):
            return (x @ W).reshape(B, N, H, 2 * hd).transpose(0, 2, 1, 3)
        q = proj(Wq)
        k = proj(Wk)
        v = proj(Wv)
        q_r, q_i = (q[..., :hd], q[..., hd:])
        k_r, k_i = (k[..., :hd], k[..., hd:])
        v_r, v_i = (v[..., :hd], v[..., hd:])
        scores = (jnp.einsum('bhnd,bhmd->bhnm', q_r, k_r) + jnp.einsum('bhnd,bhmd->bhnm', q_i, k_i)) / jnp.sqrt(jnp.float32(hd))
        causal = jnp.tril(jnp.ones((N, N), dtype=bool))
        scores = jnp.where(causal[None, None], scores, -jnp.inf)
        probs = jax.nn.softmax(scores, axis=-1)
        out_r = jnp.einsum('bhnm,bhmd->bhnd', probs, v_r)
        out_i = jnp.einsum('bhnm,bhmd->bhnd', probs, v_i)
        out = jnp.concatenate([out_r, out_i], axis=-1)
        out = out.transpose(0, 2, 1, 3).reshape(B, N, 2 * C)
        return out @ Wo

    def _L0_xattn_ref(query, key_value, Wq, bq, Wk, bk, Wv, bv, Wo, bo):
        import jax, jax.numpy as jnp
        import numpy as np
        NUM_HEADS = 16
        CLAMP = 10000.0
        B, Nq, Cq = query.shape
        Nkv = key_value.shape[1]
        H = NUM_HEADS
        D = Cq // H
        scale = D ** (-0.5)
        q = (query @ Wq + bq).reshape(B, Nq, H, D).transpose(0, 2, 1, 3)
        k = (key_value @ Wk + bk).reshape(B, Nkv, H, D).transpose(0, 2, 1, 3)
        v = (key_value @ Wv + bv).reshape(B, Nkv, H, D).transpose(0, 2, 1, 3)
        attn = jnp.einsum('bhqd,bhkd->bhqk', q, k) * scale
        attn = jnp.clip(attn, -CLAMP, CLAMP)
        attn = jax.nn.softmax(attn, axis=-1)
        attn = jnp.where(jnp.any(jnp.isnan(attn)), jnp.asarray(1.0 / Nkv, attn.dtype), attn)
        x = jnp.einsum('bhqk,bhkd->bqhd', attn, v).reshape(B, Nq, Cq)
        return x @ Wo + bo

    def _L0_ffn_ref(x, Wr, br, W_up, b_up, W_down, b_down):
        import jax, jax.numpy as jnp
        import numpy as np
        B, S, H = (4, 512, 256)
        E = 8
        GS = 2
        NG = E // GS
        F = int(H * 4 * (2.0 / 3.0))
        b, s, h = x.shape
        n_tok = b * s
        k = n_tok // E
        xf = x.reshape(n_tok, h)
        logits = xf @ Wr + br
        Sm = jax.nn.softmax(logits, axis=-1)
        G_t, idx_t = jax.lax.top_k(Sm.T, k)
        G = G_t.T
        idx = idx_t.T
        tokens = xf[idx]
        group = jnp.arange(E) // GS
        Wu = W_up[group]
        bu = b_up[group]
        mid = jax.nn.silu(jnp.einsum('keh,ehf->kef', tokens, Wu) + bu)
        out = jnp.einsum('kef,efh->keh', mid, W_down) + b_down
        y = jnp.zeros_like(xf).at[idx].add(G[..., None] * out)
        return y.reshape(b, s, h)
    x = x + _L0_attn_ref(_layernorm(x, axis=-1), L0_attn_Wq, L0_attn_Wk, L0_attn_Wv, L0_attn_Wo)
    x = x + _L0_xattn_ref(_layernorm(x, axis=-1), ctx_768, L0_xattn_Wq, L0_xattn_bq, L0_xattn_Wk, L0_xattn_bk, L0_xattn_Wv, L0_xattn_bv, L0_xattn_Wo, L0_xattn_bo)
    x = x + _L0_ffn_ref(_layernorm(x, axis=-1), L0_ffn_Wr, L0_ffn_br, L0_ffn_W_up, L0_ffn_b_up, L0_ffn_W_down, L0_ffn_b_down)
    return x

_drawn_inputs = setup_inputs


def setup_inputs(seed=0):
    import zlib

    import numpy as np

    out = dict(_drawn_inputs(seed))
    spreads = {'L0_xattn_bq': (0.0, 0.281),
     'L0_xattn_bk': (0.0, 2.0),
     'L0_xattn_bv': (0.0, 0.1),
     'L0_xattn_bo': (0.0, 0.1),
     'L0_ffn_br': (0.0, 0.1)}
    factors = {'L0_ffn_b_up': 28.555, 'L0_ffn_b_down': 8.0}
    for name, (base, spread) in spreads.items():
        noise = np.random.default_rng([zlib.crc32(name.encode()), seed]).standard_normal(out[name].shape)
        drawn = base * np.exp(spread * noise) if base else spread * noise
        out[name] = jnp.asarray(drawn.astype(out[name].dtype))
    for name, factor in factors.items():
        out[name] = (out[name] * factor).astype(out[name].dtype)
    return out
```

```python
from contextlib import ExitStack

import concourse.bass as bass
from concourse import mybir

F32, BF16, F16 = mybir.dt.float32, mybir.dt.bfloat16, mybir.dt.float16
U32, I32 = mybir.dt.uint32, mybir.dt.int32
ALU = mybir.AluOpType
ACT = mybir.ActivationFunctionType
AX = mybir.AxisListType

P = 128
SHIFT_UNIT = 64.0
MASKED = -1.0e30
LN_EPS = 1e-5
RSQRT_BITS = float(0x5F3759DF)
NEWTON_STEPS = 3
NEWTON_OPS = 4 * NEWTON_STEPS
SHIFT_ROW = 96
STACK = 98
PER_UNIT = 24 * 16
SHIFT_DMA = 2 * 16


def ahead(b, g, d):
    return b + (g + d) // 4, (g + d) % 4


def guess(dve, y, v, neg_half, var, semaphore, before):
    dve.tensor_scalar(v, var, LN_EPS, None, ALU.add).then_inc(semaphore, 1)
    dve.wait_ge(semaphore, before + 1)
    dve.tensor_scalar(y.bitcast(U32), v.bitcast(U32), 1, None, ALU.logical_shift_right).then_inc(semaphore, 1)
    dve.tensor_scalar(neg_half, v, -0.5, None, ALU.mult).then_inc(semaphore, 1)
    dve.wait_ge(semaphore, before + 3)
    dve.tensor_scalar(y.bitcast(I32), y.bitcast(I32), -1.0, RSQRT_BITS, ALU.mult, ALU.add).then_inc(semaphore, 1)


def newton(pool, y, neg_half, one_half, t, semaphore, before):
    n = before
    for _ in range(NEWTON_STEPS):
        for out, in0, in1, op in ((t, y, y, ALU.mult), (t, t, neg_half, ALU.mult), (t, t, one_half, ALU.add),
                                  (y, y, t, ALU.mult)):
            pool.tensor_tensor(out, in0, in1, op).then_inc(semaphore, 1)
            n = n + 1
            pool.wait_ge(semaphore, n)


class WorkBanks:

    def __init__(self, cross, batches):
        self.cross, self.batches = cross, batches
        self.table, self.count = {}, [0, 0]
        self.turn = 0
        for key in self.prologue():
            self._add(("pro",) + key)
        for b in range(batches):
            for g in range(4):
                for key in self.step(b, g):
                    self._add((b, g) + key)
        for key in (("wo", 0), ("wo", 1)):
            self._add(("epi",) + key)

    def _add(self, key):
        bank = self.turn % 2
        self.turn += 1
        self.table[key] = (bank, self.count[bank])
        self.count[bank] += 1

    def prologue(self):
        out = [("tr", i) for i in range(4 if self.cross else 2)]
        out += [("q", 0), ("k", 0)] + ([] if self.cross else [("q", 1), ("k", 1)])
        return out + [("mx", j, i) for j in range(4) for i in range(4)] + [("mt",)]

    def step(self, b, g):
        last = self.batches - 1
        out = []
        if g == 1 and b >= 1:
            out += [("wo", 0), ("wo", 1)]
        if (not self.cross or g % 2 == 0) and not (b == last and g >= 2):
            out += [("q",), ("k",)]
        if not (b == last and g == 3):
            out += [("mx", j, i) for j in range(4) for i in range(4)] + [("mt",)]
        if g == 0:
            out += [("v", i) for i in range(2 if self.cross else 4)]
        if g == 1 and b < last:
            out += [("tr", i) for i in range(4 if self.cross else 2)]
        return out

    def at(self, section, *key):
        if isinstance(section, (str, int)):
            return self.table[(section,) + key]
        bank, one = self.table[(1,) + key]
        again, two = self.table[(2,) + key]
        assert bank == again
        return bank, section * (two - one) + (2 * one - two)


def attention(nc, stack, name, cross, x, src, weights, consts):
    B, NT, C = x.shape[1], x.shape[2], x.shape[3]
    last_batch = B - 1
    CD = 16 if cross else 32
    CK = src.shape[-1]
    KT = [(0, P), (1, CK - P)]
    NV = 16 * CD
    SCALE = 0.25
    WID = [512] * 4 if cross else [512, 384, 256, 128]
    Q0 = [512 - w for w in WID]
    OFF = [0, 512, 1024, 1536] if cross else [0, 512, 1024, 1280]
    EXP = [1024, 1024] if cross else [896, 384]
    SPLIT = CD
    banks = WorkBanks(cross, B)
    V_USES = 2 if cross else 4
    ident, mask_qk, mask_kq, ident_b = consts["ident"], consts["mask_qk"], consts["mask_kq"], consts["ident_b"]

    def sb(n, shape, dt=F32):
        return stack.enter_context(nc.sbuf_tensor(f"{name}_{n}", shape, dt))

    def ps(n, shape):
        return stack.enter_context(nc.psum_tensor(f"{name}_{n}", shape, F32))

    def sem(n):
        return stack.enter_context(nc.semaphore(f"{name}_{n}"))

    wq = sb("wq", [P, 2, 16 * CD])
    wk = sb("wk", [P, 2, 16 * CD])
    wv = sb("wv", [P, 2, NV])
    wo = sb("wo", [P, 4, C])
    xn = sb("xn", [P, NT, C])
    stats = sb("stats", [P, NT, 6])
    meanvar = sb("meanvar", [P, NT, 2])
    rstd = sb("rstd", [P, NT])
    veps, square, neg_half, one_half = (sb(n, [P, NT]) for n in ("veps", "square", "neg_half", "one_half"))
    wait_cell = sb("wait_cell", [P, 1])
    xnT = sb("xnT", [P, 2, 512])
    qh, ql, kh, kl = (sb(n, [P, 2, 512], F16) for n in ("qh", "ql", "kh", "kl"))
    qs = sb("qs", [P, 4, 4, 512], F16)
    ks = sb("ks", [P, 4, 4, 512], F16)
    rowmax = sb("rowmax", [P, 2, 16])
    shift_h = sb("shift_h", [16, 2, P], F16)
    shift_l = sb("shift_l", [16, 2, P], F16)
    probs = sb("probs", [P, 2, 4, 2048])
    attT = sb("attT", [P, 4, 512])
    rinv = sb("rinv", [P, 512])
    if cross:
        ctx_in = sb("ctx_in", [P, NT, 2 * P])
        ctxT = sb("ctxT", [P, 2, 512])
        val = sb("val", [P, 4, 16, 32])
        raw = sb("raw", [P, 512])
        bq, bk = sb("bq", [P, 2]), sb("bk", [P, 2])
        bv, bo = sb("bv", [P, NV]), sb("bo", [P, C])
    else:
        val = sb("val", [P, 4, NV])
    kvT = ctxT if cross else xnT

    work = [ps("work0", [P, 512]), ps("work1", [P, 512])]
    score = [ps("score0", [P, 1024]), ps("score1", [P, 1024])]
    out_ps = ps("out_ps", [P, 512])
    sum_ps = ps("sum_ps", [P, 512])

    full = [sem("work0_filled"), sem("work1_filled")]
    free = [sem("work0_freed"), sem("work1_freed")]
    weights_loaded, consts_set = sem("weights_loaded"), sem("consts_set")
    src_loaded = sem("src_loaded")
    ln_guess = sem("ln_guess")
    ln_stats, ln_aggr, ln_rstd, xn_ready = sem("ln_stats"), sem("ln_aggr"), sem("ln_rstd"), sem("xn_ready")
    hi_ready = sem("hi_ready")
    restacked = [sem("restacked0"), sem("restacked1")]
    shift_hi = sem("shift_hi")
    shift_placed = [sem("shift_placed0"), sem("shift_placed1")]
    scores_ready, exp_done = sem("scores_ready"), sem("exp_done")
    pv_done, raw_ready, sums_ready = sem("pv_done"), sem("raw_ready"), sem("sums_ready")
    rinv_ready, norm_done = sem("rinv_ready"), sem("norm_done")
    bo_added = sem("bo_added")

    def unit(b, g):
        return 4 * b + g

    def turns(b, g):
        return 2 * b + g // 2

    def wait(eng, semaphore, value):
        if not isinstance(value, int) or value > 0:
            eng.wait_ge(semaphore, value)

    def fill(eng, use):
        bank, n = use
        wait(eng, free[bank], n)
        return work[bank]

    def filled(eng, use):
        bank, n = use
        eng.wait_ge(full[bank], n + 1)
        return work[bank]

    def freed(eng, use):
        eng.wait_ge(free[use[0]], use[1] + 1)

    N_TR = 4 if cross else 2

    def last_transposes(b, section):
        if isinstance(b, int) and b == 0:
            return [banks.at("pro", "tr", i) for i in range(N_TR)]
        return [banks.at(section, 1, "tr", i) for i in range(N_TR)]

    def steps(eng, emit, prologue, epilogue):
        prologue()
        for g in range(4):
            emit(0, g, True, False)
        with eng.Fori(1, last_batch) as b:
            for g in range(4):
                emit(b, g, False, False)
        for g in range(4):
            emit(last_batch, g, False, True)
        epilogue()

    block = stack.enter_context(nc.Block())

    @block.sync
    def _(sp):
        halves = 16 * CD
        sp.dma_start(wq[:, :, :], weights["Wq"].rearrange("(t p) n -> p t n", p=P)).then_inc(weights_loaded, 16)
        for w_sb, w in ((wk, weights["Wk"]), (wv, weights["Wv"])):
            for t, rows in KT:
                sp.dma_start(w_sb[0:rows, t, :], w[t * P:t * P + rows, :]).then_inc(weights_loaded, 16)
        if cross:
            sp.wait_ge(consts_set, 6)
            for j in range(4):
                sp.dma_start(wo[32 * j:32 * j + CD, :, :], weights["Wo"].rearrange(
                    "(g j r) n -> j r g n", g=4, j=4)[j]).then_inc(weights_loaded, 16)
            sp.dma_start(bq[:, :], weights["bq"].rearrange("(t p) -> p t", p=P), allow_slow_non_contiguous=True).then_inc(weights_loaded, 16)
            sp.dma_start(bk[:, :], weights["bk"].rearrange("(t p) -> p t", p=P), allow_slow_non_contiguous=True).then_inc(weights_loaded, 16)
            sp.dma_start(bv[:, :], weights["bv"].rearrange("(a n) -> a n", a=1).to_broadcast([P, NV])).then_inc(weights_loaded, 16)
            sp.dma_start(bo[:, :], weights["bo"].rearrange("(a n) -> a n", a=1).to_broadcast([P, C])).then_inc(weights_loaded, 16)
        else:
            sp.dma_start(wo[:, :, :], weights["Wo"].rearrange("(g p) n -> p g n", p=P)).then_inc(weights_loaded, 16)

        def load(b):
            if cross:
                if not (isinstance(b, int) and b == 0):
                    filled(sp, last_transposes(b - 1, b - 2)[-1])
                sp.dma_start(ctx_in[:, :, 0:CK], src[b].rearrange("(t p) c -> p t c", p=P)).then_inc(src_loaded, 16)
            else:
                wait(sp, src_loaded, 16 * b)
                sp.dma_start(x[:, b, :, :], src[b].rearrange("(t p) c -> p t c", p=P)).then_inc(src_loaded, 16)

        def restack(b, g, section, key, tail=()):
            par = (g // 2) % 2 if cross else g % 2
            rows = slice(64 * (g % 2), 64 * (g % 2) + 64) if cross else slice(0, P)
            for what, dst, parts in (("q", qs, (qh, qh, ql)), ("k", ks, (kh, kl, kh))):
                freed(sp, banks.at(section, *key, what, *tail))
                for s, part in enumerate(parts):
                    for j in range(4):
                        r0 = rows.start + CD * j
                        sp.dma_start(dst[SPLIT * s:SPLIT * s + SPLIT, g, j, :], part[r0:r0 + CD, par, :])\
                          .then_inc(restacked[g % 2], 16)

        def place_shift(b, g, section, key):
            freed(sp, banks.at(section, *key, "mt"))
            for r, part in enumerate((shift_h, shift_l)):
                sp.dma_start(qs[SHIFT_ROW + r:SHIFT_ROW + r + 1, g, :, :].rearrange("p j (i c) -> p (j i) c", c=P),
                             part[:, g % 2, :]).then_inc(shift_placed[g % 2], 16)

        def prologue():
            load(0)
            sp.wait_ge(consts_set, 3)
            restack(0, 0, "pro", (), (0,))
            restack(0, 1, "pro", (), (0,) if cross else (1,))
            place_shift(0, 0, "pro", ())

        def emit(b, g, first, last):
            if g == 0 and not last:
                load(b + 1)
            if not (last and g >= 2):
                if not cross or g % 2 == 0:
                    restack(*ahead(b, g, 2), b, (g,))
                if cross and g % 2 == 0:
                    restack(*ahead(b, g, 3), b, (g,))
            if not (last and g == 3):
                place_shift(*ahead(b, g, 1), b, (g,))

        steps(sp, emit, prologue, lambda: None)

    @block.gpsimd
    def _(pool):
        pool.memset(qs[:, :, :, :], 0.0).then_inc(consts_set, 1)
        pool.memset(ks[:, :, :, :], 0.0).then_inc(consts_set, 1)
        pool.wait_ge(consts_set, 2)
        pool.memset(ks[SHIFT_ROW:SHIFT_ROW + 2, :, :, :], SHIFT_UNIT).then_inc(consts_set, 1)
        pool.wait_ge(consts_set, 3)
        pool.memset(one_half[:, :], 1.5).then_inc(consts_set, 1)
        pool.wait_ge(consts_set, 4)
        if cross:
            pool.memset(ctx_in[:, :, CK:], 0.0).then_inc(consts_set, 1)
            pool.memset(wo[:, :, :], 0.0).then_inc(consts_set, 1)
            pool.memset(val[:, :, :, CD:], 1.0).then_inc(consts_set, 1)
            pool.wait_ge(weights_loaded, 13 * 16)

        def batch(b):
            pool.wait_ge(ln_guess, 4 * b + 4)
            newton(pool, rstd[:, :], neg_half[:, :], one_half[:, :], square[:, :], ln_rstd, NEWTON_OPS * b)
            if cross:
                pool.wait_ge(xn_ready, 4 * b + 4)
                for i in range(NT):
                    ins = pool.tensor_tensor(x[:, b, i, :], x[:, b, i, :], bo[:, :], ALU.add)
                ins.then_inc(bo_added, 1)

        batch(0)
        with pool.Fori(1, B) as b:
            batch(b)

    @block.tensor
    def _(pe):
        def transposes(b, section, g):
            pe.wait_ge(xn_ready, 4 * b + 4)
            for c in range(2):
                use = banks.at(section, *g, "tr", c)
                dst = fill(pe, use)
                for i in range(NT):
                    ins = pe.transpose(dst[:, i * P:(i + 1) * P], xn[:, i, c * P:(c + 1) * P], ident[:, :])
                ins.then_inc(full[use[0]], 1)
            if cross:
                pe.wait_ge(src_loaded, 16 * b + 16)
                for c, rows in KT:
                    use = banks.at(section, *g, "tr", 2 + c)
                    dst = fill(pe, use)
                    for i in range(NT):
                        ins = pe.transpose(dst[:, i * P:(i + 1) * P], ctx_in[:, i, c * P:(c + 1) * P], ident[:, :])
                    ins.then_inc(full[use[0]], 1)

        def project(b, g, section, key, tail=()):
            if g == 0:
                for use in last_transposes(b, section)[-2:]:
                    freed(pe, use)
            col = (g // 2) * P if cross else g * P
            for what, w in (("q", wq), ("k", wk)):
                use = banks.at(section, *key, what, *tail)
                dst = fill(pe, use)
                tiles = KT if what == "k" else [(0, P), (1, P)]
                act = kvT if what == "k" else xnT
                for t, rows in tiles:
                    ins = pe.matmul(dst[:, :], w[0:rows, t, col:col + P], act[0:rows, t, :], start=t == 0, stop=t == 1)
                ins.then_inc(full[use[0]], 1)

        def maxima(b, g, j, section, key):
            if j == 0:
                pe.wait_ge(restacked[g % 2], PER_UNIT * turns(b, g) + PER_UNIT)
            for i in range(4):
                use = banks.at(section, *key, "mx", j, i)
                dst = fill(pe, use)
                w = 512 if cross else (i + 1) * P
                ins = pe.matmul(dst[:, 0:w], qs[0:SHIFT_ROW, g, j, i * P:(i + 1) * P], ks[0:SHIFT_ROW, g, j, 0:w],
                                start=True, stop=cross)
                if not cross:
                    ins = pe.matmul(dst[:, i * P:w], ident_b[:, :], mask_qk[:, :], start=False, stop=True)
                ins.then_inc(full[use[0]], 1)

        def turn_maxima(b, g, section, key):
            use = banks.at(section, *key, "mt")
            dst = fill(pe, use)
            freed(pe, banks.at(section, *key, "mx", 3, 3))
            pe.transpose(dst[0:16, 0:P], rowmax[:, g % 2, :], ident[:, :]).then_inc(full[use[0]], 1)

        def scores(b, g, j):
            if j == 0:
                pe.wait_ge(shift_placed[g % 2], SHIFT_DMA * turns(b, g) + SHIFT_DMA)
            for half in range(2):
                wait(pe, exp_done, 8 * unit(b, g) + 2 * j + half - 1)
                for kb in (2 * half, 2 * half + 1):
                    at = OFF[kb] - 1024 * half
                    dst = score[half][:, at:at + WID[kb]]
                    ins = pe.matmul(dst, ks[0:STACK, g, j, kb * P:(kb + 1) * P], qs[0:STACK, g, j, Q0[kb]:512],
                                    start=True, stop=cross)
                    if not cross:
                        ins = pe.matmul(score[half][:, at:at + P], ident_b[:, :], mask_kq[:, :], start=False, stop=True)
                ins.then_inc(scores_ready, 1)

        def weigh(b, g, kb, section=None):
            u = unit(b, g)
            if kb == 0:
                pe.wait_ge(exp_done, 8 * u + 8)
                wait(pe, raw_ready if cross else norm_done, u)
                if g == 0:
                    for n in (V_USES - 2, V_USES - 1):
                        freed(pe, banks.at(section, 0, "v", n))
            cols = slice(Q0[kb], 512)
            for j in range(4):
                lhs = val[:, kb, 4 * g + j, :] if cross else val[:, kb, (4 * g + j) * CD:(4 * g + j + 1) * CD]
                ins = pe.matmul(out_ps[32 * j:32 * j + 32, cols], lhs, probs[:, g % 2, j, OFF[kb]:OFF[kb] + WID[kb]],
                                start=kb == 0, stop=kb == 3, tile_position=(0, 32 * j))
            if not cross:
                for j in range(4):
                    ins = pe.matmul(sum_ps[32 * j:32 * j + 32, cols], consts["ones"][:, 0:32],
                                    probs[:, g % 2, j, OFF[kb]:OFF[kb] + WID[kb]],
                                    start=kb == 0, stop=kb == 3, tile_position=(0, 32 * j))
            if kb == 3:
                ins.then_inc(pv_done, 1)

        def spread_sums(b, g):
            u = unit(b, g)
            pe.wait_ge(raw_ready, u + 1)
            wait(pe, norm_done, u)
            pe.matmul(sum_ps[:, :], consts["spread"][:, :], raw[:, :], start=True, stop=True).then_inc(sums_ready, 1)

        def values(b, g, section):
            for n in range(V_USES):
                use = banks.at(section, g, "v", n)
                dst = fill(pe, use)
                tiles = (2 * n, 2 * n + 1) if cross else (n,)
                for m, i in enumerate(tiles):
                    for t, rows in KT:
                        ins = pe.matmul(dst[:, m * NV:(m + 1) * NV], kvT[0:rows, t, i * P:(i + 1) * P],
                                        wv[0:rows, t, :], start=t == 0, stop=t == 1)
                ins.then_inc(full[use[0]], 1)

        def project_out(b, section, key):
            pe.wait_ge(norm_done, 4 * b + 4)
            for n in range(2):
                use = banks.at(section, *key, "wo", n)
                dst = fill(pe, use)
                for m in range(2):
                    i = 2 * n + m
                    for g in range(4):
                        ins = pe.matmul(dst[:, m * C:(m + 1) * C], attT[:, g, i * P:(i + 1) * P], wo[:, g, :],
                                        start=g == 0, stop=g == 3)
                ins.then_inc(full[use[0]], 1)

        def prologue():
            pe.wait_ge(weights_loaded, (13 if cross else 6) * 16)
            pe.wait_ge(consts_set, 7 if cross else 4)
            transposes(0, "pro", ())
            project(0, 0, "pro", (), (0,))
            if not cross:
                project(0, 1, "pro", (), (1,))
            for j in range(4):
                maxima(0, 0, j, "pro", ())
            turn_maxima(0, 0, "pro", ())

        def emit(b, g, first, last):
            if g == 1 and not first:
                project_out(b - 1, b, (g,))
            if (not cross or g % 2 == 0) and not (last and g >= 2):
                bb, gg = ahead(b, g, 2)
                project(bb, gg, b, (g,))
            for j in range(4):
                scores(b, g, j)
                if not (last and g == 3):
                    bb, gg = ahead(b, g, 1)
                    maxima(bb, gg, j, b, (g,))
                if not (first and g == 0):
                    weigh(*ahead(b, g, -1), j, b)
            if not (last and g == 3):
                turn_maxima(*ahead(b, g, 1), b, (g,))
            if cross and not (first and g == 0):
                spread_sums(*ahead(b, g, -1))
            if g == 0:
                values(b, g, b)
            if g == 1 and not last:
                transposes(b + 1, b, (g,))

        def epilogue():
            for kb in range(4):
                weigh(last_batch, 3, kb)
            if cross:
                spread_sums(last_batch, 3)
            project_out(last_batch, "epi", ())

        steps(pe, emit, prologue, epilogue)

    @block.scalar
    def _(act):
        def high_parts(b, g, section, key, tail=()):
            n = turns(b, g) if cross else unit(b, g)
            par = (g // 2) % 2 if cross else g % 2
            if cross:
                for r in restacked:
                    wait(act, r, PER_UNIT * (n - 1))
            else:
                wait(act, restacked[g % 2], PER_UNIT * turns(b, g))
            for what, dst in (("q", qh), ("k", kh)):
                use = banks.at(section, *key, what, *tail)
                ps_ = filled(act, use)
                if cross:
                    bias = (bq if what == "q" else bk)[:, g // 2:g // 2 + 1]
                    act.activation(dst[:, par, :], ps_[:, :], ACT.Identity, bias=bias).then_inc(hi_ready, 1)
                else:
                    act.activation(dst[:, par, :], ps_[:, :], ACT.Copy).then_inc(hi_ready, 1)

        def exps(b, g, j):
            u = unit(b, g)
            if j == 0:
                wait(act, pv_done, u - 1)
            for half in range(2):
                act.wait_ge(scores_ready, 8 * u + 2 * j + half + 1)
                act.activation(probs[:, g % 2, j, 1024 * half:1024 * half + EXP[half]], score[half][:, 0:EXP[half]],
                               ACT.Exp, scale=SCALE).then_inc(exp_done, 1)

        def shift_high(b, g, section, key):
            use = banks.at(section, *key, "mt")
            ps_ = filled(act, use)
            wait(act, shift_placed[g % 2], SHIFT_DMA * turns(b, g))
            act.activation(shift_h[:, g % 2, :], ps_[0:16, 0:P], ACT.Copy, scale=-1.0 / SHIFT_UNIT).then_inc(shift_hi, 1)

        def copy_raw(b, g):
            u = unit(b, g)
            act.wait_ge(pv_done, u + 1)
            wait(act, norm_done, u)
            act.activation(raw[:, :], out_ps[:, :], ACT.Copy).then_inc(raw_ready, 1)

        def keep_values(b, g, section):
            wait(act, pv_done, 4 * b)
            for n in range(V_USES):
                use = banks.at(section, g, "v", n)
                ps_ = filled(act, use)
                act.activation(val[:, n, :], ps_[:, :], ACT.Copy).then_inc(free[use[0]], 1)

        def keep_transposed(b, section, g):
            for c in range(4 if cross else 2):
                use = banks.at(section, *g, "tr", c)
                ps_ = filled(act, use)
                dst, rows = (xnT, P) if c < 2 else (ctxT, KT[c - 2][1])
                act.activation(dst[0:rows, c % 2, :], ps_[0:rows, :], ACT.Copy).then_inc(free[use[0]], 1)

        def prologue():
            if cross:
                act.wait_ge(weights_loaded, 13 * 16)
            keep_transposed(0, "pro", ())
            high_parts(0, 0, "pro", (), (0,))
            if not cross:
                high_parts(0, 1, "pro", (), (1,))
            shift_high(0, 0, "pro", ())

        def emit(b, g, first, last):
            if (not cross or g % 2 == 0) and not (last and g >= 2):
                bb, gg = ahead(b, g, 2)
                high_parts(bb, gg, b, (g,))
            for j in range(4):
                exps(b, g, j)
            if not (last and g == 3):
                shift_high(*ahead(b, g, 1), b, (g,))
            if cross and not (first and g == 0):
                copy_raw(*ahead(b, g, -1))
            if g == 0 and not cross:
                keep_values(b, g, b)
            if g == 1 and not last:
                keep_transposed(b + 1, b, (g,))

        def epilogue():
            if cross:
                copy_raw(last_batch, 3)

        steps(act, emit, prologue, epilogue)

    @block.vector
    def _(dve):
        def layer_norm(b, section=None):
            if not cross:
                dve.wait_ge(src_loaded, 16 * b + 16)
            for i in range(NT):
                dve.bn_stats(stats[:, i, :], x[:, b, i, :]).then_inc(ln_stats, 1)
            dve.wait_ge(ln_stats, 4 * b + 4)
            dve.memset(wait_cell[:, :], 0.0)
            for i in range(NT):
                dve.bn_aggr(meanvar[:, i, :], stats[:, i, :]).then_inc(ln_aggr, 1)
            dve.wait_ge(ln_aggr, 4 * b + 4)
            guess(dve, rstd[:, :], veps[:, :], neg_half[:, :], meanvar[:, :, 1], ln_guess, 4 * b)
            dve.wait_ge(ln_rstd, NEWTON_OPS * b + NEWTON_OPS)
            if section is not None:
                for use in last_transposes(section, section - 1)[0:2]:
                    filled(dve, use)
            for i in range(NT):
                dve.tensor_scalar(xn[:, i, :], x[:, b, i, :], meanvar[:, i, 0:1], rstd[:, i:i + 1],
                                  ALU.subtract, ALU.mult).then_inc(xn_ready, 1)

        def low_parts(b, g, section, key, tail=()):
            n = turns(b, g) if cross else unit(b, g)
            par = (g // 2) % 2 if cross else g % 2
            for m, (what, hi, lo) in enumerate((("q", qh, ql), ("k", kh, kl))):
                use = banks.at(section, *key, what, *tail)
                dve.wait_ge(hi_ready, 2 * n + m + 1)
                if cross:
                    bias = (bq if what == "q" else bk)[:, g // 2:g // 2 + 1]
                    ins = dve.scalar_tensor_tensor(out=lo[:, par, :], in0=work[use[0]][:, :], scalar=bias,
                                                   in1=hi[:, par, :], op0=ALU.add, op1=ALU.subtract)
                else:
                    ins = dve.tensor_tensor(lo[:, par, :], work[use[0]][:, :], hi[:, par, :], ALU.subtract)
                ins.then_inc(free[use[0]], 1)

        def maxima(b, g, j, section, key):
            for i in range(4):
                use = banks.at(section, *key, "mx", j, i)
                ps_ = filled(dve, use)
                w = 512 if cross else (i + 1) * P
                ins = dve.tensor_reduce(rowmax[:, g % 2, 4 * j + i:4 * j + i + 1], ps_[:, 0:w], AX.X, ALU.max)
                ins.then_inc(free[use[0]], 1)

        def shift_low(b, g, section, key):
            use = banks.at(section, *key, "mt")
            dve.wait_ge(shift_hi, unit(b, g) + 1)
            dve.scalar_tensor_tensor(out=shift_l[:, g % 2, :], in0=work[use[0]][0:16, 0:P], scalar=-1.0 / SHIFT_UNIT,
                                     in1=shift_h[:, g % 2, :], op0=ALU.mult, op1=ALU.subtract).then_inc(free[use[0]], 1)

        def normalise(b, g, section=None):
            u = unit(b, g)
            if cross:
                dve.wait_ge(sums_ready, u + 1)
            else:
                dve.wait_ge(pv_done, u + 1)
            dve.reciprocal(rinv[:, :], sum_ps[:, :]).then_inc(rinv_ready, 1)
            dve.wait_ge(rinv_ready, u + 1)
            if g == 0 and not (isinstance(b, int) and b == 0):
                filled(dve, banks.at(section, 1, "wo", 1))
            dve.tensor_tensor(attT[:, g, :], (raw if cross else out_ps)[:, :], rinv[:, :], ALU.mult).then_inc(norm_done, 1)

        def keep_values(b, g, section):
            wait(dve, pv_done, 4 * b)
            for n in range(V_USES):
                use = banks.at(section, g, "v", n)
                ps_ = filled(dve, use)
                for m in range(2):
                    ins = dve.tensor_tensor(val[:, 2 * n + m, :, 0:CD],
                                            ps_[:, m * NV:(m + 1) * NV].rearrange("p (h d) -> p h d", h=16),
                                            bv[:, :].rearrange("p (h d) -> p h d", h=16), ALU.add)
                ins.then_inc(free[use[0]], 1)

        def residual(b, section, key):
            if cross:
                dve.wait_ge(bo_added, b + 1)
            for n in range(2):
                use = banks.at(section, *key, "wo", n)
                ps_ = filled(dve, use)
                xs = x[:, b, 2 * n:2 * n + 2, :].rearrange("p t c -> p (t c)")
                dve.tensor_tensor(xs, xs, ps_[:, :], ALU.add).then_inc(free[use[0]], 1)

        def prologue():
            if cross:
                dve.wait_ge(weights_loaded, 13 * 16)
            layer_norm(0)
            low_parts(0, 0, "pro", (), (0,))
            if not cross:
                low_parts(0, 1, "pro", (), (1,))
            for j in range(4):
                maxima(0, 0, j, "pro", ())
            shift_low(0, 0, "pro", ())

        def emit(b, g, first, last):
            if g == 1 and not first:
                residual(b - 1, b, (g,))
            if (not cross or g % 2 == 0) and not (last and g >= 2):
                bb, gg = ahead(b, g, 2)
                low_parts(bb, gg, b, (g,))
            if not (last and g == 3):
                bb, gg = ahead(b, g, 1)
                for j in range(4):
                    maxima(bb, gg, j, b, (g,))
                shift_low(bb, gg, b, (g,))
            if not (first and g == 0):
                normalise(*ahead(b, g, -1), b)
            if g == 0 and cross:
                keep_values(b, g, b)
            if g == 0 and not last:
                layer_norm(b + 1, b)

        def epilogue():
            normalise(last_batch, 3)
            residual(last_batch, "epi", ())

        steps(dve, emit, prologue, epilogue)


def expert_choice(nc, stack, x, a, out):
    B, NT, C = x.shape[1], x.shape[2], x.shape[3]
    T = B * NT
    E = a["L0_ffn_W_down"].shape[0]
    F = a["L0_ffn_W_down"].shape[1]
    GROUPS = a["L0_ffn_W_up"].shape[0]
    PER_GROUP = E // GROUPS
    CAP = T * P // E
    Q = CAP // P
    FT = -(-F // P)
    FR = F - (FT - 1) * P
    BIAS_ROW = 64
    ROW = C + E
    HI, LO = CAP // 32, 32
    BITS = 30
    outer = stack
    rows = nc.dram_tensor("token_rows", [T * P, ROW], F32).ap()

    def sb(n, shape, dt=F32, s=None):
        return (s or outer).enter_context(nc.sbuf_tensor("ffn_" + n, shape, dt))

    def sem(n):
        return outer.enter_context(nc.semaphore("ffn_" + n))

    w_up = sb("w_up", [P, GROUPS, 2, F])
    w_down = sb("w_down", [P, E, FT, C])
    b_up = sb("b_up", [P, GROUPS, FT])
    idx = sb("idx", [P, E * Q], U32)
    ident = sb("ident", [P, P])
    mid = sb("mid", [P, FT, CAP])
    down_cleared, up_loaded, down_loaded = sem("down_cleared"), sem("up_loaded"), sem("down_loaded")
    DOWN_DMAS = 3 * E
    UP_DMAS = 2 + GROUPS
    x_stored, rows_stored, gates_stored = sem("x_stored"), sem("rows_stored"), sem("gates_stored")

    with ExitStack() as s:
        def sb2(n, shape, dt=F32):
            return sb(n, shape, dt, s)

        xn = sb2("xn", [P, B, NT, C])
        stats, meanvar = sb2("stats", [P, T, 6]), sb2("meanvar", [P, T, 2])
        rstd, veps, square = sb2("rstd", [P, T]), sb2("veps", [P, T]), sb2("square", [P, T])
        neg_half, one_half = sb2("neg_half", [P, T]), sb2("one_half", [P, T])
        xT = sb2("xT", [P, 2, 512])
        wr, br = sb2("wr", [P, 2, E]), sb2("br", [P, E])
        logits = sb2("logits", [P, T, E])
        red, gates, gates_e = sb2("red", [P, T]), sb2("gates", [P, T, E]), sb2("gates_e", [P, E, T])
        ones_b, before = sb2("ones_b", [P, P], BF16), sb2("before", [P, P], BF16)
        diag = sb2("diag", [P, E, LO])
        carry = sb2("carry", [P, E, T])
        iota_i = sb2("iota_i", [P, T + HI + LO], I32)
        iota = sb2("iota", [P, T + HI + LO])
        tok, count_hi, count_lo = iota[:, 0:T], iota[:, T:T + HI], iota[:, T + HI:]
        thr, trial, bit = sb2("thr", [P, E]), sb2("trial", [P, E]), sb2("bit", [P, E])
        count, need = sb2("count", [P, E]), sb2("need", [P, E])
        over = sb2("over", [P, E, T], BF16)
        gt, eq, sel = sb2("gt", [P, E, T], BF16), sb2("eq", [P, E, T], BF16), sb2("sel", [P, E, T], BF16)
        tile_sum, rank, place_i = sb2("tile_sum", [P, E, T]), sb2("rank", [P, E, T]), sb2("place_i", [P, E, T], I32)
        hi_i, lo_i = sb2("hi_i", [P, E, T], I32), sb2("lo_i", [P, E, T], I32)
        hi, lo = sb2("hi", [P, E, T]), sb2("lo", [P, E, T])
        pick_hi = sb2("pick_hi", [P, T, E, HI])
        pick_lo = xn[:, :, :, :].rearrange("p b i c -> p (b i c)").rearrange("p (t e l) -> p t e l", t=T, e=E)
        own, folded = sb2("own", [P, E, LO]), sb2("folded", [P, LO])
        turn_ps = [s.enter_context(nc.psum_tensor(f"ffn_turn{i}", [P, 512], F32)) for i in range(2)]
        logit_ps = s.enter_context(nc.psum_tensor("ffn_logit_ps", [P, 512], F32))
        count_ps = s.enter_context(nc.psum_tensor("ffn_count_ps", [P, 512], F32))
        rank_ps = s.enter_context(nc.psum_tensor("ffn_rank_ps", [P, 512], F32))
        idx_ps = s.enter_context(nc.psum_tensor("ffn_idx_ps", [P, 512], F32))
        idxT_ps = s.enter_context(nc.psum_tensor("ffn_idxT_ps", [P, 512], F32))

        consts_made, const_steps, router_loaded = sem("consts_made"), sem("const_steps"), sem("router_loaded")
        ln_stats, ln_aggr, ln_guess, ln_rstd, xn_ready = (sem(n) for n in ("ln_stats", "ln_aggr", "ln_guess", "ln_rstd", "xn_ready"))
        turned, turned_kept, logits_done, logits_kept = (sem(n) for n in ("turned", "turned_kept", "logits_done", "logits_kept"))
        chain, shifted, exps_done, gates_ready = (sem(n) for n in ("chain", "shifted", "exps_done", "gates_ready"))
        over_ready, over_counted, search, mask_ready, mask_counted = (
            sem(n) for n in ("over_ready", "over_counted", "search", "mask_ready", "mask_counted"))
        picks_ready, picked, folded_ready, idx_turned, idx_ready = (
            sem(n) for n in ("picks_ready", "picked", "folded_ready", "idx_turned", "idx_ready"))

        with nc.Block() as block:
            @block.sync
            def _(sp):
                sp.dma_start(wr[:, :, :], a["L0_ffn_Wr"].rearrange("(t p) e -> p t e", p=P)).then_inc(router_loaded, 16)
                sp.dma_start(br[:, :], a["L0_ffn_br"].rearrange("(a e) -> a e", a=1).to_broadcast([P, E])).then_inc(router_loaded, 16)
                for b in range(B):
                    sp.dma_start(out[b].rearrange("(t p) c -> p t c", p=P), x[:, b, :, :]).then_inc(x_stored, 16)
                for b in range(B):
                    sp.wait_ge(xn_ready, 4 * b + 4)
                    sp.dma_start(rows[512 * b:512 * b + 512, 0:C].rearrange("(t p) c -> p t c", p=P), xn[:, b, :, :])\
                      .then_inc(rows_stored, 16)
                sp.dma_start(w_up[:, :, :, :].rearrange("p g t f -> p (g t) f"),
                             a["L0_ffn_W_up"].rearrange("g (t p) f -> p (g t) f", p=P)).then_inc(up_loaded, 16)
                for g in range(GROUPS):
                    sp.dma_start(b_up[:, g, 0:FT - 1], a["L0_ffn_b_up"][g, 0:(FT - 1) * P].rearrange("(t p) -> p t", p=P),
                                 allow_slow_non_contiguous=True).then_inc(up_loaded, 16)
                sp.dma_start(b_up[0:FR, :, FT - 1], a["L0_ffn_b_up"][:, (FT - 1) * P:F].rearrange("g p -> p g"),
                             allow_slow_non_contiguous=True).then_inc(up_loaded, 16)
                sp.wait_ge(down_cleared, 1)
                for e in range(E):
                    w = a["L0_ffn_W_down"][e]
                    sp.dma_start(w_down[:, e, 0:FT - 1, :], w[0:(FT - 1) * P, :].rearrange("(t p) n -> p t n", p=P))\
                      .then_inc(down_loaded, 16)
                    sp.dma_start(w_down[0:FR, e, FT - 1, :], w[(FT - 1) * P:F, :]).then_inc(down_loaded, 16)
                    sp.dma_start(w_down[BIAS_ROW:BIAS_ROW + 1, e, FT - 1, :], a["L0_ffn_b_down"][e:e + 1, :])\
                      .then_inc(down_loaded, 16)
                sp.wait_ge(gates_ready, 1)
                sp.dma_start(rows[:, C:ROW].rearrange("(t p) e -> p t e", p=P), gates[:, :, :],
                             allow_slow_non_contiguous=True).then_inc(gates_stored, 16)
                sp.wait_ge(x_stored, 16 * B)
                sp.wait_ge(rows_stored, 16 * B)
                sp.wait_ge(gates_stored, 16)

            @block.gpsimd
            def _(pool):
                n = [0]

                def step(ins):
                    ins.then_inc(const_steps, 1)
                    n[0] += 1
                    pool.wait_ge(const_steps, n[0])

                pool.memset(w_down[:, :, FT - 1, :], 0.0).then_inc(down_cleared, 1)
                pool.wait_ge(down_cleared, 1)
                step(pool.memset(ident[:, :], 0.0))
                step(pool.affine_select(out=ident[:, :], in_=ident[:, :], compare_op=ALU.not_equal, fill=1.0, base=0,
                                        pattern=[[-1, P]], channel_multiplier=1))
                step(pool.memset(ones_b[:, :], 1.0))
                step(pool.memset(before[:, :], 1.0))
                step(pool.affine_select(out=before[:, :], in_=before[:, :], compare_op=ALU.is_gt, fill=0.0, base=0,
                                        pattern=[[1, P]], channel_multiplier=-1))
                step(pool.memset(diag[:, :, :], 1.0))
                step(pool.affine_select(out=diag[:, :, :], in_=diag[:, :, :], compare_op=ALU.is_ge, fill=0.0, base=0,
                                        pattern=[[-HI, E], [0, LO]], channel_multiplier=1))
                step(pool.affine_select(out=diag[:, :, :], in_=diag[:, :, :], compare_op=ALU.is_ge, fill=0.0, base=HI - 1,
                                        pattern=[[HI, E], [0, LO]], channel_multiplier=-1))
                step(pool.memset(carry[:, :, :], 1.0))
                step(pool.memset(carry[:, :, 0:1], 0.0))
                step(pool.iota(iota_i[:, 0:T], [[P, T]], base=0, channel_multiplier=1))
                step(pool.iota(iota_i[:, T:T + HI], [[1, HI]], base=1, channel_multiplier=0))
                step(pool.iota(iota_i[:, T + HI:], [[1, LO]], base=0, channel_multiplier=0))
                step(pool.tensor_copy(iota[:, :], iota_i[:, :]))
                step(pool.memset(one_half[:, :], 1.5))
                step(pool.memset(thr[:, :], 0.0))
                step(pool.memset(bit[:, :], 2.0 ** -63))
                step(pool.memset(mid[:, FT - 1, :], 0.0))
                pool.memset(mid[BIAS_ROW:BIAS_ROW + 1, FT - 1, :], 1.0).then_inc(consts_made, 1)
                pool.wait_ge(consts_made, 1)
                pool.wait_ge(ln_guess, 4)
                newton(pool, rstd[:, :], neg_half[:, :], one_half[:, :], square[:, :], ln_rstd, 0)

            @block.vector
            def _(dve):
                n = [0]

                def step(ins):
                    ins.then_inc(chain, 1)
                    n[0] += 1
                    dve.wait_ge(chain, n[0])

                with dve.Fori(0, B) as b:
                    for i in range(NT):
                        dve.bn_stats(stats[:, 4 * b + i, :], x[:, b, i, :]).then_inc(ln_stats, 1)
                dve.wait_ge(ln_stats, T)
                for t in range(T):
                    dve.bn_aggr(meanvar[:, t, :], stats[:, t, :]).then_inc(ln_aggr, 1)
                dve.wait_ge(ln_aggr, T)
                guess(dve, rstd[:, :], veps[:, :], neg_half[:, :], meanvar[:, :, 1], ln_guess, 0)
                dve.wait_ge(ln_rstd, NEWTON_OPS)
                with dve.Fori(0, B) as b:
                    for i in range(NT):
                        dve.tensor_scalar(xn[:, b, i, :], x[:, b, i, :], meanvar[:, 4 * b + i, 0:1],
                                          rstd[:, bass.ds(4 * b + i, 1)], ALU.subtract, ALU.mult).then_inc(xn_ready, 1)
                dve.wait_ge(router_loaded, 32)
                with dve.Fori(0, B) as b:
                    dve.wait_ge(logits_done, b + 1)
                    dve.tensor_tensor(logits[:, bass.ds(4 * b, 4), :], logit_ps[:, 0:NT * E].rearrange("p (t e) -> p t e", e=E),
                                      br[:, :].unsqueeze(1).broadcast_to([P, NT, E]), ALU.add).then_inc(logits_kept, 1)
                dve.wait_ge(logits_kept, B)
                step(dve.tensor_reduce(red[:, :], logits[:, :, :], AX.X, ALU.max))
                dve.tensor_tensor(logits[:, :, :], logits[:, :, :], red[:, :].unsqueeze(2).broadcast_to([P, T, E]),
                                  ALU.subtract).then_inc(shifted, 1)
                dve.wait_ge(exps_done, 1)
                step(dve.tensor_reduce(red[:, :], logits[:, :, :], AX.X, ALU.add))
                step(dve.reciprocal(red[:, :], red[:, :]))
                dve.tensor_tensor(gates[:, :, :], logits[:, :, :], red[:, :].unsqueeze(2).broadcast_to([P, T, E]),
                                  ALU.mult).then_inc(gates_ready, 1)
                dve.wait_ge(gates_ready, 1)
                step(dve.tensor_copy(gates_e[:, :, :], gates[:, :, :].rearrange("p t e -> p e t")))
                dve.wait_ge(consts_made, 1)

                def wide(v):
                    return v[:, :].unsqueeze(2).broadcast_to([P, E, T])

                with dve.Fori(0, BITS) as k:
                    dve.tensor_tensor(trial[:, :].bitcast(U32), thr[:, :].bitcast(U32), bit[:, :].bitcast(U32),
                                      ALU.bitwise_or).then_inc(search, 1)
                    dve.wait_ge(search, 5 * k + 1)
                    dve.tensor_tensor(over[:, :, :], gates_e[:, :, :], wide(trial), ALU.is_ge).then_inc(over_ready, 1)
                    dve.tensor_scalar(bit[:, :].bitcast(U32), bit[:, :].bitcast(U32), 1, None,
                                      ALU.logical_shift_right).then_inc(search, 1)
                    dve.wait_ge(over_counted, k + 1)
                    dve.tensor_reduce(count[:, :], count_ps[:, 0:E * T].rearrange("p (e t) -> p e t", e=E), AX.X, ALU.add)\
                       .then_inc(search, 1)
                    dve.wait_ge(search, 5 * k + 3)
                    dve.scalar_tensor_tensor(out=trial[:, :], in0=count[:, :], scalar=float(CAP), in1=trial[:, :],
                                             op0=ALU.is_ge, op1=ALU.mult).then_inc(search, 1)
                    dve.wait_ge(search, 5 * k + 4)
                    dve.tensor_tensor(thr[:, :], thr[:, :], trial[:, :], ALU.max).then_inc(search, 1)
                    dve.wait_ge(search, 5 * k + 5)
                step(dve.tensor_tensor(gt[:, :, :], gates_e[:, :, :], wide(thr), ALU.is_gt))
                dve.tensor_tensor(eq[:, :, :], gates_e[:, :, :], wide(thr), ALU.is_equal).then_inc(mask_ready, 1)
                dve.wait_ge(mask_counted, 1)
                step(dve.tensor_reduce(count[:, :], count_ps[:, 0:E * T].rearrange("p (e t) -> p e t", e=E), AX.X, ALU.add))
                step(dve.tensor_scalar(need[:, :], count[:, :], -1.0, float(CAP), ALU.mult, ALU.add))

                def ranks(bank):
                    step(dve.tensor_copy(tile_sum[:, :, :].rearrange("p e t -> p (e t)"), bank[:, 256:512]))
                    step(dve.tensor_tensor_scan(rank[:, :, :].rearrange("p e t -> p (e t)"),
                                                carry[:, :, :].rearrange("p e t -> p (e t)"),
                                                tile_sum[:, :, :].rearrange("p e t -> p (e t)"), 0.0, ALU.mult, ALU.add))
                    step(dve.tensor_tensor(rank[:, :, :], rank[:, :, :], tile_sum[:, :, :], ALU.subtract))
                    step(dve.tensor_tensor(rank[:, :, :].rearrange("p e t -> p (e t)"),
                                           rank[:, :, :].rearrange("p e t -> p (e t)"), bank[:, 0:256], ALU.add))

                ranks(rank_ps)
                step(dve.tensor_tensor(rank[:, :, :], rank[:, :, :], wide(need), ALU.is_lt))
                step(dve.tensor_tensor(sel[:, :, :], rank[:, :, :], eq[:, :, :], ALU.mult))
                step(dve.tensor_tensor(sel[:, :, :], sel[:, :, :], gt[:, :, :], ALU.add))
                dve.tensor_scalar(over[:, :, :], sel[:, :, :], 1.0, None, ALU.mult).then_inc(mask_ready, 1)
                dve.wait_ge(mask_counted, 2)
                ranks(rank_ps)
                step(dve.tensor_copy(place_i[:, :, :], rank[:, :, :]))
                step(dve.tensor_scalar(hi_i[:, :, :], place_i[:, :, :], 5, None, ALU.logical_shift_right))
                step(dve.tensor_scalar(lo_i[:, :, :], place_i[:, :, :], LO - 1, None, ALU.bitwise_and))
                step(dve.tensor_copy(hi[:, :, :], hi_i[:, :, :]))
                step(dve.tensor_copy(lo[:, :, :], lo_i[:, :, :]))
                step(dve.scalar_tensor_tensor(out=hi[:, :, :], in0=hi[:, :, :], scalar=1.0, in1=sel[:, :, :],
                                              op0=ALU.add, op1=ALU.mult))
                dve.wait_ge(rows_stored, 16 * B)
                for t in range(0, T, 4):
                    for e_major, table, pick, width in ((hi, count_hi, pick_hi, HI), (lo, count_lo, pick_lo, LO)):
                        for tt in range(t, t + 4):
                            ins = dve.tensor_tensor(pick[:, tt, :, :], e_major[:, :, tt:tt + 1].broadcast_to([P, E, width]),
                                                    table.unsqueeze(1).broadcast_to([P, E, width]), ALU.is_equal)
                    step(ins)
                    for tt in range(t, t + 4):
                        ins = dve.tensor_scalar(pick_lo[:, tt, :, :], pick_lo[:, tt, :, :], tok[:, tt:tt + 1], None, ALU.mult)
                    ins.then_inc(picks_ready, 1)
                dve.wait_ge(picked, 1)
                step(dve.tensor_tensor(own[:, :, :], idx_ps[:, 0:E * LO].rearrange("p (e l) -> p e l", e=E),
                                       diag[:, :, :], ALU.mult))
                dve.tensor_reduce(folded[:, :], own[:, :, :].rearrange("p e l -> p l e"), AX.X, ALU.add).then_inc(folded_ready, 1)
                dve.wait_ge(idx_turned, 1)
                for r in range(4):
                    dve.tensor_copy(idx[32 * r:32 * r + 32, :], idxT_ps[0:32, 0:P].rearrange("l (c r) -> l c r", r=4)[:, :, r])\
                       .then_inc(idx_ready, 1)

            @block.scalar
            def _(act):
                with act.Fori(0, B) as b:
                    for c in range(2):
                        act.wait_ge(turned, 2 * b + c + 1)
                        act.activation(xT[:, c, :], turn_ps[c][:, :], ACT.Copy).then_inc(turned_kept, 1)
                act.wait_ge(shifted, 1)
                act.activation(logits[:, :, :], logits[:, :, :], ACT.Exp).then_inc(exps_done, 1)

            @block.tensor
            def _(pe):
                pe.wait_ge(consts_made, 1)
                pe.wait_ge(router_loaded, 32)

                def batch(b, first):
                    pe.wait_ge(xn_ready, 4 * b + 4)
                    for c in range(2):
                        for i in range(NT):
                            ins = pe.transpose(turn_ps[c][:, i * P:(i + 1) * P],
                                               xn_static(b, i, c), ident[:, :])
                        ins.then_inc(turned, 1)
                    pe.wait_ge(turned_kept, 2 * b + 2)
                    if not first:
                        pe.wait_ge(logits_kept, b)
                    for i in range(NT):
                        for c in range(2):
                            ins = pe.matmul(logit_ps[:, i * E:(i + 1) * E], xT[:, c, i * P:(i + 1) * P], wr[:, c, :],
                                            start=c == 0, stop=c == 1)
                    ins.then_inc(logits_done, 1)

                def xn_static(b, i, c):
                    return xn[:, b, i, c * P:(c + 1) * P]

                for b in range(B):
                    batch(b, b == 0)
                with pe.Fori(0, BITS) as k:
                    pe.wait_ge(over_ready, k + 1)
                    pe.matmul(count_ps[:, 0:E * T], ones_b[:, :], over[:, :, :].rearrange("p e t -> p (e t)"),
                              start=True, stop=True).then_inc(over_counted, 1)
                flat = [m[:, :, :].rearrange("p e t -> p (e t)") for m in (gt, eq, over)]
                pe.wait_ge(mask_ready, 1)
                pe.matmul(count_ps[:, 0:E * T], ones_b[:, :], flat[0], start=True, stop=True)
                pe.matmul(rank_ps[:, 0:256], before[:, :], flat[1], start=True, stop=True)
                pe.matmul(rank_ps[:, 256:512], ones_b[:, :], flat[1], start=True, stop=True).then_inc(mask_counted, 1)
                pe.wait_ge(mask_ready, 2)
                pe.matmul(rank_ps[:, 0:256], before[:, :], flat[2], start=True, stop=True)
                pe.matmul(rank_ps[:, 256:512], ones_b[:, :], flat[2], start=True, stop=True).then_inc(mask_counted, 1)
                for t in range(T):
                    if t % 4 == 0:
                        pe.wait_ge(picks_ready, t // 4 + 1)
                    ins = pe.matmul(idx_ps[:, 0:E * LO], pick_hi[:, t, :, :].rearrange("p e h -> p (e h)"),
                                    pick_lo[:, t, :, :].rearrange("p e l -> p (e l)"), start=t == 0, stop=t == T - 1)
                ins.then_inc(picked, 1)
                pe.wait_ge(folded_ready, 1)
                pe.transpose(idxT_ps[0:LO, 0:P], folded[:, :], ident[:, :]).then_inc(idx_turned, 1)

    taken = [sb(f"taken{i}", [P, Q, ROW]) for i in range(2)]
    takenT = sb("takenT", [P, 2, CAP])
    made = [sb(f"made{i}", [P, Q, C]) for i in range(2)]
    turn_ps = [outer.enter_context(nc.psum_tensor(f"exp_turn{i}", [P, 512], F32)) for i in range(2)]
    up_ps = [outer.enter_context(nc.psum_tensor(f"exp_up{i}", [P, 512], F32)) for i in range(2)]
    down_ps = [outer.enter_context(nc.psum_tensor(f"exp_down{i}", [P, 512], F32)) for i in range(2)]
    gathered = [sem(f"gathered{i}") for i in range(2)]
    added, turned2, turned2_kept, up_done, silu_done, down_done, made_ready = (
        sem("e_" + n) for n in ("added", "turned", "turned_kept", "up_done", "silu_done", "down_done", "made_ready"))
    out_rows = out.rearrange("b n c -> (b n) c")

    with nc.Block() as block:
        @block.gpsimd
        def _(pool):
            def gather(e):
                if e >= 2:
                    pool.wait_ge(made_ready, Q * (e - 1))
                for q in range(Q):
                    pool.indirect_dma_start(
                        out=taken[e % 2][:, q, :], out_offset=None, in_=rows[:, :],
                        in_offset=bass.IndirectOffsetOnAxis(ap=idx[:, e * Q + q:e * Q + q + 1], axis=0),
                        ).then_inc(gathered[e % 2], 16)

            gather(0)
            for e in range(E):
                if e + 1 < E:
                    gather(e + 1)
                if e >= 1:
                    pool.wait_ge(added, 16 * Q * e)
                for q in range(Q):
                    pool.wait_ge(made_ready, Q * e + q + 1)
                    pool.indirect_dma_start(
                        out=out_rows, out_offset=bass.IndirectOffsetOnAxis(ap=idx[:, e * Q + q:e * Q + q + 1], axis=0),
                        in_=made[e % 2][:, q, :], in_offset=None, compute_op=ALU.add).then_inc(added, 16)
            pool.wait_ge(added, 16 * Q * E)

        @block.tensor
        def _(pe):
            def turn(e):
                pe.wait_ge(gathered[e % 2], 16 * Q * (e // 2 + 1))
                for c in range(2):
                    for q in range(Q):
                        ins = pe.transpose(turn_ps[c][:, q * P:(q + 1) * P], taken[e % 2][:, q, c * P:(c + 1) * P], ident[:, :])
                    ins.then_inc(turned2, 1)

            def up(e):
                pe.wait_ge(turned2_kept, 2 * e + 2)
                for f in range(FT):
                    n = FT * e + f
                    if n >= 2:
                        pe.wait_ge(silu_done, n - 1)
                    w = P if f < FT - 1 else FR
                    for c in range(2):
                        ins = pe.matmul(up_ps[n % 2][0:w, :], w_up[:, e // PER_GROUP, c, f * P:f * P + w], takenT[:, c, :],
                                        start=c == 0, stop=c == 1)
                    ins.then_inc(up_done, 1)

            def down(e):
                pe.wait_ge(silu_done, FT * e + FT)
                for q in range(Q):
                    n = Q * e + q
                    if n >= 2:
                        pe.wait_ge(made_ready, n - 1)
                    for f in range(FT):
                        w = P if f < FT - 1 else BIAS_ROW + 1
                        ins = pe.matmul(down_ps[n % 2][:, 0:C], mid[0:w, f, q * P:(q + 1) * P], w_down[0:w, e, f, :],
                                        start=f == 0, stop=f == FT - 1)
                    ins.then_inc(down_done, 1)

            pe.wait_ge(up_loaded, 16 * UP_DMAS)
            pe.wait_ge(down_loaded, 16 * DOWN_DMAS)
            turn(0)
            for e in range(E):
                up(e)
                if e + 1 < E:
                    turn(e + 1)
                down(e)

        @block.scalar
        def _(act):
            act.wait_ge(up_loaded, 16 * UP_DMAS)
            for e in range(E):
                for f in range(FT):
                    n = FT * e + f
                    w = P if f < FT - 1 else FR
                    act.wait_ge(up_done, n + 1)
                    act.activation(mid[0:w, f, :], up_ps[n % 2][0:w, :], ACT.Silu,
                                   bias=b_up[0:w, e // PER_GROUP, f:f + 1]).then_inc(silu_done, 1)

        @block.vector
        def _(dve):
            def keep_turned(e):
                for c in range(2):
                    dve.wait_ge(turned2, 2 * e + c + 1)
                    dve.wait_ge(up_done, FT * e) if e else None
                    dve.tensor_copy(takenT[:, c, :], turn_ps[c][:, :]).then_inc(turned2_kept, 1)

            keep_turned(0)
            for e in range(E):
                if e + 1 < E:
                    keep_turned(e + 1)
                if e >= 2:
                    dve.wait_ge(added, 16 * Q * (e - 1))
                for q in range(Q):
                    n = Q * e + q
                    dve.wait_ge(down_done, n + 1)
                    dve.tensor_scalar(made[e % 2][:, q, :], down_ps[n % 2][:, 0:C], taken[e % 2][:, q, C + e:C + e + 1],
                                      None, ALU.mult).then_inc(made_ready, 1)


def make_consts(nc, stack):
    def sb(n, shape, dt=F32):
        return stack.enter_context(nc.sbuf_tensor(n, shape, dt))

    c = {"ident": sb("ident", [P, P]), "ones": sb("ones", [P, P]), "spread": sb("spread", [P, P]),
         "ident_b": sb("ident_b", [P, P], BF16), "mask_qk": sb("mask_qk", [P, P], BF16),
         "mask_kq": sb("mask_kq", [P, P], BF16)}
    cleared, made = stack.enter_context(nc.semaphore("cleared")), stack.enter_context(nc.semaphore("made"))
    with nc.Block() as block:
        @block.gpsimd
        def _(pool):
            for n, v in (("ident", 0.0), ("spread", 0.0), ("ident_b", 0.0), ("mask_qk", 0.0), ("mask_kq", 0.0),
                         ("ones", 1.0)):
                pool.memset(c[n][:, :], v).then_inc(cleared, 1)
            pool.wait_ge(cleared, 6)
            for n in ("ident", "ident_b"):
                pool.affine_select(out=c[n][:, :], in_=c[n][:, :], compare_op=ALU.not_equal, fill=1.0, base=0,
                                   pattern=[[-1, P]], channel_multiplier=1).then_inc(made, 1)
            s = c["spread"][:, :].rearrange("p (j m) -> p j m", j=4)
            pool.affine_select(out=s, in_=s, compare_op=ALU.not_equal, fill=1.0, base=-16,
                               pattern=[[-32, 4], [0, 32]], channel_multiplier=1).then_inc(made, 1)
            pool.affine_select(out=c["mask_qk"][:, :], in_=c["mask_qk"][:, :], compare_op=ALU.is_ge, fill=MASKED,
                               base=0, pattern=[[-1, P]], channel_multiplier=1).then_inc(made, 1)
            pool.affine_select(out=c["mask_kq"][:, :], in_=c["mask_kq"][:, :], compare_op=ALU.is_ge, fill=MASKED,
                               base=0, pattern=[[1, P]], channel_multiplier=-1).then_inc(made, 1)
            pool.wait_ge(made, 5)
    return c


def decoder_block(nc, a, out, until=3):
    B, N, C = a["x"].shape
    with ExitStack() as whole:
        x = whole.enter_context(nc.sbuf_tensor("x_sb", [P, B, N // P, C], F32))
        with ExitStack() as s:
            consts = make_consts(nc, s)
            with ExitStack() as phase:
                attention(nc, phase, "self", False, x, a["x"], {n: a["L0_attn_" + n] for n in ("Wq", "Wk", "Wv", "Wo")}, consts)
            if until >= 2:
                with ExitStack() as phase:
                    attention(nc, phase, "cross", True, x, a["ctx_768"],
                          {n: a["L0_xattn_" + n] for n in ("Wq", "Wk", "Wv", "Wo", "bq", "bk", "bv", "bo")}, consts)
        if until < 3:
            st = whole.enter_context(nc.semaphore("st"))
            with nc.Block() as block:
                @block.sync
                def _(sp):
                    for b in range(B):
                        sp.dma_start(out[b].rearrange("(t p) c -> p t c", p=P), x[:, b, :, :]).then_inc(st, 16)
                    sp.wait_ge(st, 16 * B)
        else:
            expert_choice(nc, whole, x, a, out)


_INS = ["x", "ctx_768", "L0_attn_Wq", "L0_attn_Wk", "L0_attn_Wv", "L0_attn_Wo", "L0_xattn_Wq", "L0_xattn_bq",
        "L0_xattn_Wk", "L0_xattn_bk", "L0_xattn_Wv", "L0_xattn_bv", "L0_xattn_Wo", "L0_xattn_bo", "L0_ffn_Wr",
        "L0_ffn_br", "L0_ffn_W_up", "L0_ffn_b_up", "L0_ffn_W_down", "L0_ffn_b_down"]
_OUTS = [((8, 512, 256), "float32")]


def kernel(**inputs):
    import numpy as _np
    import concourse.bacc as _bacc
    from concourse import mybir as _mybir
    from concourse.bass_utils import run_bass_kernel_spmd as _run

    nc = _bacc.Bacc("TRN2", target_bir_lowering=False, num_devices=1)
    arrays, args = {}, {}
    for name in _INS:
        v = _np.ascontiguousarray(inputs[name])
        arrays[f"in_{name}_dram"] = v
        args[name] = nc.dram_tensor(f"in_{name}_dram", v.shape, _mybir.dt.from_np(v.dtype), kind="ExternalInput").ap()
    (shape, dtype), = _OUTS
    out = nc.dram_tensor("out_0_dram", shape, _mybir.dt.from_np(_np.dtype(dtype)), kind="ExternalOutput").ap()
    decoder_block(nc, args, out)
    r = _run(nc, [arrays], core_ids=[0])
    return r.results[0]["out_0_dram"]
```

```python
from contextlib import ExitStack

import concourse.bass as bass
from concourse import mybir

F32, BF16, F16 = mybir.dt.float32, mybir.dt.bfloat16, mybir.dt.float16
U32, I32 = mybir.dt.uint32, mybir.dt.int32
ALU = mybir.AluOpType
ACT = mybir.ActivationFunctionType
AX = mybir.AxisListType

P = 128
SHIFT_UNIT = 64.0
MASKED = -1.0e30
LN_EPS = 1e-5
RSQRT_BITS = float(0x5F3759DF)
NEWTON_STEPS = 3
NEWTON_OPS = 4 * NEWTON_STEPS
SHIFT_ROW = 96
STACK = 98
SHIFT_DMA = 2 * 16
CLAMP = 10000.0
RINV_SCALE = 1024.0


def ahead(b, g, d):
    return b + (g + d) // 4, (g + d) % 4


def guess(dve, y, v, neg_half, var, semaphore, before):
    dve.tensor_scalar(v, var, LN_EPS, None, ALU.add).then_inc(semaphore, 1)
    dve.wait_ge(semaphore, before + 1)
    dve.tensor_scalar(y.bitcast(U32), v.bitcast(U32), 1, None, ALU.logical_shift_right).then_inc(semaphore, 1)
    dve.tensor_scalar(neg_half, v, -0.5, None, ALU.mult).then_inc(semaphore, 1)
    dve.wait_ge(semaphore, before + 3)
    dve.tensor_scalar(y.bitcast(I32), y.bitcast(I32), -1.0, RSQRT_BITS, ALU.mult, ALU.add).then_inc(semaphore, 1)


def newton(pool, y, neg_half, one_half, t, semaphore, before):
    n = before
    for _ in range(NEWTON_STEPS):
        for out, in0, in1, op in ((t, y, y, ALU.mult), (t, t, neg_half, ALU.mult), (t, t, one_half, ALU.add),
                                  (y, y, t, ALU.mult)):
            pool.tensor_tensor(out, in0, in1, op).then_inc(semaphore, 1)
            n = n + 1
            pool.wait_ge(semaphore, n)


def between(cross, first, last, g, j):
    if g == 1 and not last and j < (2 if cross else 4):
        return [("q", j), ("k", j)]
    if g == 2 and j == 0 and not first:
        return [("wo", 0), ("wo", 1)]
    return []


class WorkBanks:

    def __init__(self, cross, batches, banks, clip):
        self.cross, self.batches, self.clip = cross, batches, clip
        self.table, self.count = {}, [0] * banks
        self.turn = 0
        for key in self.prologue():
            self._add(("pro",) + key)
        for b in range(batches):
            self.turn = 0
            for g in range(4):
                uses = self.step(b, g)
                for key in uses if b else self.step(1, g):
                    if key in uses:
                        self._add((b, g) + key)
                    else:
                        self.turn += 1
        for key in (("sp", 0), ("sp", 1), ("wo", 0), ("wo", 1)):
            self._add(("epi",) + key)

    def _add(self, key):
        bank = self.turn % len(self.count)
        self.turn += 1
        self.table[key] = (bank, self.count[bank])
        self.count[bank] += 1

    def prologue(self):
        out = [("tr", i) for i in range(4 if self.cross else 2)]
        for n in range(2 if self.cross else 4):
            out += [("q", n), ("k", n)]
        return out + [("mx", j, i) for j in range(4) for i in range(4)] + [("mt",)] + [
            ("mx", j, i) for j in (4, 5) for i in range(4)]

    def step(self, b, g):
        last = b == self.batches - 1
        out = []
        for j in range(4):
            head, there = (j + 2) % 4, not (last and g >= (3 if j < 2 else 2))
            out += [("mx", head, i) for i in (0, 1) if there]
            if j == 2 and not (last and g == 3):
                out += [("mt",)]
            extra = between(self.cross, b == 0, last, g, j)
            out += extra[:1]
            out += [("mx", head, i) for i in (2, 3) if there]
            out += extra[1:]
            if j == 3 and (b >= 1 or g >= 2):
                out += [("sp",)]
            if self.clip:
                out += [("fl", j)]
        if g == 0:
            out += [("v", i) for i in range(2 if self.cross else 4)]
        if g == 0 and not last:
            out += [("tr", i) for i in range(4 if self.cross else 2)]
        return out

    def at(self, section, *key):
        if isinstance(section, (str, int)):
            return self.table[(section,) + key]
        bank, one = self.table[(1,) + key]
        again, two = self.table[(2,) + key]
        assert bank == again
        return bank, section * (two - one) + (2 * one - two)


def attention(nc, stack, name, cross, x, src, weights, consts, guard=None, mode="plain", keep=None):
    clip, uniform = mode == "clip", mode == "uniform"
    B, NT, C = x.shape[1], x.shape[2], x.shape[3]
    last_batch = B - 1
    CD = 16 if cross else 32
    CK = src.shape[-1]
    KT = [(0, P), (1, CK - P)]
    NV = 16 * CD
    SCALE = 0.25
    WID = [512] * 4 if cross else [512, 384, 256, 128]
    Q0 = [512 - w for w in WID]
    OFF = [0, 512, 1024, 1536] if cross else [0, 512, 1024, 1280]
    EXP = [1024, 1024] if cross else [896, 384]
    SPLIT = CD
    WORK = 3
    banks = WorkBanks(cross, B, WORK, clip)
    V_USES = 2 if cross else 4
    TILES = 16 * CD // P
    RESTACKS = 3 * (2 if cross else 1)
    PER_UNIT = 16 * RESTACKS
    WEIGHTS = 4 * TILES + (16 if cross else 3)
    ident, mask_qk, mask_kq, ident_b = consts["ident"], consts["mask_qk"], consts["mask_kq"], consts["ident_b"]

    def sb(n, shape, dt=F32):
        return stack.enter_context(nc.sbuf_tensor(f"{name}_{n}", shape, dt))

    def ps(n, shape):
        return stack.enter_context(nc.psum_tensor(f"{name}_{n}", shape, F32))

    semaphores = []
    stack.callback(nc.all_engine_barrier)
    stack.callback(lambda: nc.clear_and_free_semaphores(semaphores))

    def sem(n):
        semaphores.append(nc.alloc_semaphore(f"{name}_{n}"))
        return semaphores[-1]

    wq = sb("wq", [P, 2, 16 * CD])
    wk = sb("wk", [P, 2, 16 * CD])
    wv = sb("wv", [P, 2, NV])
    wo = sb("wo", [P, 4, C])
    xn = sb("xn", [P, NT, C])
    stats = sb("stats", [P, NT, 6])
    meanvar = sb("meanvar", [P, NT, 2])
    rstd = sb("rstd", [P, NT])
    veps, square, neg_half, one_half = (sb(n, [P, NT]) for n in ("veps", "square", "neg_half", "one_half"))
    wait_cell = sb("wait_cell", [P, 1])
    xnT = sb("xnT", [P, 2, 512])
    qh, ql, kh, kl = (sb(n, [P, TILES, 512], F16) for n in ("qh", "ql", "kh", "kl"))
    qs = sb("qs", [P, 4, 4, 512], F16)
    ks = sb("ks", [P, 4, 4, 512], F16)
    rowmax = sb("rowmax", [P, 2, 16])
    shift_h = sb("shift_h", [16, 2, P], F16)
    shift_l = sb("shift_l", [16, 2, P], F16)
    probs = sb("probs", [P, 2, 4, 2048])
    attT = sb("attT", [P, 4, 512])
    raw = sb("raw", [P, 512])
    sums_c, rinv_c = sb("sums_c", [P, 16]), sb("rinv_c", [P, 16])
    rinv_cs = sb("rinv_cs", [P, 2, 16], F16)
    rinv_rows = sb("rinv_rows", [P, 512], F16)
    if cross:
        ctx_in = sb("ctx_in", [P, NT, 2 * P])
        ctxT = sb("ctxT", [P, 2, 512])
        val = sb("val", [P, 4, 16, 32])
        bq, bk = sb("bq", [P, 2]), sb("bk", [P, 2])
        bv, bo = sb("bv", [P, NV]), sb("bo", [P, C])
        is_nan = sb("is_nan", [P, 16])
    if uniform:
        zeros = sb("zeros", [P, 512])
    if clip:
        floor_w = sb("floor_w", [P, P], F16)
        floor_bias = sb("floor_bias", [P, 1])
        floors = sb("floors", [P, 512])
        odd, odd_max = sb("odd", [P, 512]), sb("odd_max", [P, 1])
    if not cross:
        val = sb("val", [P, 4, NV])
        sums = sb("sums", [P, 512])
    kvT = ctxT if cross else xnT

    work = [ps(f"work{i}", [P, 512]) for i in range(WORK)]
    score = [ps("score0", [P, 1024]), ps("score1", [P, 1024 if cross else 512])]
    out_ps = ps("out_ps", [P, 512])
    if not cross:
        sum_ps = ps("sum_ps", [P, 512])

    full = [sem(f"work{i}_filled") for i in range(WORK)]
    free = [sem(f"work{i}_freed") for i in range(WORK)]
    weights_loaded, consts_set = sem("weights_loaded"), sem("consts_set")
    first_loaded, src_loaded = sem("first_loaded"), sem("src_loaded")
    ln_guess = sem("ln_guess")
    ln_stats, ln_aggr, ln_rstd, xn_ready = sem("ln_stats"), sem("ln_aggr"), sem("ln_rstd"), sem("xn_ready")
    hi_ready = sem("hi_ready")
    restacked = {w: [sem(f"{w}_restacked{g}") for g in range(4)] for w in "qk"}
    shift_hi = sem("shift_hi")
    shift_placed = [sem("shift_placed0"), sem("shift_placed1")]
    scores_ready, exp_done = sem("scores_ready"), sem("exp_done")
    pv_done, raw_ready, sums_moved = sem("pv_done"), sem("raw_ready"), sem("sums_moved")
    rinv_steps, rinv_placed = sem("rinv_steps"), sem("rinv_placed")
    if cross:
        bo_added, noted, x_kept = sem("bo_added"), sem("noted"), sem("x_kept")
        nan_noted = sem("nan_noted")
    if clip:
        scores_bounded, maxima_clipped = sem("scores_bounded"), sem("maxima_clipped")
        probs_clipped, odd_steps = sem("probs_clipped"), sem("odd_steps")

    def unit(b, g):
        return 4 * b + g

    def turns(b, g):
        return 2 * b + g // 2

    def wait(eng, semaphore, value):
        if not isinstance(value, int) or value > 0:
            eng.wait_ge(semaphore, value)

    def fill(eng, use):
        bank, n = use
        wait(eng, free[bank], n)
        return work[bank]

    def filled(eng, use):
        bank, n = use
        eng.wait_ge(full[bank], n + 1)
        return work[bank]

    def freed(eng, use):
        eng.wait_ge(free[use[0]], use[1] + 1)

    N_TR = 4 if cross else 2

    def last_transposes(b, section):
        if isinstance(b, int) and b == 0:
            return [banks.at("pro", "tr", i) for i in range(N_TR)]
        return [banks.at(section, 0, "tr", i) for i in range(N_TR)]

    def transposed(eng, b):
        eng.wait_ge(hi_ready, 2 * TILES * b + 1)

    def maxima_of(j, g, last):
        if j < 2:
            return None if last and g == 3 else (1, j + 2)
        return None if last and g >= 2 else (2, j - 2)

    def restack(eng, what, g):
        dst, parts = (qs, (qh, qh, ql)) if what == "q" else (ks, (kh, kl, kh))
        for s, part in enumerate(parts):
            to = dst[SPLIT * s:SPLIT * s + SPLIT, g, :, :]
            for r in range(32 // CD):
                row = 32 * g + CD * r
                eng.dma_start(to if CD == 32 else to.rearrange("p (t r) n -> p r t n", t=2)[:, r],
                              part[row:row + CD, :, :]).then_inc(restacked[what][g], 16)

    def steps(eng, emit, prologue, epilogue):
        prologue()
        for g in range(4):
            emit(0, g, True, False)
        with eng.Fori(1, last_batch) as b:
            for g in range(4):
                emit(b, g, False, False)
        for g in range(4):
            emit(last_batch, g, False, True)
        epilogue()

    block = stack.enter_context(nc.Block())

    @block.sync
    def _(sp):
        if not cross:
            sp.dma_start(x[:, 0, :, :], src[0].rearrange("(t p) c -> p t c", p=P)).then_inc(first_loaded, 16)
        for w_sb, w, tiles in ((wq, weights["Wq"], [(0, P), (1, P)]), (wk, weights["Wk"], KT)):
            for t, rows in tiles:
                columns = w[t * P:t * P + rows, :].rearrange("p (g m k) -> p m g k", g=4, k=32)
                for m in range(TILES):
                    sp.dma_start(w_sb[0:rows, t, m * P:(m + 1) * P].rearrange("p (g k) -> p g k", g=4), columns[:, m])\
                      .then_inc(weights_loaded, 16)
        for t, rows in KT:
            sp.dma_start(wv[0:rows, t, :], weights["Wv"][t * P:t * P + rows, :]).then_inc(weights_loaded, 16)
        if cross:
            sp.wait_ge(consts_set, 7)
            for j in range(4):
                sp.dma_start(wo[32 * j:32 * j + CD, :, :], weights["Wo"].rearrange(
                    "(g j r) n -> j r g n", g=4, j=4)[j]).then_inc(weights_loaded, 16)
            for b_sb, w in ((bq, weights["bq"]), (bk, weights["bk"])):
                for g in range(4):
                    sp.dma_start(b_sb[32 * g:32 * g + 32, :], w[64 * g:64 * g + 64].rearrange("(t k) -> k t", t=2),
                                 allow_slow_non_contiguous=True).then_inc(weights_loaded, 16)
            sp.dma_start(bv[:, :], weights["bv"].rearrange("(a n) -> a n", a=1).to_broadcast([P, NV])).then_inc(weights_loaded, 16)
            sp.dma_start(bo[:, :], weights["bo"].rearrange("(a n) -> a n", a=1).to_broadcast([P, C])).then_inc(weights_loaded, 16)
        else:
            sp.dma_start(wo[:, :, :], weights["Wo"].rearrange("(g p) n -> p g n", p=P)).then_inc(weights_loaded, 16)

        def load_context(b):
            if not (isinstance(b, int) and b == 0):
                transposed(sp, b - 1)
            sp.dma_start(ctx_in[:, :, 0:CK], src[b].rearrange("(t p) c -> p t c", p=P)).then_inc(src_loaded, 16)

        def place_shift(b, g, section, key):
            freed(sp, banks.at(section, *key, "mt"))
            for r, part in enumerate((shift_h, shift_l)):
                sp.dma_start(qs[SHIFT_ROW + r:SHIFT_ROW + r + 1, g, :, :].rearrange("p j (i c) -> p (j i) c", c=P),
                             part[:, g % 2, :]).then_inc(shift_placed[g % 2], 16)

        def prologue():
            if cross:
                load_context(0)
            if keep is not None:
                for b in range(B):
                    sp.dma_start(keep[b].rearrange("(t p) c -> p t c", p=P), x[:, b, :, :]).then_inc(x_kept, 16)
            sp.wait_ge(consts_set, 5)
            freed(sp, banks.at("pro", "k", TILES - 1))
            for g in range(3):
                restack(sp, "q", g)
                restack(sp, "k", g)
            place_shift(0, 0, "pro", ())

        def gather_sums(b, g):
            sp.wait_ge(raw_ready, unit(b, g) + 1)
            sp.dma_start(sums_c[:, :], raw[CD:P:32, :] if cross else sums[0:P:32, :]).then_inc(sums_moved, 16)

        def place_reciprocals(b, g):
            sp.wait_ge(rinv_steps, 3 * unit(b, g) + 3)
            for part in range(2):
                sp.dma_start(rinv_rows[4 * part:4 * part + 4, :], rinv_cs[:, part, :]).then_inc(rinv_placed, 16)

        def emit(b, g, first, last):
            u = unit(b, g)
            summed = not (first and g < 2)
            if summed:
                gather_sums(*ahead(b, g, -2))
            if cross and g == 0 and not last:
                load_context(b + 1)
            if g == 0:
                if not first:
                    restack(sp, "k", 2)
                wait(sp, scores_ready, 8 * u)
                restack(sp, "q", 3)
            if g == 3 and not last:
                restack(sp, "k", 1)
            if summed:
                place_reciprocals(*ahead(b, g, -2))
            if g == 3 and not last:
                sp.wait_ge(scores_ready, 8 * u)
                restack(sp, "q", 2)
            if not (last and g == 3):
                place_shift(*ahead(b, g, 1), b, (g,))
            if g == 0:
                restack(sp, "k", 3)
            if g == 1 and not last:
                freed(sp, banks.at(b, 1, "k", TILES - 1))
                restack(sp, "q", 0)
                restack(sp, "k", 0)
            if g == 2 and not last:
                restack(sp, "q", 1)

        def epilogue():
            for g in (2, 3):
                gather_sums(last_batch, g)
                place_reciprocals(last_batch, g)

        steps(sp, emit, prologue, epilogue)

    @block.gpsimd
    def _(pool):
        if not cross:
            for b in range(1, B):
                wait(pool, src_loaded, 16 * (b - 1))
                pool.dma_start(x[:, b, :, :], src[b].rearrange("(t p) c -> p t c", p=P)).then_inc(src_loaded, 16)
        pool.memset(qs[:, :, :, :], 0.0).then_inc(consts_set, 1)
        pool.memset(ks[:, :, :, :], 0.0).then_inc(consts_set, 1)
        pool.wait_ge(consts_set, 2)
        pool.memset(ks[SHIFT_ROW:SHIFT_ROW + 2, :, :, :], SHIFT_UNIT).then_inc(consts_set, 1)
        pool.wait_ge(consts_set, 3)
        pool.memset(one_half[:, :], 1.5).then_inc(consts_set, 1)
        pool.wait_ge(consts_set, 4)
        pool.memset(rinv_rows[:, :], 0.0).then_inc(consts_set, 1)
        pool.wait_ge(consts_set, 5)
        if cross:
            pool.memset(ctx_in[:, :, CK:], 0.0).then_inc(consts_set, 1)
            pool.memset(wo[:, :, :], 0.0).then_inc(consts_set, 1)
            pool.memset(val[:, :, :, CD:], 1.0).then_inc(consts_set, 1)
            if uniform:
                pool.memset(zeros[:, :], 0.0).then_inc(consts_set, 1)
            if clip:
                pool.memset(floor_w[:, :], 0.0).then_inc(consts_set, 1)
                pool.memset(floor_bias[:, :], -CLAMP).then_inc(consts_set, 1)
                pool.wait_ge(consts_set, 10)
                pool.memset(floor_w[SHIFT_ROW:SHIFT_ROW + 2, :], SHIFT_UNIT).then_inc(consts_set, 1)
                pool.wait_ge(consts_set, 11)
            pool.wait_ge(weights_loaded, 16 * WEIGHTS)

        def deviations(b):
            pool.wait_ge(ln_guess, 4 * b + 4)
            newton(pool, rstd[:, :], neg_half[:, :], one_half[:, :], square[:, :], ln_rstd, NEWTON_OPS * b)
            if cross:
                pool.wait_ge(xn_ready, 4 * b + 4)
                if keep is not None and isinstance(b, int) and b == 0:
                    pool.wait_ge(x_kept, 16 * B)
                for i in range(NT):
                    ins = pool.tensor_tensor(x[:, b, i, :], x[:, b, i, :], bo[:, :], ALU.add)
                ins.then_inc(bo_added, 1)

        def prologue():
            deviations(0)

        def emit(b, g, first, last):
            if g == 0 and not last:
                deviations(b + 1)

        steps(pool, emit, prologue, lambda: None)

    @block.tensor
    def _(pe):
        def transposes(b, section, g):
            pe.wait_ge(xn_ready, 4 * b + 4)
            for c in range(2):
                use = banks.at(section, *g, "tr", c)
                dst = fill(pe, use)
                for i in range(NT):
                    ins = pe.transpose(dst[:, i * P:(i + 1) * P], xn[:, i, c * P:(c + 1) * P], ident[:, :])
                ins.then_inc(full[use[0]], 1)
            if cross:
                pe.wait_ge(src_loaded, 16 * b + 16)
                for c, rows in KT:
                    use = banks.at(section, *g, "tr", 2 + c)
                    dst = fill(pe, use)
                    for i in range(NT):
                        ins = pe.transpose(dst[:, i * P:(i + 1) * P], ctx_in[:, i, c * P:(c + 1) * P], ident[:, :])
                    ins.then_inc(full[use[0]], 1)

        def project(b, what, tile, section, key):
            if what == "q" and tile == 0:
                for use in last_transposes(b, section)[-2:]:
                    freed(pe, use)
            use = banks.at(section, *key, what, tile)
            dst = fill(pe, use)
            w, tokens, tiles = (wk, kvT, KT) if what == "k" else (wq, xnT, [(0, P), (1, P)])
            for t, rows in tiles:
                ins = pe.matmul(dst[:, :], w[0:rows, t, tile * P:(tile + 1) * P], tokens[0:rows, t, :],
                                start=t == 0, stop=t == 1)
            ins.then_inc(full[use[0]], 1)

        def maxima(b, g, j, section, key, tiles=range(4), key_head=None):
            for i in tiles:
                if j == 0 and i == 0:
                    for r in restacked.values():
                        pe.wait_ge(r[g], PER_UNIT * b + PER_UNIT)
                use = banks.at(section, *key, "mx", j if key_head is None else key_head, i)
                dst = fill(pe, use)
                w = 512 if cross else (i + 1) * P
                ins = pe.matmul(dst[:, 0:w], qs[0:SHIFT_ROW, g, j, i * P:(i + 1) * P], ks[0:SHIFT_ROW, g, j, 0:w],
                                start=True, stop=cross)
                if not cross:
                    ins = pe.matmul(dst[:, i * P:w], ident_b[:, :], mask_qk[:, :], start=False, stop=True)
                ins.then_inc(full[use[0]], 1)

        def turn_maxima(b, g, section, key):
            use = banks.at(section, *key, "mt")
            last_maximum = banks.at(section, *key, "mx", 3, 3)
            dst = fill(pe, use)
            if use[0] != last_maximum[0]:
                freed(pe, last_maximum)
            if clip:
                pe.wait_ge(maxima_clipped, unit(b, g) + 1)
            pe.transpose(dst[0:16, 0:P], rowmax[:, g % 2, :], ident[:, :]).then_inc(full[use[0]], 1)

        def scores(b, g, j, half):
            if j == 0 and half == 0:
                pe.wait_ge(shift_placed[g % 2], SHIFT_DMA * turns(b, g) + SHIFT_DMA)
            wait(pe, exp_done, 8 * unit(b, g) + 2 * j + half - 1)
            for kb in (2 * half, 2 * half + 1):
                at = OFF[kb] - 1024 * half
                dst = score[half][:, at:at + WID[kb]]
                ins = pe.matmul(dst, ks[0:STACK, g, j, kb * P:(kb + 1) * P], qs[0:STACK, g, j, Q0[kb]:512],
                                start=True, stop=cross)
                if not cross:
                    ins = pe.matmul(score[half][:, at:at + P], ident_b[:, :], mask_kq[:, :], start=False, stop=True)
            ins.then_inc(scores_ready, 1)

        def weigh(b, g, kb, section=None):
            u = unit(b, g)
            if kb == 0:
                if clip:
                    pe.wait_ge(probs_clipped, 4 * u + 4)
                else:
                    pe.wait_ge(exp_done, 8 * u + 8)
                wait(pe, raw_ready, u)
                if g == 0:
                    for n in (V_USES - 2, V_USES - 1):
                        freed(pe, banks.at(section, 0, "v", n))
            cols = slice(Q0[kb], 512)
            for j in range(4):
                lhs = val[:, kb, 4 * g + j, :] if cross else val[:, kb, (4 * g + j) * CD:(4 * g + j + 1) * CD]
                ins = pe.matmul(out_ps[32 * j:32 * j + 32, cols], lhs, probs[:, g % 2, j, OFF[kb]:OFF[kb] + WID[kb]],
                                start=kb == 0, stop=kb == 3, tile_position=(0, 32 * j))
            if kb == 3 and cross:
                ins.then_inc(pv_done, 1)

        def add_up(b, g, kb):
            for j in range(4):
                ins = pe.matmul(sum_ps[32 * j:32 * j + 32, Q0[kb]:512], consts["ones"][:, 0:32],
                                probs[:, g % 2, j, OFF[kb]:OFF[kb] + WID[kb]],
                                start=kb == 0, stop=kb == 3, tile_position=(0, 32 * j))
            if kb == 3:
                ins.then_inc(pv_done, 1)

        def spread(b, g, use):
            pe.wait_ge(rinv_placed, 32 * unit(b, g) + 32)
            dst = fill(pe, use)
            pe.matmul(dst[:, :], consts["spread"][:, :], rinv_rows[:, :], start=True, stop=True).then_inc(full[use[0]], 1)

        def values(b, g, section):
            for n in range(V_USES):
                use = banks.at(section, g, "v", n)
                dst = fill(pe, use)
                tiles = (2 * n, 2 * n + 1) if cross else (n,)
                for m, i in enumerate(tiles):
                    for t, rows in KT:
                        ins = pe.matmul(dst[:, m * NV:(m + 1) * NV], kvT[0:rows, t, i * P:(i + 1) * P],
                                        wv[0:rows, t, :], start=t == 0, stop=t == 1)
                ins.then_inc(full[use[0]], 1)

        def project_out(b, n, section, key, last_spread):
            if n == 0:
                freed(pe, last_spread)
            use = banks.at(section, *key, "wo", n)
            dst = fill(pe, use)
            for m in range(2):
                i = 2 * n + m
                for g in range(4):
                    ins = pe.matmul(dst[:, m * C:(m + 1) * C], attT[:, g, i * P:(i + 1) * P], wo[:, g, :],
                                    start=g == 0, stop=g == 3)
            ins.then_inc(full[use[0]], 1)

        def prologue():
            pe.wait_ge(weights_loaded, 16 * WEIGHTS)
            pe.wait_ge(consts_set, 11 if clip else 9 if uniform else 8 if cross else 5)
            transposes(0, "pro", ())
            for t in range(TILES):
                project(0, "q", t, "pro", ())
                project(0, "k", t, "pro", ())
            for j in range(4):
                maxima(0, 0, j, "pro", ())
            turn_maxima(0, 0, "pro", ())
            for j in range(2):
                maxima(0, 1, j, "pro", (), key_head=4 + j)

        def emit(b, g, first, last):
            begun = not (first and g == 0)
            for j in range(4):
                def tile(i):
                    if maxima_of(j, g, last):
                        d, head = maxima_of(j, g, last)
                        maxima(*ahead(b, g, d), head, b, (g,), (i,))

                def extra(kind, n):
                    if kind == "wo":
                        project_out(b - 1, n, b, (g,), banks.at(b, 1, "sp"))
                    else:
                        project(b + 1, kind, n, b, (g,))

                extras = between(cross, first, last, g, j)
                tile(0)
                scores(b, g, j, 0)
                tile(1)
                if j == 2 and not (last and g == 3):
                    turn_maxima(*ahead(b, g, 1), b, (g,))
                scores(b, g, j, 1)
                if extras:
                    extra(*extras[0])
                tile(2)
                if begun:
                    weigh(*ahead(b, g, -1), j, b)
                tile(3)
                if extras:
                    extra(*extras[1])
                if j == 3 and not (first and g < 2):
                    spread(*ahead(b, g, -2), banks.at(b, g, "sp"))
                if clip:
                    use = banks.at(b, g, "fl", j)
                    dst = fill(pe, use)
                    pe.matmul(dst[:, :], floor_w[0:STACK, :], qs[0:STACK, g, j, :], start=True, stop=True)\
                      .then_inc(full[use[0]], 1)
                if begun and not cross:
                    add_up(*ahead(b, g, -1), j)
            if g == 0:
                values(b, g, b)
            if g == 0 and not last:
                transposes(b + 1, b, (g,))

        def epilogue():
            for kb in range(4):
                weigh(last_batch, 3, kb)
                if not cross:
                    add_up(last_batch, 3, kb)
            for g in (2, 3):
                spread(last_batch, g, banks.at("epi", "sp", g - 2))
            for n in range(2):
                project_out(last_batch, n, "epi", (), banks.at("epi", "sp", 1))

        steps(pe, emit, prologue, epilogue)

    @block.scalar
    def _(act):
        def high_part(b, what, tile, section, key):
            if what == "q" and tile == 0 and not (isinstance(b, int) and b == 0):
                for r in restacked.values():
                    act.wait_ge(r[3], PER_UNIT * b)
            dst = qh if what == "q" else kh
            ps_ = filled(act, banks.at(section, *key, what, tile))
            if uniform:
                act.activation(dst[:, tile, :], zeros[:, :], ACT.Copy).then_inc(hi_ready, 1)
            elif cross:
                bias = (bq if what == "q" else bk)[:, tile:tile + 1]
                act.activation(dst[:, tile, :], ps_[:, :], ACT.Identity, bias=bias).then_inc(hi_ready, 1)
            else:
                act.activation(dst[:, tile, :], ps_[:, :], ACT.Copy).then_inc(hi_ready, 1)

        def exps(b, g, j, half):
            u = unit(b, g)
            if j == 0 and half == 0:
                wait(act, pv_done, u - 1)
            act.wait_ge(scores_bounded if clip else scores_ready, 8 * u + 2 * j + half + 1)
            act.activation(probs[:, g % 2, j, 1024 * half:1024 * half + EXP[half]], score[half][:, 0:EXP[half]],
                           ACT.Exp, scale=SCALE).then_inc(exp_done, 1)

        def shift_high(b, g, section, key):
            use = banks.at(section, *key, "mt")
            ps_ = filled(act, use)
            wait(act, shift_placed[g % 2], SHIFT_DMA * turns(b, g))
            act.activation(shift_h[:, g % 2, :], ps_[0:16, 0:P], ACT.Copy, scale=-1.0 / SHIFT_UNIT).then_inc(shift_hi, 1)

        def copy_raw(b, g, spread_before=None):
            act.wait_ge(pv_done, unit(b, g) + 1)
            if spread_before:
                freed(act, spread_before)
            if not cross:
                act.activation(sums[:, :], sum_ps[:, :], ACT.Copy)
            act.activation(raw[:, :], out_ps[:, :], ACT.Copy).then_inc(raw_ready, 1)

        def keep_values(b, g, section):
            wait(act, pv_done, 4 * b)
            for n in range(V_USES):
                use = banks.at(section, g, "v", n)
                ps_ = filled(act, use)
                act.activation(val[:, n, :], ps_[:, :], ACT.Copy).then_inc(free[use[0]], 1)

        def keep_transposed(b, section, g):
            for c in range(4 if cross else 2):
                use = banks.at(section, *g, "tr", c)
                ps_ = filled(act, use)
                dst, rows = (xnT, P) if c < 2 else (ctxT, KT[c - 2][1])
                act.activation(dst[0:rows, c % 2, :], ps_[0:rows, :], ACT.Copy).then_inc(free[use[0]], 1)

        def prologue():
            if cross:
                act.wait_ge(weights_loaded, 16 * WEIGHTS)
            keep_transposed(0, "pro", ())
            for t in range(TILES):
                high_part(0, "q", t, "pro", ())
                high_part(0, "k", t, "pro", ())
            shift_high(0, 0, "pro", ())

        def emit(b, g, first, last):
            if not (first and g < 2):
                before = ahead(b, g, -1)
                copy_raw(*ahead(b, g, -2), None if first and g == 2 else banks.at(*before, "sp"))
            for j in range(4):
                exps(b, g, j, 0)
                if j == 2 and not (last and g == 3):
                    shift_high(*ahead(b, g, 1), b, (g,))
                exps(b, g, j, 1)
                for kind, n in between(cross, first, last, g, j):
                    if kind != "wo":
                        high_part(b + 1, kind, n, b, (g,))
                if clip:
                    use = banks.at(b, g, "fl", j)
                    ps_ = filled(act, use)
                    wait(act, probs_clipped, 4 * unit(b, g) + j)
                    act.activation(floors[:, :], ps_[:, :], ACT.Exp, scale=SCALE, bias=floor_bias[:, 0:1])\
                       .then_inc(free[use[0]], 1)
            if g == 0 and not cross:
                keep_values(b, g, b)
            if g == 0 and not last:
                keep_transposed(b + 1, b, (g,))

        def epilogue():
            copy_raw(last_batch, 2, banks.at(last_batch, 3, "sp"))
            copy_raw(last_batch, 3, banks.at("epi", "sp", 0))

        steps(act, emit, prologue, epilogue)

    @block.vector
    def _(dve):
        def statistics(b):
            if not cross:
                if isinstance(b, int) and b == 0:
                    dve.wait_ge(first_loaded, 16)
                else:
                    dve.wait_ge(src_loaded, 16 * b)
            for i in range(NT):
                dve.bn_stats(stats[:, i, :], x[:, b, i, :]).then_inc(ln_stats, 1)
            dve.wait_ge(ln_stats, 4 * b + 4)
            dve.memset(wait_cell[:, :], 0.0)
            for i in range(NT):
                dve.bn_aggr(meanvar[:, i, :], stats[:, i, :]).then_inc(ln_aggr, 1)
            dve.wait_ge(ln_aggr, 4 * b + 4)
            guess(dve, rstd[:, :], veps[:, :], neg_half[:, :], meanvar[:, :, 1], ln_guess, 4 * b)

        def layer_norm(b):
            dve.wait_ge(ln_rstd, NEWTON_OPS * b + NEWTON_OPS)
            if not (isinstance(b, int) and b == 0):
                transposed(dve, b - 1)
            for i in range(NT):
                dve.tensor_scalar(xn[:, i, :], x[:, b, i, :], meanvar[:, i, 0:1], rstd[:, i:i + 1],
                                  ALU.subtract, ALU.mult).then_inc(xn_ready, 1)

        def low_part(b, what, tile, section, key):
            m, hi, lo = (0, qh, ql) if what == "q" else (1, kh, kl)
            use = banks.at(section, *key, what, tile)
            dve.wait_ge(hi_ready, 2 * (TILES * b + tile) + m + 1)
            if uniform:
                ins = dve.memset(lo[:, tile, :], 0.0)
            elif cross:
                bias = (bq if what == "q" else bk)[:, tile:tile + 1]
                ins = dve.scalar_tensor_tensor(out=lo[:, tile, :], in0=work[use[0]][:, :], scalar=bias,
                                               in1=hi[:, tile, :], op0=ALU.add, op1=ALU.subtract)
            else:
                ins = dve.tensor_tensor(lo[:, tile, :], work[use[0]][:, :], hi[:, tile, :], ALU.subtract)
            ins.then_inc(free[use[0]], 1)

        def maxima(b, g, j, section, key, tiles=range(4), key_head=None):
            for i in tiles:
                use = banks.at(section, *key, "mx", j if key_head is None else key_head, i)
                ps_ = filled(dve, use)
                w = 512 if cross else (i + 1) * P
                ins = dve.tensor_reduce(rowmax[:, g % 2, 4 * j + i:4 * j + i + 1], ps_[:, 0:w], AX.X, ALU.max)
                ins.then_inc(free[use[0]], 1)
            if clip and j == 3 and i == 3:
                freed(dve, use)
                dve.tensor_scalar(rowmax[:, g % 2, :], rowmax[:, g % 2, :], CLAMP / SCALE, -CLAMP / SCALE,
                                  ALU.min, ALU.max).then_inc(maxima_clipped, 1)
            if cross and mode == "plain" and j == 3 and i == 3:
                wait(dve, noted, 2 * unit(b, g))
                freed(dve, use)
                for place, op in (("highest", ALU.max), ("lowest", ALU.min)):
                    dve.tensor_tensor(guard[place][:, :], guard[place][:, :], rowmax[:, g % 2, :], op).then_inc(noted, 1)

        def bound_scores(b, g, j, half):
            h = 8 * unit(b, g) + 2 * j + half
            dve.wait_ge(scores_ready, h + 1)
            for n in range(2):
                s = score[half][:, 512 * n:512 * n + 512]
                m = 4 * (2 * h + n)
                dve.tensor_copy(odd[:, :], s).then_inc(odd_steps, 1)
                dve.wait_ge(odd_steps, m + 1)
                dve.tensor_tensor(odd[:, :], odd[:, :], odd[:, :], ALU.not_equal).then_inc(odd_steps, 1)
                dve.wait_ge(odd_steps, m + 2)
                dve.tensor_reduce(odd_max[:, :], odd[:, :], AX.X, ALU.max).then_inc(odd_steps, 1)
                dve.wait_ge(odd_steps, m + 3)
                dve.tensor_tensor(guard["nan"][:, 0:1], guard["nan"][:, 0:1], odd_max[:, :], ALU.max).then_inc(odd_steps, 1)
                dve.wait_ge(odd_steps, m + 4)
                ins = dve.tensor_scalar(s, s, 0.0, None, ALU.min)
            ins.then_inc(scores_bounded, 1)

        def lift_probs(b, g, j):
            dve.wait_ge(exp_done, 8 * unit(b, g) + 2 * j + 2)
            freed(dve, banks.at(b, g, "fl", j))
            for kb in range(4):
                p = probs[:, g % 2, j, 512 * kb:512 * kb + 512]
                ins = dve.tensor_tensor(p, p, floors[:, :], ALU.max)
            ins.then_inc(probs_clipped, 1)

        def shift_low(b, g, section, key):
            use = banks.at(section, *key, "mt")
            dve.wait_ge(shift_hi, unit(b, g) + 1)
            dve.scalar_tensor_tensor(out=shift_l[:, g % 2, :], in0=work[use[0]][0:16, 0:P], scalar=-1.0 / SHIFT_UNIT,
                                     in1=shift_h[:, g % 2, :], op0=ALU.mult, op1=ALU.subtract).then_inc(free[use[0]], 1)

        def reciprocals(b, g):
            u = unit(b, g)
            dve.wait_ge(sums_moved, 16 * u + 16)
            if mode == "plain" and cross:
                dve.tensor_tensor(is_nan[:, :], sums_c[:, :], sums_c[:, :], ALU.not_equal).then_inc(nan_noted, 1)
                dve.wait_ge(nan_noted, 2 * u + 1)
                dve.tensor_tensor(guard["nan"][:, :], guard["nan"][:, :], is_nan[:, :], ALU.max).then_inc(nan_noted, 1)
            dve.reciprocal(rinv_c[:, :], sums_c[:, :]).then_inc(rinv_steps, 1)
            dve.wait_ge(rinv_steps, 3 * u + 1)
            dve.tensor_scalar(rinv_cs[:, 0, :], rinv_c[:, :], RINV_SCALE, None, ALU.mult).then_inc(rinv_steps, 1)
            dve.wait_ge(rinv_steps, 3 * u + 2)
            dve.scalar_tensor_tensor(out=rinv_cs[:, 1, :], in0=rinv_c[:, :], scalar=RINV_SCALE, in1=rinv_cs[:, 0, :],
                                     op0=ALU.mult, op1=ALU.subtract).then_inc(rinv_steps, 1)

        def normalise(b, g, use):
            ps_ = filled(dve, use)
            dve.tensor_tensor(attT[:, g, :], raw[:, :], ps_[:, :], ALU.mult).then_inc(free[use[0]], 1)

        def keep_values(b, g, section):
            wait(dve, pv_done, 4 * b)
            for n in range(V_USES):
                use = banks.at(section, g, "v", n)
                ps_ = filled(dve, use)
                for m in range(2):
                    ins = dve.tensor_tensor(val[:, 2 * n + m, :, 0:CD],
                                            ps_[:, m * NV:(m + 1) * NV].rearrange("p (h d) -> p h d", h=16),
                                            bv[:, :].rearrange("p (h d) -> p h d", h=16), ALU.add)
                ins.then_inc(free[use[0]], 1)

        def residual(b, n, section, key):
            if cross and n == 0:
                dve.wait_ge(bo_added, b + 1)
            use = banks.at(section, *key, "wo", n)
            ps_ = filled(dve, use)
            xs = x[:, b, 2 * n:2 * n + 2, :].rearrange("p t c -> p (t c)")
            dve.tensor_tensor(xs, xs, ps_[:, :], ALU.add).then_inc(free[use[0]], 1)

        def prologue():
            if cross:
                dve.wait_ge(weights_loaded, 16 * WEIGHTS)
            statistics(0)
            layer_norm(0)
            for t in range(TILES):
                low_part(0, "q", t, "pro", ())
                low_part(0, "k", t, "pro", ())
            for j in range(4):
                maxima(0, 0, j, "pro", ())
            shift_low(0, 0, "pro", ())
            for j in range(2):
                maxima(0, 1, j, "pro", (), key_head=4 + j)

        def emit(b, g, first, last):
            if g == 0 and not last:
                statistics(b + 1)
            for j in range(4):
                def some(tiles):
                    if maxima_of(j, g, last):
                        d, head = maxima_of(j, g, last)
                        maxima(*ahead(b, g, d), head, b, (g,), tiles)

                def extra(kind, n):
                    if kind == "wo":
                        residual(b - 1, n, b, (g,))
                    else:
                        low_part(b + 1, kind, n, b, (g,))

                extras = between(cross, first, last, g, j)
                some((0, 1))
                if clip:
                    bound_scores(b, g, j, 0)
                if j == 2 and not (last and g == 3):
                    shift_low(*ahead(b, g, 1), b, (g,))
                if clip:
                    bound_scores(b, g, j, 1)
                if extras:
                    extra(*extras[0])
                some((2, 3))
                if extras:
                    extra(*extras[1])
                if j == 3 and not (first and g < 2):
                    normalise(*ahead(b, g, -2), banks.at(b, g, "sp"))
                if clip:
                    lift_probs(b, g, j)
                if j == 1 and g == 0 and not last:
                    layer_norm(b + 1)
                if j == 1 and not (first and g < 2):
                    reciprocals(*ahead(b, g, -2))
            if g == 0 and cross:
                keep_values(b, g, b)

        def epilogue():
            for g in (2, 3):
                reciprocals(last_batch, g)
                normalise(last_batch, g, banks.at("epi", "sp", g - 2))
            for n in range(2):
                residual(last_batch, n, "epi", ())

        steps(dve, emit, prologue, epilogue)


def expert_choice(nc, stack, x, a, out):
    B, NT, C = x.shape[1], x.shape[2], x.shape[3]
    T = B * NT
    E = a["L0_ffn_W_down"].shape[0]
    F = a["L0_ffn_W_down"].shape[1]
    GROUPS = a["L0_ffn_W_up"].shape[0]
    PER_GROUP = E // GROUPS
    CAP = T * P // E
    Q = CAP // P
    FT = -(-F // P)
    FR = F - (FT - 1) * P
    BIAS_ROW = 64
    ROW = C + E
    HI, LO = CAP // 32, 32
    BITS = 30
    outer = stack
    rows = nc.dram_tensor("token_rows", [T * P, ROW], F32).ap()

    def sb(n, shape, dt=F32, s=None):
        return (s or outer).enter_context(nc.sbuf_tensor("ffn_" + n, shape, dt))

    def sem(n):
        return outer.enter_context(nc.semaphore("ffn_" + n))

    w_up = sb("w_up", [P, GROUPS, 2, F])
    w_down = sb("w_down", [P, E, FT, C])
    b_up = sb("b_up", [P, GROUPS, FT])
    idx = sb("idx", [P, E * Q], U32)
    ident = sb("ident", [P, P])
    mid = sb("mid", [P, FT, CAP])
    down_cleared, up_loaded, down_loaded = sem("down_cleared"), sem("up_loaded"), sem("down_loaded")
    DOWN_DMAS = 3 * E
    UP_DMAS = 2 + GROUPS
    x_stored, rows_stored, gates_stored = sem("x_stored"), sem("rows_stored"), sem("gates_stored")

    with ExitStack() as s:
        def sb2(n, shape, dt=F32):
            return sb(n, shape, dt, s)

        xn = sb2("xn", [P, B, NT, C])
        stats, meanvar = sb2("stats", [P, T, 6]), sb2("meanvar", [P, T, 2])
        rstd, veps, square = sb2("rstd", [P, T]), sb2("veps", [P, T]), sb2("square", [P, T])
        neg_half, one_half = sb2("neg_half", [P, T]), sb2("one_half", [P, T])
        xT = sb2("xT", [P, 2, 512])
        wr, br = sb2("wr", [P, 2, E]), sb2("br", [P, E])
        logits = sb2("logits", [P, T, E])
        red, gates, gates_e = sb2("red", [P, T]), sb2("gates", [P, T, E]), sb2("gates_e", [P, E, T])
        ones_b, before = sb2("ones_b", [P, P], BF16), sb2("before", [P, P], BF16)
        diag = sb2("diag", [P, E, LO])
        carry = sb2("carry", [P, E, T])
        iota_i = sb2("iota_i", [P, T + HI + LO], I32)
        iota = sb2("iota", [P, T + HI + LO])
        tok, count_hi, count_lo = iota[:, 0:T], iota[:, T:T + HI], iota[:, T + HI:]
        thr, trial, bit = sb2("thr", [P, E]), sb2("trial", [P, E]), sb2("bit", [P, E])
        count, need = sb2("count", [P, E]), sb2("need", [P, E])
        over = sb2("over", [P, E, T], BF16)
        gt, eq, sel = sb2("gt", [P, E, T], BF16), sb2("eq", [P, E, T], BF16), sb2("sel", [P, E, T], BF16)
        tile_sum, rank, place_i = sb2("tile_sum", [P, E, T]), sb2("rank", [P, E, T]), sb2("place_i", [P, E, T], I32)
        hi_i, lo_i = sb2("hi_i", [P, E, T], I32), sb2("lo_i", [P, E, T], I32)
        hi, lo = sb2("hi", [P, E, T]), sb2("lo", [P, E, T])
        pick_hi = sb2("pick_hi", [P, T, E, HI])
        pick_lo = xn[:, :, :, :].rearrange("p b i c -> p (b i c)").rearrange("p (t e l) -> p t e l", t=T, e=E)
        own, folded = sb2("own", [P, E, LO]), sb2("folded", [P, LO])
        turn_ps = [s.enter_context(nc.psum_tensor(f"ffn_turn{i}", [P, 512], F32)) for i in range(2)]
        logit_ps = s.enter_context(nc.psum_tensor("ffn_logit_ps", [P, 512], F32))
        count_ps = s.enter_context(nc.psum_tensor("ffn_count_ps", [P, 512], F32))
        rank_ps = s.enter_context(nc.psum_tensor("ffn_rank_ps", [P, 512], F32))
        idx_ps = s.enter_context(nc.psum_tensor("ffn_idx_ps", [P, 512], F32))
        idxT_ps = s.enter_context(nc.psum_tensor("ffn_idxT_ps", [P, 512], F32))

        consts_made, const_steps, router_loaded = sem("consts_made"), sem("const_steps"), sem("router_loaded")
        ln_stats, ln_aggr, ln_guess, ln_rstd, xn_ready = (sem(n) for n in ("ln_stats", "ln_aggr", "ln_guess", "ln_rstd", "xn_ready"))
        turned, turned_kept, logits_done, logits_kept = (sem(n) for n in ("turned", "turned_kept", "logits_done", "logits_kept"))
        chain, shifted, exps_done, gates_ready = (sem(n) for n in ("chain", "shifted", "exps_done", "gates_ready"))
        over_ready, over_counted, search, mask_ready, mask_counted = (
            sem(n) for n in ("over_ready", "over_counted", "search", "mask_ready", "mask_counted"))
        picks_ready, picked, folded_ready, idx_turned, idx_ready = (
            sem(n) for n in ("picks_ready", "picked", "folded_ready", "idx_turned", "idx_ready"))

        with nc.Block() as block:
            @block.sync
            def _(sp):
                sp.dma_start(wr[:, :, :], a["L0_ffn_Wr"].rearrange("(t p) e -> p t e", p=P)).then_inc(router_loaded, 16)
                sp.dma_start(br[:, :], a["L0_ffn_br"].rearrange("(a e) -> a e", a=1).to_broadcast([P, E])).then_inc(router_loaded, 16)
                for b in range(B):
                    sp.dma_start(out[b].rearrange("(t p) c -> p t c", p=P), x[:, b, :, :]).then_inc(x_stored, 16)
                for b in range(B):
                    sp.wait_ge(xn_ready, 4 * b + 4)
                    sp.dma_start(rows[512 * b:512 * b + 512, 0:C].rearrange("(t p) c -> p t c", p=P), xn[:, b, :, :])\
                      .then_inc(rows_stored, 16)
                sp.dma_start(w_up[:, :, :, :].rearrange("p g t f -> p (g t) f"),
                             a["L0_ffn_W_up"].rearrange("g (t p) f -> p (g t) f", p=P)).then_inc(up_loaded, 16)
                for g in range(GROUPS):
                    sp.dma_start(b_up[:, g, 0:FT - 1], a["L0_ffn_b_up"][g, 0:(FT - 1) * P].rearrange("(t p) -> p t", p=P),
                                 allow_slow_non_contiguous=True).then_inc(up_loaded, 16)
                sp.dma_start(b_up[0:FR, :, FT - 1], a["L0_ffn_b_up"][:, (FT - 1) * P:F].rearrange("g p -> p g"),
                             allow_slow_non_contiguous=True).then_inc(up_loaded, 16)
                sp.wait_ge(down_cleared, 1)
                for e in range(E):
                    w = a["L0_ffn_W_down"][e]
                    sp.dma_start(w_down[:, e, 0:FT - 1, :], w[0:(FT - 1) * P, :].rearrange("(t p) n -> p t n", p=P))\
                      .then_inc(down_loaded, 16)
                    sp.dma_start(w_down[0:FR, e, FT - 1, :], w[(FT - 1) * P:F, :]).then_inc(down_loaded, 16)
                    sp.dma_start(w_down[BIAS_ROW:BIAS_ROW + 1, e, FT - 1, :], a["L0_ffn_b_down"][e:e + 1, :])\
                      .then_inc(down_loaded, 16)
                sp.wait_ge(gates_ready, 1)
                sp.dma_start(rows[:, C:ROW].rearrange("(t p) e -> p t e", p=P), gates[:, :, :],
                             allow_slow_non_contiguous=True).then_inc(gates_stored, 16)
                sp.wait_ge(x_stored, 16 * B)
                sp.wait_ge(rows_stored, 16 * B)
                sp.wait_ge(gates_stored, 16)

            @block.gpsimd
            def _(pool):
                n = [0]

                def step(ins):
                    ins.then_inc(const_steps, 1)
                    n[0] += 1
                    pool.wait_ge(const_steps, n[0])

                pool.memset(w_down[:, :, FT - 1, :], 0.0).then_inc(down_cleared, 1)
                pool.wait_ge(down_cleared, 1)
                step(pool.memset(ident[:, :], 0.0))
                step(pool.affine_select(out=ident[:, :], in_=ident[:, :], compare_op=ALU.not_equal, fill=1.0, base=0,
                                        pattern=[[-1, P]], channel_multiplier=1))
                step(pool.memset(ones_b[:, :], 1.0))
                step(pool.memset(before[:, :], 1.0))
                step(pool.affine_select(out=before[:, :], in_=before[:, :], compare_op=ALU.is_gt, fill=0.0, base=0,
                                        pattern=[[1, P]], channel_multiplier=-1))
                step(pool.memset(diag[:, :, :], 1.0))
                step(pool.affine_select(out=diag[:, :, :], in_=diag[:, :, :], compare_op=ALU.is_ge, fill=0.0, base=0,
                                        pattern=[[-HI, E], [0, LO]], channel_multiplier=1))
                step(pool.affine_select(out=diag[:, :, :], in_=diag[:, :, :], compare_op=ALU.is_ge, fill=0.0, base=HI - 1,
                                        pattern=[[HI, E], [0, LO]], channel_multiplier=-1))
                step(pool.memset(carry[:, :, :], 1.0))
                step(pool.memset(carry[:, :, 0:1], 0.0))
                step(pool.iota(iota_i[:, 0:T], [[P, T]], base=0, channel_multiplier=1))
                step(pool.iota(iota_i[:, T:T + HI], [[1, HI]], base=1, channel_multiplier=0))
                step(pool.iota(iota_i[:, T + HI:], [[1, LO]], base=0, channel_multiplier=0))
                step(pool.tensor_copy(iota[:, :], iota_i[:, :]))
                step(pool.memset(one_half[:, :], 1.5))
                step(pool.memset(thr[:, :], 0.0))
                step(pool.memset(bit[:, :], 2.0 ** -63))
                step(pool.memset(mid[:, FT - 1, :], 0.0))
                pool.memset(mid[BIAS_ROW:BIAS_ROW + 1, FT - 1, :], 1.0).then_inc(consts_made, 1)
                pool.wait_ge(consts_made, 1)
                pool.wait_ge(ln_guess, 4)
                newton(pool, rstd[:, :], neg_half[:, :], one_half[:, :], square[:, :], ln_rstd, 0)

            @block.vector
            def _(dve):
                n = [0]

                def step(ins):
                    ins.then_inc(chain, 1)
                    n[0] += 1
                    dve.wait_ge(chain, n[0])

                with dve.Fori(0, B) as b:
                    for i in range(NT):
                        dve.bn_stats(stats[:, 4 * b + i, :], x[:, b, i, :]).then_inc(ln_stats, 1)
                dve.wait_ge(ln_stats, T)
                for t in range(T):
                    dve.bn_aggr(meanvar[:, t, :], stats[:, t, :]).then_inc(ln_aggr, 1)
                dve.wait_ge(ln_aggr, T)
                guess(dve, rstd[:, :], veps[:, :], neg_half[:, :], meanvar[:, :, 1], ln_guess, 0)
                dve.wait_ge(ln_rstd, NEWTON_OPS)
                with dve.Fori(0, B) as b:
                    for i in range(NT):
                        dve.tensor_scalar(xn[:, b, i, :], x[:, b, i, :], meanvar[:, 4 * b + i, 0:1],
                                          rstd[:, bass.ds(4 * b + i, 1)], ALU.subtract, ALU.mult).then_inc(xn_ready, 1)
                dve.wait_ge(router_loaded, 32)
                with dve.Fori(0, B) as b:
                    dve.wait_ge(logits_done, b + 1)
                    dve.tensor_tensor(logits[:, bass.ds(4 * b, 4), :], logit_ps[:, 0:NT * E].rearrange("p (t e) -> p t e", e=E),
                                      br[:, :].unsqueeze(1).broadcast_to([P, NT, E]), ALU.add).then_inc(logits_kept, 1)
                dve.wait_ge(logits_kept, B)
                step(dve.tensor_reduce(red[:, :], logits[:, :, :], AX.X, ALU.max))
                dve.tensor_tensor(logits[:, :, :], logits[:, :, :], red[:, :].unsqueeze(2).broadcast_to([P, T, E]),
                                  ALU.subtract).then_inc(shifted, 1)
                dve.wait_ge(exps_done, 1)
                step(dve.tensor_reduce(red[:, :], logits[:, :, :], AX.X, ALU.add))
                step(dve.reciprocal(red[:, :], red[:, :]))
                dve.tensor_tensor(gates[:, :, :], logits[:, :, :], red[:, :].unsqueeze(2).broadcast_to([P, T, E]),
                                  ALU.mult).then_inc(gates_ready, 1)
                dve.wait_ge(gates_ready, 1)
                step(dve.tensor_copy(gates_e[:, :, :], gates[:, :, :].rearrange("p t e -> p e t")))
                dve.wait_ge(consts_made, 1)

                def wide(v):
                    return v[:, :].unsqueeze(2).broadcast_to([P, E, T])

                with dve.Fori(0, BITS) as k:
                    dve.tensor_tensor(trial[:, :].bitcast(U32), thr[:, :].bitcast(U32), bit[:, :].bitcast(U32),
                                      ALU.bitwise_or).then_inc(search, 1)
                    dve.wait_ge(search, 5 * k + 1)
                    dve.tensor_tensor(over[:, :, :], gates_e[:, :, :], wide(trial), ALU.is_ge).then_inc(over_ready, 1)
                    dve.tensor_scalar(bit[:, :].bitcast(U32), bit[:, :].bitcast(U32), 1, None,
                                      ALU.logical_shift_right).then_inc(search, 1)
                    dve.wait_ge(over_counted, k + 1)
                    dve.tensor_reduce(count[:, :], count_ps[:, 0:E * T].rearrange("p (e t) -> p e t", e=E), AX.X, ALU.add)\
                       .then_inc(search, 1)
                    dve.wait_ge(search, 5 * k + 3)
                    dve.scalar_tensor_tensor(out=trial[:, :], in0=count[:, :], scalar=float(CAP), in1=trial[:, :],
                                             op0=ALU.is_ge, op1=ALU.mult).then_inc(search, 1)
                    dve.wait_ge(search, 5 * k + 4)
                    dve.tensor_tensor(thr[:, :], thr[:, :], trial[:, :], ALU.max).then_inc(search, 1)
                    dve.wait_ge(search, 5 * k + 5)
                step(dve.tensor_tensor(gt[:, :, :], gates_e[:, :, :], wide(thr), ALU.is_gt))
                dve.tensor_tensor(eq[:, :, :], gates_e[:, :, :], wide(thr), ALU.is_equal).then_inc(mask_ready, 1)
                dve.wait_ge(mask_counted, 1)
                step(dve.tensor_reduce(count[:, :], count_ps[:, 0:E * T].rearrange("p (e t) -> p e t", e=E), AX.X, ALU.add))
                step(dve.tensor_scalar(need[:, :], count[:, :], -1.0, float(CAP), ALU.mult, ALU.add))

                def ranks(bank):
                    step(dve.tensor_copy(tile_sum[:, :, :].rearrange("p e t -> p (e t)"), bank[:, 256:512]))
                    step(dve.tensor_tensor_scan(rank[:, :, :].rearrange("p e t -> p (e t)"),
                                                carry[:, :, :].rearrange("p e t -> p (e t)"),
                                                tile_sum[:, :, :].rearrange("p e t -> p (e t)"), 0.0, ALU.mult, ALU.add))
                    step(dve.tensor_tensor(rank[:, :, :], rank[:, :, :], tile_sum[:, :, :], ALU.subtract))
                    step(dve.tensor_tensor(rank[:, :, :].rearrange("p e t -> p (e t)"),
                                           rank[:, :, :].rearrange("p e t -> p (e t)"), bank[:, 0:256], ALU.add))

                ranks(rank_ps)
                step(dve.tensor_tensor(rank[:, :, :], rank[:, :, :], wide(need), ALU.is_lt))
                step(dve.tensor_tensor(sel[:, :, :], rank[:, :, :], eq[:, :, :], ALU.mult))
                step(dve.tensor_tensor(sel[:, :, :], sel[:, :, :], gt[:, :, :], ALU.add))
                dve.tensor_scalar(over[:, :, :], sel[:, :, :], 1.0, None, ALU.mult).then_inc(mask_ready, 1)
                dve.wait_ge(mask_counted, 2)
                ranks(rank_ps)
                step(dve.tensor_copy(place_i[:, :, :], rank[:, :, :]))
                step(dve.tensor_scalar(hi_i[:, :, :], place_i[:, :, :], 5, None, ALU.logical_shift_right))
                step(dve.tensor_scalar(lo_i[:, :, :], place_i[:, :, :], LO - 1, None, ALU.bitwise_and))
                step(dve.tensor_copy(hi[:, :, :], hi_i[:, :, :]))
                step(dve.tensor_copy(lo[:, :, :], lo_i[:, :, :]))
                step(dve.scalar_tensor_tensor(out=hi[:, :, :], in0=hi[:, :, :], scalar=1.0, in1=sel[:, :, :],
                                              op0=ALU.add, op1=ALU.mult))
                dve.wait_ge(rows_stored, 16 * B)
                for t in range(0, T, 4):
                    for e_major, table, pick, width in ((hi, count_hi, pick_hi, HI), (lo, count_lo, pick_lo, LO)):
                        for tt in range(t, t + 4):
                            ins = dve.tensor_tensor(pick[:, tt, :, :], e_major[:, :, tt:tt + 1].broadcast_to([P, E, width]),
                                                    table.unsqueeze(1).broadcast_to([P, E, width]), ALU.is_equal)
                    step(ins)
                    for tt in range(t, t + 4):
                        ins = dve.tensor_scalar(pick_lo[:, tt, :, :], pick_lo[:, tt, :, :], tok[:, tt:tt + 1], None, ALU.mult)
                    ins.then_inc(picks_ready, 1)
                dve.wait_ge(picked, 1)
                step(dve.tensor_tensor(own[:, :, :], idx_ps[:, 0:E * LO].rearrange("p (e l) -> p e l", e=E),
                                       diag[:, :, :], ALU.mult))
                dve.tensor_reduce(folded[:, :], own[:, :, :].rearrange("p e l -> p l e"), AX.X, ALU.add).then_inc(folded_ready, 1)
                dve.wait_ge(idx_turned, 1)
                for r in range(4):
                    dve.tensor_copy(idx[32 * r:32 * r + 32, :], idxT_ps[0:32, 0:P].rearrange("l (c r) -> l c r", r=4)[:, :, r])\
                       .then_inc(idx_ready, 1)

            @block.scalar
            def _(act):
                with act.Fori(0, B) as b:
                    for c in range(2):
                        act.wait_ge(turned, 2 * b + c + 1)
                        act.activation(xT[:, c, :], turn_ps[c][:, :], ACT.Copy).then_inc(turned_kept, 1)
                act.wait_ge(shifted, 1)
                act.activation(logits[:, :, :], logits[:, :, :], ACT.Exp).then_inc(exps_done, 1)

            @block.tensor
            def _(pe):
                pe.wait_ge(consts_made, 1)
                pe.wait_ge(router_loaded, 32)

                def batch(b, first):
                    pe.wait_ge(xn_ready, 4 * b + 4)
                    for c in range(2):
                        for i in range(NT):
                            ins = pe.transpose(turn_ps[c][:, i * P:(i + 1) * P],
                                               xn_static(b, i, c), ident[:, :])
                        ins.then_inc(turned, 1)
                    pe.wait_ge(turned_kept, 2 * b + 2)
                    if not first:
                        pe.wait_ge(logits_kept, b)
                    for i in range(NT):
                        for c in range(2):
                            ins = pe.matmul(logit_ps[:, i * E:(i + 1) * E], xT[:, c, i * P:(i + 1) * P], wr[:, c, :],
                                            start=c == 0, stop=c == 1)
                    ins.then_inc(logits_done, 1)

                def xn_static(b, i, c):
                    return xn[:, b, i, c * P:(c + 1) * P]

                for b in range(B):
                    batch(b, b == 0)
                with pe.Fori(0, BITS) as k:
                    pe.wait_ge(over_ready, k + 1)
                    pe.matmul(count_ps[:, 0:E * T], ones_b[:, :], over[:, :, :].rearrange("p e t -> p (e t)"),
                              start=True, stop=True).then_inc(over_counted, 1)
                flat = [m[:, :, :].rearrange("p e t -> p (e t)") for m in (gt, eq, over)]
                pe.wait_ge(mask_ready, 1)
                pe.matmul(count_ps[:, 0:E * T], ones_b[:, :], flat[0], start=True, stop=True)
                pe.matmul(rank_ps[:, 0:256], before[:, :], flat[1], start=True, stop=True)
                pe.matmul(rank_ps[:, 256:512], ones_b[:, :], flat[1], start=True, stop=True).then_inc(mask_counted, 1)
                pe.wait_ge(mask_ready, 2)
                pe.matmul(rank_ps[:, 0:256], before[:, :], flat[2], start=True, stop=True)
                pe.matmul(rank_ps[:, 256:512], ones_b[:, :], flat[2], start=True, stop=True).then_inc(mask_counted, 1)
                for t in range(T):
                    if t % 4 == 0:
                        pe.wait_ge(picks_ready, t // 4 + 1)
                    ins = pe.matmul(idx_ps[:, 0:E * LO], pick_hi[:, t, :, :].rearrange("p e h -> p (e h)"),
                                    pick_lo[:, t, :, :].rearrange("p e l -> p (e l)"), start=t == 0, stop=t == T - 1)
                ins.then_inc(picked, 1)
                pe.wait_ge(folded_ready, 1)
                pe.transpose(idxT_ps[0:LO, 0:P], folded[:, :], ident[:, :]).then_inc(idx_turned, 1)

    taken = [sb(f"taken{i}", [P, Q, ROW]) for i in range(2)]
    takenT = sb("takenT", [P, 2, CAP])
    made = [sb(f"made{i}", [P, Q, C]) for i in range(2)]
    turn_ps = [outer.enter_context(nc.psum_tensor(f"exp_turn{i}", [P, 512], F32)) for i in range(2)]
    up_ps = [outer.enter_context(nc.psum_tensor(f"exp_up{i}", [P, 512], F32)) for i in range(2)]
    down_ps = [outer.enter_context(nc.psum_tensor(f"exp_down{i}", [P, 512], F32)) for i in range(2)]
    gathered = [sem(f"gathered{i}") for i in range(2)]
    added, turned2, turned2_kept, up_done, silu_done, down_done, made_ready = (
        sem("e_" + n) for n in ("added", "turned", "turned_kept", "up_done", "silu_done", "down_done", "made_ready"))
    out_rows = out.rearrange("b n c -> (b n) c")

    with nc.Block() as block:
        @block.gpsimd
        def _(pool):
            def gather(e):
                if e >= 2:
                    pool.wait_ge(made_ready, Q * (e - 1))
                for q in range(Q):
                    pool.indirect_dma_start(
                        out=taken[e % 2][:, q, :], out_offset=None, in_=rows[:, :],
                        in_offset=bass.IndirectOffsetOnAxis(ap=idx[:, e * Q + q:e * Q + q + 1], axis=0),
                        ).then_inc(gathered[e % 2], 16)

            gather(0)
            for e in range(E):
                if e + 1 < E:
                    gather(e + 1)
                if e >= 1:
                    pool.wait_ge(added, 16 * Q * e)
                for q in range(Q):
                    pool.wait_ge(made_ready, Q * e + q + 1)
                    pool.indirect_dma_start(
                        out=out_rows, out_offset=bass.IndirectOffsetOnAxis(ap=idx[:, e * Q + q:e * Q + q + 1], axis=0),
                        in_=made[e % 2][:, q, :], in_offset=None, compute_op=ALU.add).then_inc(added, 16)
            pool.wait_ge(added, 16 * Q * E)

        @block.tensor
        def _(pe):
            def turn(e):
                pe.wait_ge(gathered[e % 2], 16 * Q * (e // 2 + 1))
                for c in range(2):
                    for q in range(Q):
                        ins = pe.transpose(turn_ps[c][:, q * P:(q + 1) * P], taken[e % 2][:, q, c * P:(c + 1) * P], ident[:, :])
                    ins.then_inc(turned2, 1)

            def up(e):
                pe.wait_ge(turned2_kept, 2 * e + 2)
                for f in range(FT):
                    n = FT * e + f
                    if n >= 2:
                        pe.wait_ge(silu_done, n - 1)
                    w = P if f < FT - 1 else FR
                    for c in range(2):
                        ins = pe.matmul(up_ps[n % 2][0:w, :], w_up[:, e // PER_GROUP, c, f * P:f * P + w], takenT[:, c, :],
                                        start=c == 0, stop=c == 1)
                    ins.then_inc(up_done, 1)

            def down(e):
                pe.wait_ge(silu_done, FT * e + FT)
                for q in range(Q):
                    n = Q * e + q
                    if n >= 2:
                        pe.wait_ge(made_ready, n - 1)
                    for f in range(FT):
                        w = P if f < FT - 1 else BIAS_ROW + 1
                        ins = pe.matmul(down_ps[n % 2][:, 0:C], mid[0:w, f, q * P:(q + 1) * P], w_down[0:w, e, f, :],
                                        start=f == 0, stop=f == FT - 1)
                    ins.then_inc(down_done, 1)

            pe.wait_ge(up_loaded, 16 * UP_DMAS)
            pe.wait_ge(down_loaded, 16 * DOWN_DMAS)
            turn(0)
            for e in range(E):
                up(e)
                if e + 1 < E:
                    turn(e + 1)
                down(e)

        @block.scalar
        def _(act):
            act.wait_ge(up_loaded, 16 * UP_DMAS)
            for e in range(E):
                for f in range(FT):
                    n = FT * e + f
                    w = P if f < FT - 1 else FR
                    act.wait_ge(up_done, n + 1)
                    act.activation(mid[0:w, f, :], up_ps[n % 2][0:w, :], ACT.Silu,
                                   bias=b_up[0:w, e // PER_GROUP, f:f + 1]).then_inc(silu_done, 1)

        @block.vector
        def _(dve):
            def keep_turned(e):
                for c in range(2):
                    dve.wait_ge(turned2, 2 * e + c + 1)
                    dve.wait_ge(up_done, FT * e) if e else None
                    dve.tensor_copy(takenT[:, c, :], turn_ps[c][:, :]).then_inc(turned2_kept, 1)

            keep_turned(0)
            for e in range(E):
                if e + 1 < E:
                    keep_turned(e + 1)
                if e >= 2:
                    dve.wait_ge(added, 16 * Q * (e - 1))
                for q in range(Q):
                    n = Q * e + q
                    dve.wait_ge(down_done, n + 1)
                    dve.tensor_scalar(made[e % 2][:, q, :], down_ps[n % 2][:, 0:C], taken[e % 2][:, q, C + e:C + e + 1],
                                      None, ALU.mult).then_inc(made_ready, 1)


def make_consts(nc, stack):
    def sb(n, shape, dt=F32):
        return stack.enter_context(nc.sbuf_tensor(n, shape, dt))

    c = {"ident": sb("ident", [P, P]), "ones": sb("ones", [P, P]), "spread": sb("spread", [P, P], F16),
         "ident_b": sb("ident_b", [P, P], BF16), "mask_qk": sb("mask_qk", [P, P], BF16),
         "mask_kq": sb("mask_kq", [P, P], BF16)}
    cleared, made = stack.enter_context(nc.semaphore("cleared")), stack.enter_context(nc.semaphore("made"))
    with nc.Block() as block:
        @block.gpsimd
        def _(pool):
            for n, v in (("ident", 0.0), ("spread", 0.0), ("ident_b", 0.0), ("mask_qk", 0.0), ("mask_kq", 0.0),
                         ("ones", 1.0)):
                pool.memset(c[n][:, :], v).then_inc(cleared, 1)
            pool.wait_ge(cleared, 6)
            for n in ("ident", "ident_b"):
                pool.affine_select(out=c[n][:, :], in_=c[n][:, :], compare_op=ALU.not_equal, fill=1.0, base=0,
                                   pattern=[[-1, P]], channel_multiplier=1).then_inc(made, 1)
            s = c["spread"][:, :].rearrange("p (j m) -> p j m", j=4)
            for n, base in enumerate((0, -4)):
                pool.affine_select(out=s, in_=s, compare_op=ALU.not_equal, fill=1.0 / RINV_SCALE, base=base,
                                   pattern=[[-1, 4], [0, 32]], channel_multiplier=1).then_inc(made, 1)
                pool.wait_ge(made, 3 + n)
            pool.affine_select(out=c["mask_qk"][:, :], in_=c["mask_qk"][:, :], compare_op=ALU.is_ge, fill=MASKED,
                               base=0, pattern=[[-1, P]], channel_multiplier=1).then_inc(made, 1)
            pool.affine_select(out=c["mask_kq"][:, :], in_=c["mask_kq"][:, :], compare_op=ALU.is_ge, fill=MASKED,
                               base=0, pattern=[[1, P]], channel_multiplier=-1).then_inc(made, 1)
            pool.wait_ge(made, 6)
    return c


def clear_guard(nc, stack, guard, flag_i):
    cleared = stack.enter_context(nc.semaphore("guard_cleared"))
    with nc.Block() as block:
        @block.gpsimd
        def _(pool):
            for n in ("highest", "lowest", "nan"):
                pool.memset(guard[n][:, :], 0.0).then_inc(cleared, 1)
            pool.memset(flag_i[:, :], 0).then_inc(cleared, 1)
            pool.wait_ge(cleared, 4)


def raise_flag(nc, guard, flag_i, consts, which):
    with ExitStack() as s:
        steps, summed = (s.enter_context(nc.semaphore(f"flag{which}_{n}")) for n in ("steps", "summed"))
        cell = s.enter_context(nc.sbuf_tensor(f"flag{which}_cell", [P, 3, 16], F32))
        total = s.enter_context(nc.sbuf_tensor(f"flag{which}_total", [P, 1], F32))
        flag_ps = s.enter_context(nc.psum_tensor(f"flag{which}_ps", [P, 512], F32))
        with nc.Block() as block:
            @block.vector
            def _(dve):
                dve.tensor_scalar(cell[:, 0, :], guard["highest"][:, :], 4.0 * CLAMP, None, ALU.is_gt).then_inc(steps, 1)
                dve.tensor_scalar(cell[:, 1, :], guard["lowest"][:, :], -4.0 * (CLAMP - 110.0), None, ALU.is_lt).then_inc(steps, 1)
                dve.tensor_copy(cell[:, 2, :], guard["nan"][:, :]).then_inc(steps, 1)
                dve.wait_ge(steps, 3)
                dve.tensor_reduce(total[:, :], cell[:, 2 * which:, :].rearrange("p a b -> p (a b)"), AX.X, ALU.max).then_inc(steps, 1)
                dve.memset(guard["nan"][:, :], 0.0).then_inc(steps, 1)
                dve.wait_ge(summed, 1)
                dve.tensor_copy(flag_i[:, which:which + 1], flag_ps[:, 0:1]).then_inc(steps, 1)
                dve.wait_ge(steps, 6)

            @block.tensor
            def _(pe):
                pe.wait_ge(steps, 4)
                pe.matmul(flag_ps[:, 0:1], consts["ones"][:, :], total[:, :], start=True, stop=True).then_inc(summed, 1)


def restore(nc, name, x, kept):
    with ExitStack() as s:
        loaded = s.enter_context(nc.semaphore(f"{name}_x_loaded"))
        with nc.Block() as block:
            @block.sync
            def _(sp):
                for b in range(x.shape[1]):
                    sp.dma_start(x[:, b, :, :], kept[b].rearrange("(t p) c -> p t c", p=P)).then_inc(loaded, 16)
                sp.wait_ge(loaded, 16 * x.shape[1])


def decoder_block(nc, a, out, until=3):
    B, N, C = a["x"].shape
    with ExitStack() as whole:
        x = whole.enter_context(nc.sbuf_tensor("x_sb", [P, B, N // P, C], F32))
        flag_i = whole.enter_context(nc.sbuf_tensor("flag_i", [P, 2], I32))
        with ExitStack() as s:
            consts = make_consts(nc, s)
            with ExitStack() as phase:
                attention(nc, phase, "self", False, x, a["x"], {n: a["L0_attn_" + n] for n in ("Wq", "Wk", "Wv", "Wo")}, consts)
            if until >= 2:
                ctx = a["ctx_768"]
                w = {n: a["L0_xattn_" + n] for n in ("Wq", "Wk", "Wv", "Wo", "bq", "bk", "bv", "bo")}
                kept = nc.dram_tensor("x_kept", [B, N, C], F32).ap()
                guard = {n: s.enter_context(nc.sbuf_tensor("guard_" + n, [P, 16], F32)) for n in ("highest", "lowest", "nan")}
                clear_guard(nc, s, guard, flag_i)
                with ExitStack() as phase:
                    attention(nc, phase, "cross", True, x, ctx, w, consts, guard, "plain", kept)
                raise_flag(nc, guard, flag_i, consts, 0)
                flag = nc.values_load(flag_i[0:1, 0:1], min_val=0, max_val=P)
                with nc.If(flag > 0):
                    nc.all_engine_barrier()
                    restore(nc, "clip", x, kept)
                    with ExitStack() as phase:
                        attention(nc, phase, "clip", True, x, ctx, w, consts, guard, "clip")
                    raise_flag(nc, guard, flag_i, consts, 1)
                flag = nc.values_load(flag_i[0:1, 1:2], min_val=0, max_val=P)
                with nc.If(flag > 0):
                    nc.all_engine_barrier()
                    restore(nc, "uniform", x, kept)
                    with ExitStack() as phase:
                        attention(nc, phase, "uniform", True, x, ctx, w, consts, guard, "uniform")
        if until < 3:
            st = whole.enter_context(nc.semaphore("st"))
            with nc.Block() as block:
                @block.sync
                def _(sp):
                    for b in range(B):
                        sp.dma_start(out[b].rearrange("(t p) c -> p t c", p=P), x[:, b, :, :]).then_inc(st, 16)
                    sp.wait_ge(st, 16 * B)
        else:
            expert_choice(nc, whole, x, a, out)


_INS = ["x", "ctx_768", "L0_attn_Wq", "L0_attn_Wk", "L0_attn_Wv", "L0_attn_Wo", "L0_xattn_Wq", "L0_xattn_bq",
        "L0_xattn_Wk", "L0_xattn_bk", "L0_xattn_Wv", "L0_xattn_bv", "L0_xattn_Wo", "L0_xattn_bo", "L0_ffn_Wr",
        "L0_ffn_br", "L0_ffn_W_up", "L0_ffn_b_up", "L0_ffn_W_down", "L0_ffn_b_down"]
_OUTS = [((8, 512, 256), "float32")]


def kernel(**inputs):
    import numpy as _np
    import concourse.bacc as _bacc
    from concourse import mybir as _mybir
    from concourse.bass_utils import run_bass_kernel_spmd as _run

    nc = _bacc.Bacc("TRN2", target_bir_lowering=False, num_devices=1)
    arrays, args = {}, {}
    for name in _INS:
        v = _np.ascontiguousarray(inputs[name])
        arrays[f"in_{name}_dram"] = v
        args[name] = nc.dram_tensor(f"in_{name}_dram", v.shape, _mybir.dt.from_np(v.dtype), kind="ExternalInput").ap()
    (shape, dtype), = _OUTS
    out = nc.dram_tensor("out_0_dram", shape, _mybir.dt.from_np(_np.dtype(dtype)), kind="ExternalOutput").ap()
    decoder_block(nc, args, out)
    r = _run(nc, [arrays], core_ids=[0])
    return r.results[0]["out_0_dram"]
```

```python
from contextlib import ExitStack

import concourse.bass as bass
from concourse import mybir

F32, BF16, F16 = mybir.dt.float32, mybir.dt.bfloat16, mybir.dt.float16
U32, I32 = mybir.dt.uint32, mybir.dt.int32
ALU = mybir.AluOpType
ACT = mybir.ActivationFunctionType
AX = mybir.AxisListType

P = 128
SHIFT_UNIT = 64.0
MASKED = -1.0e30
LN_EPS = 1e-5
RSQRT_BITS = float(0x5F3759DF)
NEWTON_STEPS = 3
NEWTON_OPS = 4 * NEWTON_STEPS
SHIFT_ROW = 96
STACK = 98
SHIFT_DMA = 2 * 16
CLAMP = 10000.0
RINV_SCALE = 1024.0


def ahead(b, g, d):
    return b + (g + d) // 4, (g + d) % 4


def guess(dve, y, v, neg_half, var, semaphore, before):
    dve.tensor_scalar(v, var, LN_EPS, None, ALU.add).then_inc(semaphore, 1)
    dve.wait_ge(semaphore, before + 1)
    dve.tensor_scalar(y.bitcast(U32), v.bitcast(U32), 1, None, ALU.logical_shift_right).then_inc(semaphore, 1)
    dve.tensor_scalar(neg_half, v, -0.5, None, ALU.mult).then_inc(semaphore, 1)
    dve.wait_ge(semaphore, before + 3)
    dve.tensor_scalar(y.bitcast(I32), y.bitcast(I32), -1.0, RSQRT_BITS, ALU.mult, ALU.add).then_inc(semaphore, 1)


def newton(pool, y, neg_half, one_half, t, semaphore, before):
    n = before
    for _ in range(NEWTON_STEPS):
        for out, in0, in1, op in ((t, y, y, ALU.mult), (t, t, neg_half, ALU.mult), (t, t, one_half, ALU.add),
                                  (y, y, t, ALU.mult)):
            pool.tensor_tensor(out, in0, in1, op).then_inc(semaphore, 1)
            n = n + 1
            pool.wait_ge(semaphore, n)


def between(cross, first, last, g, j):
    if g == 1 and not last and (j < 2 or not cross):
        return [("q", j), ("k", j)]
    if g == 2 and j == 0 and not first:
        return [("wo", 0), ("wo", 1)]
    return []


class WorkBanks:

    def __init__(self, cross, batches, banks, clip):
        self.cross, self.batches, self.clip = cross, batches, clip
        self.table, self.count = {}, [0] * banks
        self.turn = 0
        for key in self.prologue():
            self._add(("pro",) + key)
        for b in range(batches):
            self.turn = 0
            for g in range(4):
                uses = self.step(b, g)
                for key in uses if b else self.step(1, g):
                    if key in uses:
                        self._add((b, g) + key)
                    else:
                        self.turn += 1
        for key in (("sp", 0), ("sp", 1), ("wo", 0), ("wo", 1)):
            self._add(("epi",) + key)

    def _add(self, key):
        bank = self.turn % len(self.count)
        self.turn += 1
        self.table[key] = (bank, self.count[bank])
        self.count[bank] += 1

    def prologue(self):
        out = [("tr", i) for i in range(4 if self.cross else 2)]
        for n in range(2 if self.cross else 4):
            out += [("q", n), ("k", n)]
        return out + [("mx", j, i) for j in range(4) for i in range(4)] + [("mt",)] + [
            ("mx", j, i) for j in (4, 5) for i in range(4)]

    def step(self, b, g):
        last = b == self.batches - 1
        out = []
        for j in range(4):
            head, there = (j + 2) % 4, not (last and g >= (3 if j < 2 else 2))
            out += [("mx", head, i) for i in (0, 1) if there]
            if j == 2 and not (last and g == 3):
                out += [("mt",)]
            extra = between(self.cross, b == 0, last, g, j)
            out += extra[:1]
            out += [("mx", head, 2)] if there else []
            out += extra[1:]
            out += [("mx", head, 3)] if there else []
            if j == 3 and (b >= 1 or g >= 2):
                out += [("sp",)]
            if self.clip:
                out += [("fl", j)]
        if g == 0:
            out += [("v", i) for i in range(2 if self.cross else 4)]
        if g == 0 and not last:
            out += [("tr", i) for i in range(4 if self.cross else 2)]
        return out

    def at(self, section, *key):
        if isinstance(section, (str, int)):
            return self.table[(section,) + key]
        bank, one = self.table[(1,) + key]
        again, two = self.table[(2,) + key]
        assert bank == again
        return bank, section * (two - one) + (2 * one - two)


def attention(nc, stack, name, cross, x, src, weights, consts, guard=None, mode="plain", keep=None):
    clip, uniform = mode == "clip", mode == "uniform"
    B, NT, C = x.shape[1], x.shape[2], x.shape[3]
    last_batch = B - 1
    CD = 16 if cross else 32
    CK = src.shape[-1]
    KT = [(0, P), (1, CK - P)]
    NV = 16 * CD
    SCALE = 0.25
    WID = [512] * 4 if cross else [512, 384, 256, 128]
    Q0 = [512 - w for w in WID]
    OFF = [sum(WID[:kb]) for kb in range(4)]
    HALF = [OFF[0], OFF[2]]
    EXP = [WID[0] + WID[1], WID[2] + WID[3]]
    SPLIT = CD
    WORK = 3
    banks = WorkBanks(cross, B, WORK, clip)
    V_USES = 2 if cross else 4
    PRODUCTS = [(t, i, j) for t in range(2) for i, j in ((0, 0), (0, 1), (1, 0))]
    TILES = 16 * CD // P
    ROUNDS = 2 if cross else 1
    PER_ROUND = 3 * 16
    CONSTS = 14 if clip else 12 if uniform else 11 if cross else 3
    WEIGHTS = 4 * TILES + (16 if cross else 3)
    ident, mask_qk, mask_kq, ident_b = consts["ident"], consts["mask_qk"], consts["mask_kq"], consts["ident_b"]

    def sb(n, shape, dt=F32):
        return stack.enter_context(nc.sbuf_tensor(f"{name}_{n}", shape, dt))

    def ps(n, shape):
        return stack.enter_context(nc.psum_tensor(f"{name}_{n}", shape, F32))

    semaphores = []
    stack.callback(nc.all_engine_barrier)
    stack.callback(lambda: nc.clear_and_free_semaphores(semaphores))

    def sem(n):
        semaphores.append(nc.alloc_semaphore(f"{name}_{n}"))
        return semaphores[-1]

    wq, wk, wv = ([sb(f"{n}_{part}", [P, 2, 16 * CD], F16) for part in ("high", "low")] for n in ("wq", "wk", "wv"))
    wo = sb("wo", [P, 4, C])
    xn = sb("xn", [P, NT, C])
    stats = sb("stats", [P, NT, 6])
    meanvar = sb("meanvar", [P, NT, 2])
    rstd = sb("rstd", [P, NT])
    veps, square, neg_half, one_half = (sb(n, [P, NT]) for n in ("veps", "square", "neg_half", "one_half"))
    wait_cell = sb("wait_cell", [P, 1])
    xnT = [sb(f"xnT_{part}", [P, 2, 512], F16) for part in ("high", "low")]
    qh, ql, kh, kl = (sb(n, [P, TILES, 512], F16) for n in ("qh", "ql", "kh", "kl"))
    qs = sb("qs", [P, 4, 4, 512], F16)
    ks = sb("ks", [P, 4, 4, 512], F16)
    rowmax = sb("rowmax", [P, 2, 16])
    shift_h = sb("shift_h", [16, 2, P], F16)
    shift_l = sb("shift_l", [16, 2, P], F16)
    probs = sb("probs", [P, 2, 4, sum(WID)])
    whole_w = probs[:, 0, :, :].rearrange("p j n -> p (j n)")[:, 0:3 * 2 * NV].rearrange("p (w t n) -> p w t n", w=3, t=2)
    SPLITS = [(w, parts, t, rows) for w, parts in enumerate((wq, wk, wv))
              for t, rows in (KT if w else [(0, P), (1, P)])]
    attT = sb("attT", [P, 4, 512])
    raw = sb("raw", [P, 512])
    sums_c, rinv_c = sb("sums_c", [P, 16]), sb("rinv_c", [P, 16])
    rinv_cs = sb("rinv_cs", [P, 2, 16], F16)
    rinv_rows = sb("rinv_rows", [P, 512], F16)
    if cross:
        ctx_in = sb("ctx_in", [P, NT, 2 * P])
        ctxT = [sb(f"ctxT_{part}", [P, 2, 512], F16) for part in ("high", "low")]
        val = sb("val", [P, 4, 16, 32])
        bq, bk = sb("bq", [P, 2]), sb("bk", [P, 2])
        bv, bo = sb("bv", [P, NV]), sb("bo", [P, C])
        is_nan = sb("is_nan", [P, 16])
    if uniform:
        zeros = sb("zeros", [P, 512])
    if clip:
        floor_w = sb("floor_w", [P, P], F16)
        floor_bias = sb("floor_bias", [P, 1])
        floors = sb("floors", [P, 512])
        odd, odd_max = sb("odd", [P, 512]), sb("odd_max", [P, 1])
    if not cross:
        val = sb("val", [P, 4, NV])
        sums = sb("sums", [P, 512])
        added = sb("added", [P, 2, 4, 512])
    kvT = ctxT if cross else xnT

    work = [ps(f"work{i}", [P, 512]) for i in range(WORK)]
    score = [ps("score0", [P, 1024]), ps("score1", [P, 1024 if cross else 512])]
    out_ps = ps("out_ps", [P, 512])
    if not cross:
        sum_ps = ps("sum_ps", [P, 512])

    full = [sem(f"work{i}_filled") for i in range(WORK)]
    free = [sem(f"work{i}_freed") for i in range(WORK)]
    weights_loaded, consts_set = sem("weights_loaded"), sem("consts_set")
    first_loaded, second_loaded, src_loaded = sem("first_loaded"), sem("second_loaded"), sem("src_loaded")
    ks_cleared = sem("ks_cleared")
    weights_high, weights_low, turned_high = sem("weights_high"), sem("weights_low"), sem("turned_high")
    ln_guess = sem("ln_guess")
    ln_stats, ln_aggr, ln_rstd, xn_ready = sem("ln_stats"), sem("ln_aggr"), sem("ln_rstd"), sem("xn_ready")
    hi_ready = sem("hi_ready")
    restacked = {w: [[sem(f"{w}_restacked{g}_{r}") for r in range(ROUNDS)] for g in range(4)] for w in "qk"}
    shift_hi = sem("shift_hi")
    shift_placed = [sem("shift_placed0"), sem("shift_placed1")]
    scores_ready, exp_done = sem("scores_ready"), sem("exp_done")
    pv_done, raw_ready, sums_moved = sem("pv_done"), sem("raw_ready"), sem("sums_moved")
    rinv_steps, rinv_placed = sem("rinv_steps"), sem("rinv_placed")
    if not cross:
        blocks_added = sem("blocks_added")
    if cross:
        bo_added, noted, x_kept = sem("bo_added"), sem("noted"), sem("x_kept")
        nan_noted = sem("nan_noted")
    if clip:
        scores_bounded, maxima_clipped = sem("scores_bounded"), sem("maxima_clipped")
        probs_clipped, odd_steps = sem("probs_clipped"), sem("odd_steps")

    def unit(b, g):
        return 4 * b + g

    def turns(b, g):
        return 2 * b + g // 2

    def wait(eng, semaphore, value):
        if not isinstance(value, int) or value > 0:
            eng.wait_ge(semaphore, value)

    def fill(eng, use):
        bank, n = use
        wait(eng, free[bank], n)
        return work[bank]

    def filled(eng, use):
        bank, n = use
        eng.wait_ge(full[bank], n + 1)
        return work[bank]

    def freed(eng, use):
        eng.wait_ge(free[use[0]], use[1] + 1)

    N_TR = 4 if cross else 2

    def last_transposes(b, section):
        if isinstance(b, int) and b == 0:
            return [banks.at("pro", "tr", i) for i in range(N_TR)]
        return [banks.at(section, 0, "tr", i) for i in range(N_TR)]

    def transposed(eng, b):
        eng.wait_ge(hi_ready, 2 * TILES * b + 1)

    def maxima_of(j, g, last):
        if j < 2:
            return None if last and g == 3 else (1, j + 2)
        return None if last and g >= 2 else (2, j - 2)

    def restack(eng, whats, g):
        for r in range(ROUNDS):
            for what in whats:
                dst, parts = (qs, (qh, qh, ql)) if what == "q" else (ks, (kh, kl, kh))
                for s, part in enumerate(parts):
                    to = dst[SPLIT * s:SPLIT * s + SPLIT, g, :, :]
                    row = 32 * g + CD * r
                    eng.dma_start(to if CD == 32 else to.rearrange("p (t r) n -> p r t n", t=2)[:, r],
                                  part[row:row + CD, :, :]).then_inc(restacked[what][g][r], 16)

    def steps(eng, emit, prologue, epilogue):
        prologue()
        for g in range(4):
            emit(0, g, True, False)
        with eng.Fori(1, last_batch) as b:
            for g in range(4):
                emit(b, g, False, False)
        for g in range(4):
            emit(last_batch, g, False, True)
        epilogue()

    block = stack.enter_context(nc.Block())

    @block.sync
    def _(sp):
        def load_context(b):
            if not (isinstance(b, int) and b == 0):
                transposed(sp, b - 1)
            sp.dma_start(ctx_in[:, :, 0:CK], src[b].rearrange("(t p) c -> p t c", p=P)).then_inc(src_loaded, 16)

        if not cross:
            sp.dma_start(x[:, 0, :, :], src[0].rearrange("(t p) c -> p t c", p=P)).then_inc(first_loaded, 16)
            sp.dma_start(x[:, 1, :, :], src[1].rearrange("(t p) c -> p t c", p=P)).then_inc(second_loaded, 16)
        else:
            load_context(0)
        for w_sb, w, tiles in ((whole_w[:, 0], weights["Wq"], [(0, P), (1, P)]), (whole_w[:, 1], weights["Wk"], KT)):
            for t, rows in tiles:
                columns = w[t * P:t * P + rows, :].rearrange("p (g m k) -> p m g k", g=4, k=32)
                for m in range(TILES):
                    sp.dma_start(w_sb[0:rows, t, m * P:(m + 1) * P].rearrange("p (g k) -> p g k", g=4), columns[:, m])\
                      .then_inc(weights_loaded, 16)
        for t, rows in KT:
            sp.dma_start(whole_w[0:rows, 2, t, :], weights["Wv"][t * P:t * P + rows, :]).then_inc(weights_loaded, 16)
        if cross:
            sp.wait_ge(consts_set, 2)
            for j in range(4):
                sp.dma_start(wo[32 * j:32 * j + CD, :, :], weights["Wo"].rearrange(
                    "(g j r) n -> j r g n", g=4, j=4)[j]).then_inc(weights_loaded, 16)
            for b_sb, w in ((bq, weights["bq"]), (bk, weights["bk"])):
                for g in range(4):
                    sp.dma_start(b_sb[32 * g:32 * g + 32, :], w[64 * g:64 * g + 64].rearrange("(t k) -> k t", t=2),
                                 allow_slow_non_contiguous=True).then_inc(weights_loaded, 16)
            sp.dma_start(bv[:, :], weights["bv"].rearrange("(a n) -> a n", a=1).to_broadcast([P, NV])).then_inc(weights_loaded, 16)
            sp.dma_start(bo[:, :], weights["bo"].rearrange("(a n) -> a n", a=1).to_broadcast([P, C])).then_inc(weights_loaded, 16)
        else:
            sp.dma_start(wo[:, :, :], weights["Wo"].rearrange("(g p) n -> p g n", p=P)).then_inc(weights_loaded, 16)

        def place_shift(b, g, section, key):
            freed(sp, banks.at(section, *key, "mt"))
            for r, part in enumerate((shift_h, shift_l)):
                sp.dma_start(qs[SHIFT_ROW + r:SHIFT_ROW + r + 1, g, :, :].rearrange("p j (i c) -> p (j i) c", c=P),
                             part[:, g % 2, :]).then_inc(shift_placed[g % 2], 16)

        def prologue():
            if cross:
                sp.wait_ge(consts_set, 9)
                sp.wait_ge(ks_cleared, 1)
            freed(sp, banks.at("pro", "k", TILES - 1))
            for g in range(3):
                restack(sp, "qk", g)
            place_shift(0, 0, "pro", ())
            if keep is not None:
                for b in range(B):
                    sp.dma_start(keep[b].rearrange("(t p) c -> p t c", p=P), x[:, b, :, :]).then_inc(x_kept, 16)
            if not cross:
                for b in range(2, B):
                    sp.dma_start(x[:, b, :, :], src[b].rearrange("(t p) c -> p t c", p=P)).then_inc(src_loaded, 16)

        def place_reciprocals(b, g):
            sp.wait_ge(rinv_steps, 3 * unit(b, g) + 3)
            for part in range(2):
                sp.dma_start(rinv_rows[4 * part:4 * part + 4, :], rinv_cs[:, part, :]).then_inc(rinv_placed, 16)

        def emit(b, g, first, last):
            u = unit(b, g)
            summed = not (first and g < 2)
            if cross and g == 0 and not last:
                load_context(b + 1)
            if g == 0 and not cross:
                wait(sp, scores_ready, 8 * u)
                restack(sp, "q", 3)
            if summed:
                place_reciprocals(*ahead(b, g, -2))
            if not (last and g == 3):
                place_shift(*ahead(b, g, 1), b, (g,))
            if g == 0:
                if cross:
                    wait(sp, scores_ready, 8 * u)
                restack(sp, "qk" if cross else "k", 3)
            elif not last:
                if g == 1:
                    freed(sp, banks.at(b, 1, "k", TILES - 1))
                elif g == 3:
                    sp.wait_ge(scores_ready, 8 * u)
                restack(sp, "qk", g - 1)

        def epilogue():
            for g in (2, 3):
                place_reciprocals(last_batch, g)

        steps(sp, emit, prologue, epilogue)

    @block.gpsimd
    def _(pool):
        cleared = [0]

        def clear(to, value):
            pool.memset(to, value).then_inc(consts_set, 1)
            cleared[0] += 1
            pool.wait_ge(consts_set, cleared[0])

        def deviations(b):
            pool.wait_ge(ln_guess, 4 * b + 4)
            newton(pool, rstd[:, :], neg_half[:, :], one_half[:, :], square[:, :], ln_rstd, NEWTON_OPS * b)

        def add_blocks(b, g, j):
            u = unit(b, g)
            if j == 0:
                wait(pool, pv_done, u - 1)
            pool.wait_ge(exp_done, 8 * u + 2 * j + 2)
            to, n = added[:, g % 2, j, :], 12 * u + 3 * j
            for kb in range(1, 4):
                p = probs[:, g % 2, j, OFF[kb]:OFF[kb] + WID[kb]]
                before = probs[:, g % 2, j, Q0[kb]:512] if kb == 1 else to[:, Q0[kb]:512]
                pool.tensor_tensor(to[:, Q0[kb]:512], before, p, ALU.add).then_inc(blocks_added, 1)
                if kb == 1:
                    pool.tensor_copy(to[:, 0:P], probs[:, g % 2, j, 0:P])
                if kb < 3:
                    pool.wait_ge(blocks_added, n + kb)

        def add_bias(b):
            pool.wait_ge(xn_ready, 4 * b + 4)
            if isinstance(b, int) and b == 0:
                pool.wait_ge(weights_loaded, 16 * WEIGHTS)
                if keep is not None:
                    pool.wait_ge(x_kept, 16 * B)
            for i in range(NT):
                ins = pool.tensor_tensor(x[:, b, i, :], x[:, b, i, :], bo[:, :], ALU.add)
            ins.then_inc(bo_added, 1)

        def prologue():
            clear(one_half[:, :], 1.5)
            if cross:
                clear(wo[:, :, :], 0.0)
                clear(ctx_in[:, :, CK:], 0.0)
                for part in wk + wv:
                    clear(part[CK - P:, 1, :], 0.0)
            deviations(0)
            clear(rinv_rows[:, :], 0.0)
            if cross:
                clear(qs[0:SHIFT_ROW, :, :, :], 0.0)
                clear(val[:, :, :, CD:], 1.0)
            clear(ks[SHIFT_ROW:SHIFT_ROW + 2, :, :, :], SHIFT_UNIT)
            if uniform:
                clear(zeros[:, :], 0.0)
            if clip:
                clear(floor_w[:, :], 0.0)
                clear(floor_bias[:, :], -CLAMP)
                clear(floor_w[SHIFT_ROW:SHIFT_ROW + 2, :], SHIFT_UNIT)
            assert cleared[0] == CONSTS

        def emit(b, g, first, last):
            if g == 0 and not last:
                deviations(b + 1)
            if g == 2 and cross:
                add_bias(b)
            if not cross:
                for j in range(4):
                    add_blocks(b, g, j)

        steps(pool, emit, prologue, lambda: None)

    @block.tensor
    def _(pe):
        def transposes(b, section, g):
            pe.wait_ge(xn_ready, 4 * b + 4)
            for c in range(2):
                use = banks.at(section, *g, "tr", c)
                dst = fill(pe, use)
                for i in range(NT):
                    ins = pe.transpose(dst[:, i * P:(i + 1) * P], xn[:, i, c * P:(c + 1) * P], ident[:, :])
                ins.then_inc(full[use[0]], 1)
            if cross:
                pe.wait_ge(src_loaded, 16 * b + 16)
                for c, rows in KT:
                    use = banks.at(section, *g, "tr", 2 + c)
                    dst = fill(pe, use)
                    for i in range(NT):
                        ins = pe.transpose(dst[:, i * P:(i + 1) * P], ctx_in[:, i, c * P:(c + 1) * P], ident[:, :])
                    ins.then_inc(full[use[0]], 1)

        def project(b, what, tile, section, key):
            if what == "q" and tile == 0:
                for use in last_transposes(b, section)[-2:]:
                    freed(pe, use)
            use = banks.at(section, *key, what, tile)
            dst = fill(pe, use)
            w, tokens = (wk, kvT) if what == "k" else (wq, xnT)
            for n, (t, i, j) in enumerate(PRODUCTS):
                ins = pe.matmul(dst[:, :], w[i][:, t, tile * P:(tile + 1) * P], tokens[j][:, t, :],
                                start=n == 0, stop=n == len(PRODUCTS) - 1)
            ins.then_inc(full[use[0]], 1)

        def maxima(b, g, j, section, key, tiles=range(4), key_head=None):
            for i in tiles:
                if j < ROUNDS and i == 0:
                    for what in "qk":
                        pe.wait_ge(restacked[what][g][j], PER_ROUND * b + PER_ROUND)
                use = banks.at(section, *key, "mx", j if key_head is None else key_head, i)
                dst = fill(pe, use)
                w = 512 if cross else (i + 1) * P
                ins = pe.matmul(dst[:, 0:w], qs[0:SHIFT_ROW, g, j, i * P:(i + 1) * P], ks[0:SHIFT_ROW, g, j, 0:w],
                                start=True, stop=cross)
                if not cross:
                    ins = pe.matmul(dst[:, i * P:w], ident_b[:, :], mask_qk[:, :], start=False, stop=True)
                ins.then_inc(full[use[0]], 1)

        def turn_maxima(b, g, section, key):
            use = banks.at(section, *key, "mt")
            last_maximum = banks.at(section, *key, "mx", 3, 3)
            dst = fill(pe, use)
            if use[0] != last_maximum[0]:
                freed(pe, last_maximum)
            if clip:
                pe.wait_ge(maxima_clipped, unit(b, g) + 1)
            pe.transpose(dst[0:16, 0:P], rowmax[:, g % 2, :], ident[:, :]).then_inc(full[use[0]], 1)

        def scores(b, g, j, half):
            if j == 0 and half == 0:
                pe.wait_ge(shift_placed[g % 2], SHIFT_DMA * turns(b, g) + SHIFT_DMA)
            wait(pe, exp_done, 8 * unit(b, g) + 2 * j + half - 1)
            for kb in (2 * half, 2 * half + 1):
                at = OFF[kb] - HALF[half]
                dst = score[half][:, at:at + WID[kb]]
                ins = pe.matmul(dst, ks[0:STACK, g, j, kb * P:(kb + 1) * P], qs[0:STACK, g, j, Q0[kb]:512],
                                start=True, stop=cross)
                if not cross:
                    ins = pe.matmul(score[half][:, at:at + P], ident_b[:, :], mask_kq[:, :], start=False, stop=True)
            ins.then_inc(scores_ready, 1)

        def weigh(b, g, kb, section=None):
            u = unit(b, g)
            if kb == 0:
                if clip:
                    pe.wait_ge(probs_clipped, 4 * u + 4)
                else:
                    pe.wait_ge(exp_done, 8 * u + 8)
                wait(pe, raw_ready, u)
                if g == 0:
                    for n in (V_USES - 2, V_USES - 1):
                        freed(pe, banks.at(section, 0, "v", n))
            cols = slice(Q0[kb], 512)
            for j in range(4):
                lhs = val[:, kb, 4 * g + j, :] if cross else val[:, kb, (4 * g + j) * CD:(4 * g + j + 1) * CD]
                ins = pe.matmul(out_ps[32 * j:32 * j + 32, cols], lhs, probs[:, g % 2, j, OFF[kb]:OFF[kb] + WID[kb]],
                                start=kb == 0, stop=kb == 3, tile_position=(0, 32 * j))
            if kb == 3 and cross:
                ins.then_inc(pv_done, 1)

        def add_up(b, g):
            pe.wait_ge(blocks_added, 12 * unit(b, g) + 12)
            for j in range(4):
                ins = pe.matmul(sum_ps[32 * j:32 * j + 32, :], consts["ones"][:, 0:32], added[:, g % 2, j, :],
                                start=True, stop=True, tile_position=(0, 32 * j))
            ins.then_inc(pv_done, 1)

        def spread(b, g, use):
            pe.wait_ge(rinv_placed, 32 * unit(b, g) + 32)
            dst = fill(pe, use)
            pe.matmul(dst[:, :], consts["spread"][:, :], rinv_rows[:, :], start=True, stop=True).then_inc(full[use[0]], 1)

        def values(b, g, section):
            for n in range(V_USES):
                use = banks.at(section, g, "v", n)
                dst = fill(pe, use)
                tiles = (2 * n, 2 * n + 1) if cross else (n,)
                for m, i in enumerate(tiles):
                    for k, (t, part, w_part) in enumerate(PRODUCTS):
                        ins = pe.matmul(dst[:, m * NV:(m + 1) * NV], kvT[part][:, t, i * P:(i + 1) * P],
                                        wv[w_part][:, t, :], start=k == 0, stop=k == len(PRODUCTS) - 1)
                ins.then_inc(full[use[0]], 1)

        def project_out(b, n, section, key, last_spread):
            if n == 0:
                freed(pe, last_spread)
            use = banks.at(section, *key, "wo", n)
            dst = fill(pe, use)
            for m in range(2):
                i = 2 * n + m
                for g in range(4):
                    ins = pe.matmul(dst[:, m * C:(m + 1) * C], attT[:, g, i * P:(i + 1) * P], wo[:, g, :],
                                    start=g == 0, stop=g == 3)
            ins.then_inc(full[use[0]], 1)

        def prologue():
            pe.wait_ge(weights_loaded, 16 * WEIGHTS)
            pe.wait_ge(weights_low, 6)
            if cross:
                pe.wait_ge(consts_set, 7)
            transposes(0, "pro", ())
            for t in range(TILES):
                project(0, "q", t, "pro", ())
                project(0, "k", t, "pro", ())
            for j in range(4):
                maxima(0, 0, j, "pro", ())
            turn_maxima(0, 0, "pro", ())
            for j in range(2):
                maxima(0, 1, j, "pro", (), key_head=4 + j)
            pe.wait_ge(consts_set, CONSTS)

        def emit(b, g, first, last):
            begun = not (first and g == 0)
            for j in range(4):
                def tile(i):
                    if maxima_of(j, g, last):
                        d, head = maxima_of(j, g, last)
                        maxima(*ahead(b, g, d), head, b, (g,), (i,))

                def extra(kind, n):
                    if kind == "wo":
                        project_out(b - 1, n, b, (g,), banks.at(b, 1, "sp"))
                    else:
                        project(b + 1, kind, n, b, (g,))

                extras = between(cross, first, last, g, j)
                tile(0)
                scores(b, g, j, 0)
                tile(1)
                scores(b, g, j, 1)
                if j == 2 and not (last and g == 3):
                    turn_maxima(*ahead(b, g, 1), b, (g,))
                if extras:
                    extra(*extras[0])
                tile(2)
                if extras:
                    extra(*extras[1])
                if begun:
                    weigh(*ahead(b, g, -1), j, b)
                tile(3)
                if j == 3 and not (first and g < 2):
                    spread(*ahead(b, g, -2), banks.at(b, g, "sp"))
                if clip:
                    use = banks.at(b, g, "fl", j)
                    dst = fill(pe, use)
                    pe.matmul(dst[:, :], floor_w[0:STACK, :], qs[0:STACK, g, j, :], start=True, stop=True)\
                      .then_inc(full[use[0]], 1)
                if begun and not cross and j == 3:
                    add_up(*ahead(b, g, -1))
            if g == 0:
                values(b, g, b)
            if g == 0 and not last:
                transposes(b + 1, b, (g,))

        def epilogue():
            for kb in range(4):
                weigh(last_batch, 3, kb)
            if not cross:
                add_up(last_batch, 3)
            for g in (2, 3):
                spread(last_batch, g, banks.at("epi", "sp", g - 2))
            for n in range(2):
                project_out(last_batch, n, "epi", (), banks.at("epi", "sp", 1))

        steps(pe, emit, prologue, epilogue)

    @block.scalar
    def _(act):
        def high_part(b, what, tile, section, key):
            if what == "q" and tile == 0 and not (isinstance(b, int) and b == 0):
                for done in restacked["q"][3] + restacked["k"][3]:
                    act.wait_ge(done, PER_ROUND * b)
            dst = qh if what == "q" else kh
            ps_ = filled(act, banks.at(section, *key, what, tile))
            if uniform:
                act.activation(dst[:, tile, :], zeros[:, :], ACT.Copy).then_inc(hi_ready, 1)
            elif cross:
                bias = (bq if what == "q" else bk)[:, tile:tile + 1]
                act.activation(dst[:, tile, :], ps_[:, :], ACT.Identity, bias=bias).then_inc(hi_ready, 1)
            else:
                act.activation(dst[:, tile, :], ps_[:, :], ACT.Copy).then_inc(hi_ready, 1)

        def exps(b, g, j, half):
            u = unit(b, g)
            if j == 0 and half == 0:
                wait(act, pv_done, u - 1)
            act.wait_ge(scores_bounded if clip else scores_ready, 8 * u + 2 * j + half + 1)
            act.activation(probs[:, g % 2, j, HALF[half]:HALF[half] + EXP[half]], score[half][:, 0:EXP[half]],
                           ACT.Exp, scale=SCALE).then_inc(exp_done, 1)

        def shift_high(b, g, section, key):
            use = banks.at(section, *key, "mt")
            ps_ = filled(act, use)
            wait(act, shift_placed[g % 2], SHIFT_DMA * turns(b, g))
            act.activation(shift_h[:, g % 2, :], ps_[0:16, 0:P], ACT.Copy, scale=-1.0 / SHIFT_UNIT).then_inc(shift_hi, 1)

        def copy_raw(b, g, spread_before=None):
            act.wait_ge(pv_done, unit(b, g) + 1)
            if spread_before:
                freed(act, spread_before)
            if not cross:
                act.activation(sums[:, :], sum_ps[:, :], ACT.Copy)
            act.activation(raw[:, :], out_ps[:, :], ACT.Copy).then_inc(raw_ready, 1)

        def keep_values(b, g, section):
            wait(act, pv_done, 4 * b)
            for n in range(V_USES):
                use = banks.at(section, g, "v", n)
                ps_ = filled(act, use)
                act.activation(val[:, n, :], ps_[:, :], ACT.Copy).then_inc(free[use[0]], 1)

        def gather_sums(b, g):
            act.wait_ge(raw_ready, unit(b, g) + 1)
            act.dma_start(sums_c[:, :], raw[CD:P:32, :] if cross else sums[0:P:32, :]).then_inc(sums_moved, 16)

        def turned_highs(b, section, g):
            for c in range(N_TR):
                use = banks.at(section, *g, "tr", c)
                ps_ = filled(act, use)
                act.activation((xnT if c < 2 else ctxT)[0][:, c % 2, :], ps_[:, :], ACT.Copy).then_inc(turned_high, 1)

        def prologue():
            act.wait_ge(weights_loaded, 16 * WEIGHTS)
            if cross:
                act.wait_ge(consts_set, CONSTS if mode != "plain" else 7)
            for w, parts, t, rows in SPLITS:
                act.activation(parts[0][0:rows, t, :], whole_w[0:rows, w, t, :], ACT.Copy).then_inc(weights_high, 1)
            turned_highs(0, "pro", ())
            for t in range(TILES):
                high_part(0, "q", t, "pro", ())
                high_part(0, "k", t, "pro", ())
            shift_high(0, 0, "pro", ())

        def emit(b, g, first, last):
            if not (first and g < 2):
                before = ahead(b, g, -1)
                copy_raw(*ahead(b, g, -2), None if first and g == 2 else banks.at(*before, "sp"))
            for j in range(4):
                exps(b, g, j, 0)
                if j == 0 and not (first and g < 2):
                    gather_sums(*ahead(b, g, -2))
                if j == 2 and not (last and g == 3):
                    shift_high(*ahead(b, g, 1), b, (g,))
                exps(b, g, j, 1)
                for kind, n in between(cross, first, last, g, j):
                    if kind != "wo":
                        high_part(b + 1, kind, n, b, (g,))
                if clip:
                    use = banks.at(b, g, "fl", j)
                    ps_ = filled(act, use)
                    wait(act, probs_clipped, 4 * unit(b, g) + j)
                    act.activation(floors[:, :], ps_[:, :], ACT.Exp, scale=SCALE, bias=floor_bias[:, 0:1])\
                       .then_inc(free[use[0]], 1)
            if g == 0 and not cross:
                keep_values(b, g, b)
            if g == 0 and not last:
                turned_highs(b + 1, b, (g,))

        def epilogue():
            copy_raw(last_batch, 2, banks.at(last_batch, 3, "sp"))
            gather_sums(last_batch, 2)
            copy_raw(last_batch, 3, banks.at("epi", "sp", 0))
            gather_sums(last_batch, 3)

        steps(act, emit, prologue, epilogue)

    @block.vector
    def _(dve):
        def statistics(b, tiles=range(4)):
            if not cross and tiles[0] == 0:
                if isinstance(b, int) and b < 2:
                    dve.wait_ge((first_loaded, second_loaded)[b], 16)
                else:
                    dve.wait_ge(src_loaded, 16 * (B - 2))
            for i in tiles:
                dve.bn_stats(stats[:, i, :], x[:, b, i, :]).then_inc(ln_stats, 1)

        def variances(b):
            dve.wait_ge(ln_stats, 4 * b + 4)
            dve.memset(wait_cell[:, :], 0.0)
            for i in range(NT):
                dve.bn_aggr(meanvar[:, i, :], stats[:, i, :]).then_inc(ln_aggr, 1)
            dve.wait_ge(ln_aggr, 4 * b + 4)
            guess(dve, rstd[:, :], veps[:, :], neg_half[:, :], meanvar[:, :, 1], ln_guess, 4 * b)

        def turned_lows(b, section, g):
            for c in range(N_TR):
                use = banks.at(section, *g, "tr", c)
                high, low = xnT if c < 2 else ctxT
                dve.wait_ge(turned_high, N_TR * b + c + 1)
                dve.tensor_tensor(low[:, c % 2, :], work[use[0]][:, :], high[:, c % 2, :], ALU.subtract)\
                   .then_inc(free[use[0]], 1)

        def layer_norm(b, tiles=range(4)):
            if tiles[0] == 0:
                dve.wait_ge(ln_rstd, NEWTON_OPS * b + NEWTON_OPS)
                if not (isinstance(b, int) and b == 0):
                    transposed(dve, b - 1)
            for i in tiles:
                dve.tensor_scalar(xn[:, i, :], x[:, b, i, :], meanvar[:, i, 0:1], rstd[:, i:i + 1],
                                  ALU.subtract, ALU.mult).then_inc(xn_ready, 1)

        def low_part(b, what, tile, section, key):
            m, hi, lo = (0, qh, ql) if what == "q" else (1, kh, kl)
            use = banks.at(section, *key, what, tile)
            dve.wait_ge(hi_ready, 2 * (TILES * b + tile) + m + 1)
            if uniform:
                ins = dve.memset(lo[:, tile, :], 0.0)
            elif cross:
                bias = (bq if what == "q" else bk)[:, tile:tile + 1]
                ins = dve.scalar_tensor_tensor(out=lo[:, tile, :], in0=work[use[0]][:, :], scalar=bias,
                                               in1=hi[:, tile, :], op0=ALU.add, op1=ALU.subtract)
            else:
                ins = dve.tensor_tensor(lo[:, tile, :], work[use[0]][:, :], hi[:, tile, :], ALU.subtract)
            ins.then_inc(free[use[0]], 1)

        def maxima(b, g, j, section, key, tiles=range(4), key_head=None):
            for i in tiles:
                use = banks.at(section, *key, "mx", j if key_head is None else key_head, i)
                ps_ = filled(dve, use)
                w = 512 if cross else (i + 1) * P
                ins = dve.tensor_reduce(rowmax[:, g % 2, 4 * j + i:4 * j + i + 1], ps_[:, 0:w], AX.X, ALU.max)
                ins.then_inc(free[use[0]], 1)
            if clip and j == 3 and i == 3:
                freed(dve, use)
                dve.tensor_scalar(rowmax[:, g % 2, :], rowmax[:, g % 2, :], CLAMP / SCALE, -CLAMP / SCALE,
                                  ALU.min, ALU.max).then_inc(maxima_clipped, 1)
        def note_maxima(b, g, section, key):
            wait(dve, noted, 2 * unit(b, g))
            freed(dve, banks.at(section, *key, "mx", 3, 3))
            for place, op in (("highest", ALU.max), ("lowest", ALU.min)):
                dve.tensor_tensor(guard[place][:, :], guard[place][:, :], rowmax[:, g % 2, :], op).then_inc(noted, 1)

        def bound_scores(b, g, j, half):
            h = 8 * unit(b, g) + 2 * j + half
            dve.wait_ge(scores_ready, h + 1)
            for n in range(2):
                s = score[half][:, 512 * n:512 * n + 512]
                m = 4 * (2 * h + n)
                dve.tensor_copy(odd[:, :], s).then_inc(odd_steps, 1)
                dve.wait_ge(odd_steps, m + 1)
                dve.tensor_tensor(odd[:, :], odd[:, :], odd[:, :], ALU.not_equal).then_inc(odd_steps, 1)
                dve.wait_ge(odd_steps, m + 2)
                dve.tensor_reduce(odd_max[:, :], odd[:, :], AX.X, ALU.max).then_inc(odd_steps, 1)
                dve.wait_ge(odd_steps, m + 3)
                dve.tensor_tensor(guard["nan"][:, 0:1], guard["nan"][:, 0:1], odd_max[:, :], ALU.max).then_inc(odd_steps, 1)
                dve.wait_ge(odd_steps, m + 4)
                ins = dve.tensor_scalar(s, s, 0.0, None, ALU.min)
            ins.then_inc(scores_bounded, 1)

        def lift_probs(b, g, j):
            dve.wait_ge(exp_done, 8 * unit(b, g) + 2 * j + 2)
            freed(dve, banks.at(b, g, "fl", j))
            for kb in range(4):
                p = probs[:, g % 2, j, 512 * kb:512 * kb + 512]
                ins = dve.tensor_tensor(p, p, floors[:, :], ALU.max)
            ins.then_inc(probs_clipped, 1)

        def shift_low(b, g, section, key):
            use = banks.at(section, *key, "mt")
            dve.wait_ge(shift_hi, unit(b, g) + 1)
            dve.scalar_tensor_tensor(out=shift_l[:, g % 2, :], in0=work[use[0]][0:16, 0:P], scalar=-1.0 / SHIFT_UNIT,
                                     in1=shift_h[:, g % 2, :], op0=ALU.mult, op1=ALU.subtract).then_inc(free[use[0]], 1)

        def reciprocals(b, g, part):
            u = unit(b, g)
            plain = mode == "plain" and cross
            if part == 0:
                dve.wait_ge(sums_moved, 16 * u + 16)
                if plain:
                    dve.tensor_tensor(is_nan[:, :], sums_c[:, :], sums_c[:, :], ALU.not_equal).then_inc(nan_noted, 1)
                dve.reciprocal(rinv_c[:, :], sums_c[:, :]).then_inc(rinv_steps, 1)
            elif part == 1:
                dve.wait_ge(rinv_steps, 3 * u + 1)
                dve.tensor_scalar(rinv_cs[:, 0, :], rinv_c[:, :], RINV_SCALE, None, ALU.mult).then_inc(rinv_steps, 1)
                if plain:
                    dve.wait_ge(nan_noted, 2 * u + 1)
                    dve.tensor_tensor(guard["nan"][:, :], guard["nan"][:, :], is_nan[:, :], ALU.max).then_inc(nan_noted, 1)
            else:
                dve.wait_ge(rinv_steps, 3 * u + 2)
                dve.scalar_tensor_tensor(out=rinv_cs[:, 1, :], in0=rinv_c[:, :], scalar=RINV_SCALE,
                                         in1=rinv_cs[:, 0, :], op0=ALU.mult, op1=ALU.subtract).then_inc(rinv_steps, 1)

        def normalise(b, g, use):
            ps_ = filled(dve, use)
            dve.tensor_tensor(attT[:, g, :], raw[:, :], ps_[:, :], ALU.mult).then_inc(free[use[0]], 1)

        def keep_values(b, g, section):
            wait(dve, pv_done, 4 * b)
            for n in range(V_USES):
                use = banks.at(section, g, "v", n)
                ps_ = filled(dve, use)
                for m in range(2):
                    ins = dve.tensor_tensor(val[:, 2 * n + m, :, 0:CD],
                                            ps_[:, m * NV:(m + 1) * NV].rearrange("p (h d) -> p h d", h=16),
                                            bv[:, :].rearrange("p (h d) -> p h d", h=16), ALU.add)
                ins.then_inc(free[use[0]], 1)

        def residual(b, n, section, key):
            if cross and n == 0:
                dve.wait_ge(bo_added, b + 1)
            use = banks.at(section, *key, "wo", n)
            ps_ = filled(dve, use)
            xs = x[:, b, 2 * n:2 * n + 2, :].rearrange("p t c -> p (t c)")
            dve.tensor_tensor(xs, xs, ps_[:, :], ALU.add).then_inc(free[use[0]], 1)

        def prologue():
            statistics(0)
            variances(0)
            if cross:
                dve.memset(ks[0:SHIFT_ROW, :, :, :], 0.0).then_inc(ks_cleared, 1)
            layer_norm(0)
            if cross:
                dve.wait_ge(consts_set, 7)
            for n, (w, parts, t, rows) in enumerate(SPLITS):
                dve.wait_ge(weights_high, n + 1)
                dve.tensor_tensor(parts[1][0:rows, t, :], whole_w[0:rows, w, t, :], parts[0][0:rows, t, :],
                                  ALU.subtract).then_inc(weights_low, 1)
            turned_lows(0, "pro", ())
            for t in range(TILES):
                low_part(0, "q", t, "pro", ())
                low_part(0, "k", t, "pro", ())
            for j in range(4):
                maxima(0, 0, j, "pro", ())
            shift_low(0, 0, "pro", ())
            if mode == "plain" and cross:
                note_maxima(0, 0, "pro", ())
            for j in range(2):
                maxima(0, 1, j, "pro", (), key_head=4 + j)

        def emit(b, g, first, last):
            for j in range(4):
                def some(tiles):
                    if maxima_of(j, g, last):
                        d, head = maxima_of(j, g, last)
                        maxima(*ahead(b, g, d), head, b, (g,), tiles)

                def extra(kind, n):
                    if kind == "wo":
                        residual(b - 1, n, b, (g,))
                    else:
                        low_part(b + 1, kind, n, b, (g,))

                extras = between(cross, first, last, g, j)
                some((0, 1))
                if clip:
                    bound_scores(b, g, j, 0)
                summed = not (first and g < 2)
                if j == 0 and g == 0 and not last:
                    statistics(b + 1, (0, 1))
                if j == 3 and g == 0 and not last:
                    layer_norm(b + 1, (0, 1))
                if j in (1, 2) and summed:
                    reciprocals(*ahead(b, g, -2), 2 * (j - 1))
                if j == 2 and not (last and g == 3):
                    shift_low(*ahead(b, g, 1), b, (g,))
                if clip:
                    bound_scores(b, g, j, 1)
                if extras:
                    extra(*extras[0])
                some((2,))
                if extras:
                    extra(*extras[1])
                some((3,))
                if j == 3 and not (first and g < 2):
                    normalise(*ahead(b, g, -2), banks.at(b, g, "sp"))
                if clip:
                    lift_probs(b, g, j)
                if j == 0 and g == 0 and not last:
                    statistics(b + 1, (2, 3))
                if j == 1 and g == 0 and not last:
                    variances(b + 1)
                if j == 3 and g == 0 and not last:
                    layer_norm(b + 1, (2, 3))
                if j == 1 and summed:
                    reciprocals(*ahead(b, g, -2), 1)
                if j == 2 and mode == "plain" and cross and not (last and g == 3):
                    note_maxima(*ahead(b, g, 1), b, (g,))
            if g == 0 and cross:
                keep_values(b, g, b)
            if g == 0 and not last:
                turned_lows(b + 1, b, (g,))

        def epilogue():
            for g in (2, 3):
                for part in range(3):
                    reciprocals(last_batch, g, part)
                normalise(last_batch, g, banks.at("epi", "sp", g - 2))
            for n in range(2):
                residual(last_batch, n, "epi", ())

        steps(dve, emit, prologue, epilogue)


def expert_choice(nc, stack, x, a, out):
    B, NT, C = x.shape[1], x.shape[2], x.shape[3]
    T = B * NT
    E = a["L0_ffn_W_down"].shape[0]
    F = a["L0_ffn_W_down"].shape[1]
    GROUPS = a["L0_ffn_W_up"].shape[0]
    PER_GROUP = E // GROUPS
    CAP = T * P // E
    Q = CAP // P
    FT = -(-F // P)
    FR = F - (FT - 1) * P
    BIAS_ROW = 64
    ROW = C + E
    HI, LO = CAP // 32, 32
    BITS = 30
    outer = stack
    rows = nc.dram_tensor("token_rows", [T * P, ROW], F32).ap()

    def sb(n, shape, dt=F32, s=None):
        return (s or outer).enter_context(nc.sbuf_tensor("ffn_" + n, shape, dt))

    def sem(n):
        return outer.enter_context(nc.semaphore("ffn_" + n))

    w_up = sb("w_up", [P, GROUPS, 2, F])
    w_down = sb("w_down", [P, E, FT, C])
    b_up = sb("b_up", [P, GROUPS, FT])
    idx = sb("idx", [P, E * Q], U32)
    ident = sb("ident", [P, P])
    mid = sb("mid", [P, FT, CAP])
    down_cleared, up_loaded, down_loaded = sem("down_cleared"), sem("up_loaded"), sem("down_loaded")
    DOWN_DMAS = 3 * E
    UP_DMAS = 2 + GROUPS
    x_stored, rows_stored, gates_stored = sem("x_stored"), sem("rows_stored"), sem("gates_stored")

    with ExitStack() as s:
        def sb2(n, shape, dt=F32):
            return sb(n, shape, dt, s)

        xn = sb2("xn", [P, B, NT, C])
        stats, meanvar = sb2("stats", [P, T, 6]), sb2("meanvar", [P, T, 2])
        rstd, veps, square = sb2("rstd", [P, T]), sb2("veps", [P, T]), sb2("square", [P, T])
        neg_half, one_half = sb2("neg_half", [P, T]), sb2("one_half", [P, T])
        xT = sb2("xT", [P, 2, 2, 512])
        wr, br = sb2("wr", [P, 2, E]), sb2("br", [P, E])
        logits = sb2("logits", [P, T, E])
        red, gates, gates_e = sb2("red", [P, T]), sb2("gates", [P, T, E]), sb2("gates_e", [P, E, T])
        ones_b, before = sb2("ones_b", [P, P], BF16), sb2("before", [P, P], BF16)
        diag = sb2("diag", [P, E, LO])
        carry = sb2("carry", [P, E, T])
        iota_i = sb2("iota_i", [P, T + HI + LO], I32)
        iota = sb2("iota", [P, T + HI + LO])
        tok, count_hi, count_lo = iota[:, 0:T], iota[:, T:T + HI], iota[:, T + HI:]
        thr, best = sb2("thr", [P, E]), sb2("best", [P, E])
        trial, bits = sb2("trial", [P, 3, E]), sb2("bits", [P, 3, E])
        counts = sb2("counts", [P, 3, E])
        count, need = sb2("count", [P, E]), sb2("need", [P, E])
        over = sb2("over", [P, 3, E, T], BF16)
        gt, eq, sel = sb2("gt", [P, E, T], BF16), sb2("eq", [P, E, T], BF16), sb2("sel", [P, E, T], BF16)
        tile_sum, rank, place_i = sb2("tile_sum", [P, E, T]), sb2("rank", [P, E, T]), sb2("place_i", [P, E, T], I32)
        hi_i, lo_i = sb2("hi_i", [P, E, T], I32), sb2("lo_i", [P, E, T], I32)
        hi, lo = sb2("hi", [P, E, T]), sb2("lo", [P, E, T])
        pick_hi = sb2("pick_hi", [P, T, E, HI])
        pick_lo = xn[:, :, :, :].rearrange("p b i c -> p (b i c)").rearrange("p (t e l) -> p t e l", t=T, e=E)
        own, folded = sb2("own", [P, E, LO]), sb2("folded", [P, LO])
        turn_ps = [s.enter_context(nc.psum_tensor(f"ffn_turn{i}", [P, 512], F32)) for i in range(3)]
        logit_ps = s.enter_context(nc.psum_tensor("ffn_logit_ps", [P, 512], F32))
        count_ps = s.enter_context(nc.psum_tensor("ffn_count_ps", [P, 1024], F32))
        rank_ps = s.enter_context(nc.psum_tensor("ffn_rank_ps", [P, 512], F32))
        idx_ps = s.enter_context(nc.psum_tensor("ffn_idx_ps", [P, 512], F32))
        idxT_ps = turn_ps[0]

        consts_made, const_steps, router_loaded = sem("consts_made"), sem("const_steps"), sem("router_loaded")
        ln_stats, ln_aggr, ln_guess, ln_rstd, xn_ready = (sem(n) for n in ("ln_stats", "ln_aggr", "ln_guess", "ln_rstd", "xn_ready"))
        turned, turned_kept, logits_done = (sem(n) for n in ("turned", "turned_kept", "logits_done"))
        chain, shifted, exps_done, gates_ready = (sem(n) for n in ("chain", "shifted", "exps_done", "gates_ready"))
        over_ready, over_counted, search, mask_ready, mask_counted = (
            sem(n) for n in ("over_ready", "over_counted", "search", "mask_ready", "mask_counted"))
        picks_ready, picked, folded_ready, idx_turned, idx_ready = (
            sem(n) for n in ("picks_ready", "picked", "folded_ready", "idx_turned", "idx_ready"))

        with nc.Block() as block:
            @block.sync
            def _(sp):
                sp.dma_start(wr[:, :, :], a["L0_ffn_Wr"].rearrange("(t p) e -> p t e", p=P)).then_inc(router_loaded, 16)
                sp.dma_start(br[:, :], a["L0_ffn_br"].rearrange("(a e) -> a e", a=1).to_broadcast([P, E])).then_inc(router_loaded, 16)
                for b in range(B):
                    sp.dma_start(out[b].rearrange("(t p) c -> p t c", p=P), x[:, b, :, :]).then_inc(x_stored, 16)
                for b in range(B):
                    sp.wait_ge(xn_ready, 4 * b + 4)
                    sp.dma_start(rows[512 * b:512 * b + 512, 0:C].rearrange("(t p) c -> p t c", p=P), xn[:, b, :, :])\
                      .then_inc(rows_stored, 16)
                sp.dma_start(w_up[:, :, :, :].rearrange("p g t f -> p (g t) f"),
                             a["L0_ffn_W_up"].rearrange("g (t p) f -> p (g t) f", p=P)).then_inc(up_loaded, 16)
                for g in range(GROUPS):
                    sp.dma_start(b_up[:, g, 0:FT - 1], a["L0_ffn_b_up"][g, 0:(FT - 1) * P].rearrange("(t p) -> p t", p=P),
                                 allow_slow_non_contiguous=True).then_inc(up_loaded, 16)
                sp.dma_start(b_up[0:FR, :, FT - 1], a["L0_ffn_b_up"][:, (FT - 1) * P:F].rearrange("g p -> p g"),
                             allow_slow_non_contiguous=True).then_inc(up_loaded, 16)
                sp.wait_ge(down_cleared, 1)
                for e in range(E):
                    w = a["L0_ffn_W_down"][e]
                    sp.dma_start(w_down[:, e, 0:FT - 1, :], w[0:(FT - 1) * P, :].rearrange("(t p) n -> p t n", p=P))\
                      .then_inc(down_loaded, 16)
                    sp.dma_start(w_down[0:FR, e, FT - 1, :], w[(FT - 1) * P:F, :]).then_inc(down_loaded, 16)
                    sp.dma_start(w_down[BIAS_ROW:BIAS_ROW + 1, e, FT - 1, :], a["L0_ffn_b_down"][e:e + 1, :])\
                      .then_inc(down_loaded, 16)
                sp.wait_ge(gates_ready, 1)
                sp.dma_start(rows[:, C:ROW].rearrange("(t p) e -> p t e", p=P), gates[:, :, :],
                             allow_slow_non_contiguous=True).then_inc(gates_stored, 16)
                sp.wait_ge(x_stored, 16 * B)
                sp.wait_ge(rows_stored, 16 * B)
                sp.wait_ge(gates_stored, 16)

            @block.gpsimd
            def _(pool):
                n = [0]

                def step(ins):
                    ins.then_inc(const_steps, 1)
                    n[0] += 1
                    pool.wait_ge(const_steps, n[0])

                pool.memset(w_down[:, :, FT - 1, :], 0.0).then_inc(down_cleared, 1)
                pool.wait_ge(down_cleared, 1)
                step(pool.memset(ident[:, :], 0.0))
                step(pool.affine_select(out=ident[:, :], in_=ident[:, :], compare_op=ALU.not_equal, fill=1.0, base=0,
                                        pattern=[[-1, P]], channel_multiplier=1))
                step(pool.memset(ones_b[:, :], 1.0))
                step(pool.memset(before[:, :], 1.0))
                step(pool.affine_select(out=before[:, :], in_=before[:, :], compare_op=ALU.is_gt, fill=0.0, base=0,
                                        pattern=[[1, P]], channel_multiplier=-1))
                step(pool.memset(diag[:, :, :], 1.0))
                step(pool.affine_select(out=diag[:, :, :], in_=diag[:, :, :], compare_op=ALU.is_ge, fill=0.0, base=0,
                                        pattern=[[-HI, E], [0, LO]], channel_multiplier=1))
                step(pool.affine_select(out=diag[:, :, :], in_=diag[:, :, :], compare_op=ALU.is_ge, fill=0.0, base=HI - 1,
                                        pattern=[[HI, E], [0, LO]], channel_multiplier=-1))
                step(pool.memset(carry[:, :, :], 1.0))
                step(pool.memset(carry[:, :, 0:1], 0.0))
                step(pool.iota(iota_i[:, 0:T], [[P, T]], base=0, channel_multiplier=1))
                step(pool.iota(iota_i[:, T:T + HI], [[1, HI]], base=1, channel_multiplier=0))
                step(pool.iota(iota_i[:, T + HI:], [[1, LO]], base=0, channel_multiplier=0))
                step(pool.tensor_copy(iota[:, :], iota_i[:, :]))
                step(pool.memset(one_half[:, :], 1.5))
                step(pool.memset(thr[:, :], 0.0))
                for which, value in enumerate((2.0 ** -95, 2.0 ** -63, 2.0 ** -31)):
                    step(pool.memset(bits[:, which, :], value))
                step(pool.memset(mid[:, FT - 1, :], 0.0))
                pool.memset(mid[BIAS_ROW:BIAS_ROW + 1, FT - 1, :], 1.0).then_inc(consts_made, 1)
                pool.wait_ge(consts_made, 1)
                pool.wait_ge(ln_guess, 4)
                newton(pool, rstd[:, :], neg_half[:, :], one_half[:, :], square[:, :], ln_rstd, 0)

            @block.vector
            def _(dve):
                n = [0]

                def step(ins):
                    ins.then_inc(chain, 1)
                    n[0] += 1
                    dve.wait_ge(chain, n[0])

                for b in range(B):
                    for i in range(NT):
                        dve.bn_stats(stats[:, 4 * b + i, :], x[:, b, i, :]).then_inc(ln_stats, 1)
                dve.wait_ge(ln_stats, T)
                for t in range(T):
                    dve.bn_aggr(meanvar[:, t, :], stats[:, t, :]).then_inc(ln_aggr, 1)
                dve.wait_ge(ln_aggr, T)
                guess(dve, rstd[:, :], veps[:, :], neg_half[:, :], meanvar[:, :, 1], ln_guess, 0)
                dve.wait_ge(ln_rstd, NEWTON_OPS)
                for b in range(B):
                    for i in range(NT):
                        dve.tensor_scalar(xn[:, b, i, :], x[:, b, i, :], meanvar[:, 4 * b + i, 0:1],
                                          rstd[:, 4 * b + i:4 * b + i + 1], ALU.subtract, ALU.mult).then_inc(xn_ready, 1)
                dve.wait_ge(router_loaded, 32)
                dve.wait_ge(logits_done, B)
                step(dve.tensor_tensor(logits[:, :, :], logit_ps[:, 0:T * E].rearrange("p (t e) -> p t e", e=E),
                                       br[:, :].unsqueeze(1).broadcast_to([P, T, E]), ALU.add))
                step(dve.tensor_reduce(red[:, :], logits[:, :, :], AX.X, ALU.max))
                dve.tensor_tensor(logits[:, :, :], logits[:, :, :], red[:, :].unsqueeze(2).broadcast_to([P, T, E]),
                                  ALU.subtract).then_inc(shifted, 1)
                dve.wait_ge(exps_done, 1)
                step(dve.tensor_reduce(red[:, :], logits[:, :, :], AX.X, ALU.add))
                step(dve.reciprocal(red[:, :], red[:, :]))
                dve.tensor_tensor(gates[:, :, :], logits[:, :, :], red[:, :].unsqueeze(2).broadcast_to([P, T, E]),
                                  ALU.mult).then_inc(gates_ready, 1)
                dve.wait_ge(gates_ready, 1)
                step(dve.tensor_copy(gates_e[:, :, :], gates[:, :, :].rearrange("p t e -> p e t")))
                dve.wait_ge(consts_made, 1)

                def wide(v):
                    return v[:, :].unsqueeze(2).broadcast_to([P, E, T])

                with dve.Fori(0, BITS // 2) as k:
                    dve.tensor_tensor(trial[:, :, :].bitcast(U32), thr[:, :].bitcast(U32).unsqueeze(1).broadcast_to([P, 3, E]),
                                      bits[:, :, :].bitcast(U32), ALU.bitwise_or).then_inc(search, 1)
                    dve.wait_ge(search, 6 * k + 1)
                    for which in range(3):
                        ins = dve.tensor_tensor(over[:, which, :, :], gates_e[:, :, :],
                                                trial[:, which, :].unsqueeze(2).broadcast_to([P, E, T]), ALU.is_ge)
                    ins.then_inc(over_ready, 1)
                    dve.tensor_scalar(bits[:, :, :].bitcast(U32), bits[:, :, :].bitcast(U32), 2, None,
                                      ALU.logical_shift_right).then_inc(search, 1)
                    dve.wait_ge(over_counted, k + 1)
                    dve.tensor_reduce(counts[:, :, :].rearrange("p n e -> p (n e)"),
                                      count_ps[:, 0:3 * E * T].rearrange("p (n t) -> p n t", t=T), AX.X, ALU.add)\
                       .then_inc(search, 1)
                    dve.wait_ge(search, 6 * k + 3)
                    dve.scalar_tensor_tensor(out=trial[:, :, :], in0=counts[:, :, :], scalar=float(CAP), in1=trial[:, :, :],
                                             op0=ALU.is_ge, op1=ALU.mult).then_inc(search, 1)
                    dve.wait_ge(search, 6 * k + 4)
                    dve.tensor_reduce(best[:, :], trial[:, :, :].rearrange("p n e -> p e n"), AX.X, ALU.max).then_inc(search, 1)
                    dve.wait_ge(search, 6 * k + 5)
                    dve.tensor_tensor(thr[:, :], thr[:, :], best[:, :], ALU.max).then_inc(search, 1)
                    dve.wait_ge(search, 6 * k + 6)
                step(dve.tensor_tensor(gt[:, :, :], gates_e[:, :, :], wide(thr), ALU.is_gt))
                dve.tensor_tensor(eq[:, :, :], gates_e[:, :, :], wide(thr), ALU.is_equal).then_inc(mask_ready, 1)
                dve.wait_ge(mask_counted, 1)
                step(dve.tensor_reduce(count[:, :], count_ps[:, 0:E * T].rearrange("p (e t) -> p e t", e=E), AX.X, ALU.add))
                step(dve.tensor_scalar(need[:, :], count[:, :], -1.0, float(CAP), ALU.mult, ALU.add))

                def ranks(bank):
                    step(dve.tensor_copy(tile_sum[:, :, :].rearrange("p e t -> p (e t)"), bank[:, 256:512]))
                    step(dve.tensor_tensor_scan(rank[:, :, :].rearrange("p e t -> p (e t)"),
                                                carry[:, :, :].rearrange("p e t -> p (e t)"),
                                                tile_sum[:, :, :].rearrange("p e t -> p (e t)"), 0.0, ALU.mult, ALU.add))
                    step(dve.tensor_tensor(rank[:, :, :], rank[:, :, :], tile_sum[:, :, :], ALU.subtract))
                    step(dve.tensor_tensor(rank[:, :, :].rearrange("p e t -> p (e t)"),
                                           rank[:, :, :].rearrange("p e t -> p (e t)"), bank[:, 0:256], ALU.add))

                ranks(rank_ps)
                step(dve.tensor_tensor(rank[:, :, :], rank[:, :, :], wide(need), ALU.is_lt))
                step(dve.tensor_tensor(sel[:, :, :], rank[:, :, :], eq[:, :, :], ALU.mult))
                step(dve.tensor_tensor(sel[:, :, :], sel[:, :, :], gt[:, :, :], ALU.add))
                dve.tensor_scalar(over[:, 0, :, :], sel[:, :, :], 1.0, None, ALU.mult).then_inc(mask_ready, 1)
                dve.wait_ge(mask_counted, 2)
                ranks(rank_ps)
                step(dve.tensor_copy(place_i[:, :, :], rank[:, :, :]))
                step(dve.tensor_scalar(hi_i[:, :, :], place_i[:, :, :], 5, None, ALU.logical_shift_right))
                step(dve.tensor_scalar(lo_i[:, :, :], place_i[:, :, :], LO - 1, None, ALU.bitwise_and))
                step(dve.tensor_copy(hi[:, :, :], hi_i[:, :, :]))
                step(dve.tensor_copy(lo[:, :, :], lo_i[:, :, :]))
                step(dve.scalar_tensor_tensor(out=hi[:, :, :], in0=hi[:, :, :], scalar=1.0, in1=sel[:, :, :],
                                              op0=ALU.add, op1=ALU.mult))
                dve.wait_ge(rows_stored, 16 * B)
                for t in range(0, T, 4):
                    for e_major, table, pick, width in ((hi, count_hi, pick_hi, HI), (lo, count_lo, pick_lo, LO)):
                        for tt in range(t, t + 4):
                            ins = dve.tensor_tensor(pick[:, tt, :, :], e_major[:, :, tt:tt + 1].broadcast_to([P, E, width]),
                                                    table.unsqueeze(1).broadcast_to([P, E, width]), ALU.is_equal)
                    step(ins)
                    for tt in range(t, t + 4):
                        ins = dve.tensor_scalar(pick_lo[:, tt, :, :], pick_lo[:, tt, :, :], tok[:, tt:tt + 1], None, ALU.mult)
                    ins.then_inc(picks_ready, 1)
                dve.wait_ge(picked, 1)
                step(dve.tensor_tensor(own[:, :, :], idx_ps[:, 0:E * LO].rearrange("p (e l) -> p e l", e=E),
                                       diag[:, :, :], ALU.mult))
                dve.tensor_reduce(folded[:, :], own[:, :, :].rearrange("p e l -> p l e"), AX.X, ALU.add).then_inc(folded_ready, 1)
                dve.wait_ge(idx_turned, 1)
                for r in range(4):
                    dve.tensor_copy(idx[32 * r:32 * r + 32, :], idxT_ps[0:32, 0:P].rearrange("l (c r) -> l c r", r=4)[:, :, r])\
                       .then_inc(idx_ready, 1)

            @block.scalar
            def _(act):
                for n in range(2 * B):
                    act.wait_ge(turned, n + 1)
                    act.activation(xT[:, (n // 2) % 2, n % 2, :], turn_ps[n % 3][:, :], ACT.Copy).then_inc(turned_kept, 1)
                act.wait_ge(shifted, 1)
                act.activation(logits[:, :, :], logits[:, :, :], ACT.Exp).then_inc(exps_done, 1)

            @block.tensor
            def _(pe):
                pe.wait_ge(consts_made, 1)
                pe.wait_ge(router_loaded, 32)

                def turn(b):
                    pe.wait_ge(xn_ready, 4 * b + 4)
                    for c in range(2):
                        n = 2 * b + c
                        if n >= 3:
                            pe.wait_ge(turned_kept, n - 2)
                        for i in range(NT):
                            ins = pe.transpose(turn_ps[n % 3][:, i * P:(i + 1) * P], xn[:, b, i, c * P:(c + 1) * P], ident[:, :])
                        ins.then_inc(turned, 1)

                def route(b):
                    pe.wait_ge(turned_kept, 2 * b + 2)
                    for i in range(NT):
                        for c in range(2):
                            ins = pe.matmul(logit_ps[:, (4 * b + i) * E:(4 * b + i + 1) * E],
                                            xT[:, b % 2, c, i * P:(i + 1) * P], wr[:, c, :], start=c == 0, stop=c == 1)
                    ins.then_inc(logits_done, 1)

                turn(0)
                for b in range(B):
                    if b + 1 < B:
                        turn(b + 1)
                    route(b)
                with pe.Fori(0, BITS // 2) as k:
                    pe.wait_ge(over_ready, k + 1)
                    pe.matmul(count_ps[:, 0:2 * E * T], ones_b[:, :], over[:, 0:2, :, :].rearrange("p n e t -> p (n e t)"),
                              start=True, stop=True)
                    pe.matmul(count_ps[:, 2 * E * T:3 * E * T], ones_b[:, :], over[:, 2, :, :].rearrange("p e t -> p (e t)"),
                              start=True, stop=True).then_inc(over_counted, 1)
                flat = [m.rearrange("p e t -> p (e t)") for m in (gt[:, :, :], eq[:, :, :], over[:, 0, :, :])]
                pe.wait_ge(mask_ready, 1)
                pe.matmul(count_ps[:, 0:E * T], ones_b[:, :], flat[0], start=True, stop=True)
                pe.matmul(rank_ps[:, 0:256], before[:, :], flat[1], start=True, stop=True)
                pe.matmul(rank_ps[:, 256:512], ones_b[:, :], flat[1], start=True, stop=True).then_inc(mask_counted, 1)
                pe.wait_ge(mask_ready, 2)
                pe.matmul(rank_ps[:, 0:256], before[:, :], flat[2], start=True, stop=True)
                pe.matmul(rank_ps[:, 256:512], ones_b[:, :], flat[2], start=True, stop=True).then_inc(mask_counted, 1)
                for t in range(T):
                    if t % 4 == 0:
                        pe.wait_ge(picks_ready, t // 4 + 1)
                    ins = pe.matmul(idx_ps[:, 0:E * LO], pick_hi[:, t, :, :].rearrange("p e h -> p (e h)"),
                                    pick_lo[:, t, :, :].rearrange("p e l -> p (e l)"), start=t == 0, stop=t == T - 1)
                ins.then_inc(picked, 1)
                pe.wait_ge(folded_ready, 1)
                pe.transpose(idxT_ps[0:LO, 0:P], folded[:, :], ident[:, :]).then_inc(idx_turned, 1)

    taken = [sb(f"taken{i}", [P, Q, ROW]) for i in range(2)]
    takenT = sb("takenT", [P, 2, CAP])
    made = [sb(f"made{i}", [P, Q, C]) for i in range(2)]
    turn_ps = [outer.enter_context(nc.psum_tensor(f"exp_turn{i}", [P, 512], F32)) for i in range(2)]
    up_ps = [outer.enter_context(nc.psum_tensor(f"exp_up{i}", [P, 512], F32)) for i in range(2)]
    down_ps = [outer.enter_context(nc.psum_tensor(f"exp_down{i}", [P, 512], F32)) for i in range(2)]
    gathered = [sem(f"gathered{i}") for i in range(2)]
    added, turned2, turned2_kept, up_done, silu_done, down_done, made_ready = (
        sem("e_" + n) for n in ("added", "turned", "turned_kept", "up_done", "silu_done", "down_done", "made_ready"))
    out_rows = out.rearrange("b n c -> (b n) c")

    with nc.Block() as block:
        @block.gpsimd
        def _(pool):
            def gather(e):
                if e >= 2:
                    pool.wait_ge(made_ready, Q * (e - 1))
                for q in range(Q):
                    pool.indirect_dma_start(
                        out=taken[e % 2][:, q, :], out_offset=None, in_=rows[:, :],
                        in_offset=bass.IndirectOffsetOnAxis(ap=idx[:, e * Q + q:e * Q + q + 1], axis=0),
                        ).then_inc(gathered[e % 2], 16)

            gather(0)
            for e in range(E):
                if e + 1 < E:
                    gather(e + 1)
                if e >= 1:
                    pool.wait_ge(added, 16 * Q * e)
                for q in range(Q):
                    pool.wait_ge(made_ready, Q * e + q + 1)
                    pool.indirect_dma_start(
                        out=out_rows, out_offset=bass.IndirectOffsetOnAxis(ap=idx[:, e * Q + q:e * Q + q + 1], axis=0),
                        in_=made[e % 2][:, q, :], in_offset=None, compute_op=ALU.add).then_inc(added, 16)
            pool.wait_ge(added, 16 * Q * E)

        @block.tensor
        def _(pe):
            def turn(e):
                pe.wait_ge(gathered[e % 2], 16 * Q * (e // 2 + 1))
                for c in range(2):
                    for q in range(Q):
                        ins = pe.transpose(turn_ps[c][:, q * P:(q + 1) * P], taken[e % 2][:, q, c * P:(c + 1) * P], ident[:, :])
                    ins.then_inc(turned2, 1)

            def up(e):
                pe.wait_ge(turned2_kept, 2 * e + 2)
                for f in range(FT):
                    n = FT * e + f
                    if n >= 2:
                        pe.wait_ge(silu_done, n - 1)
                    w = P if f < FT - 1 else FR
                    for c in range(2):
                        ins = pe.matmul(up_ps[n % 2][0:w, :], w_up[:, e // PER_GROUP, c, f * P:f * P + w], takenT[:, c, :],
                                        start=c == 0, stop=c == 1)
                    ins.then_inc(up_done, 1)

            def down(e):
                pe.wait_ge(silu_done, FT * e + FT)
                for q in range(Q):
                    n = Q * e + q
                    if n >= 2:
                        pe.wait_ge(made_ready, n - 1)
                    for f in range(FT):
                        w = P if f < FT - 1 else BIAS_ROW + 1
                        ins = pe.matmul(down_ps[n % 2][:, 0:C], mid[0:w, f, q * P:(q + 1) * P], w_down[0:w, e, f, :],
                                        start=f == 0, stop=f == FT - 1)
                    ins.then_inc(down_done, 1)

            pe.wait_ge(up_loaded, 16 * UP_DMAS)
            pe.wait_ge(down_loaded, 16 * DOWN_DMAS)
            turn(0)
            for e in range(E):
                up(e)
                if e + 1 < E:
                    turn(e + 1)
                down(e)

        @block.scalar
        def _(act):
            act.wait_ge(up_loaded, 16 * UP_DMAS)
            for e in range(E):
                for f in range(FT):
                    n = FT * e + f
                    w = P if f < FT - 1 else FR
                    act.wait_ge(up_done, n + 1)
                    act.activation(mid[0:w, f, :], up_ps[n % 2][0:w, :], ACT.Silu,
                                   bias=b_up[0:w, e // PER_GROUP, f:f + 1]).then_inc(silu_done, 1)

        @block.vector
        def _(dve):
            def keep_turned(e):
                for c in range(2):
                    dve.wait_ge(turned2, 2 * e + c + 1)
                    dve.wait_ge(up_done, FT * e) if e else None
                    dve.tensor_copy(takenT[:, c, :], turn_ps[c][:, :]).then_inc(turned2_kept, 1)

            keep_turned(0)
            for e in range(E):
                if e + 1 < E:
                    keep_turned(e + 1)
                if e >= 2:
                    dve.wait_ge(added, 16 * Q * (e - 1))
                for q in range(Q):
                    n = Q * e + q
                    dve.wait_ge(down_done, n + 1)
                    dve.tensor_scalar(made[e % 2][:, q, :], down_ps[n % 2][:, 0:C], taken[e % 2][:, q, C + e:C + e + 1],
                                      None, ALU.mult).then_inc(made_ready, 1)


def make_consts(nc, stack):
    def sb(n, shape, dt=F32):
        return stack.enter_context(nc.sbuf_tensor(n, shape, dt))

    c = {"ident": sb("ident", [P, P]), "ones": sb("ones", [P, P]), "spread": sb("spread", [P, P], F16),
         "ident_b": sb("ident_b", [P, P], BF16), "mask_qk": sb("mask_qk", [P, P], BF16),
         "mask_kq": sb("mask_kq", [P, P], BF16)}
    cleared, made = stack.enter_context(nc.semaphore("cleared")), stack.enter_context(nc.semaphore("made"))
    with nc.Block() as block:
        @block.gpsimd
        def _(pool):
            for n, v in (("ident", 0.0), ("spread", 0.0), ("ident_b", 0.0), ("mask_qk", 0.0), ("mask_kq", 0.0),
                         ("ones", 1.0)):
                pool.memset(c[n][:, :], v).then_inc(cleared, 1)
            pool.wait_ge(cleared, 6)
            for n in ("ident", "ident_b"):
                pool.affine_select(out=c[n][:, :], in_=c[n][:, :], compare_op=ALU.not_equal, fill=1.0, base=0,
                                   pattern=[[-1, P]], channel_multiplier=1).then_inc(made, 1)
            s = c["spread"][:, :].rearrange("p (j m) -> p j m", j=4)
            for n, base in enumerate((0, -4)):
                pool.affine_select(out=s, in_=s, compare_op=ALU.not_equal, fill=1.0 / RINV_SCALE, base=base,
                                   pattern=[[-1, 4], [0, 32]], channel_multiplier=1).then_inc(made, 1)
                pool.wait_ge(made, 3 + n)
            pool.affine_select(out=c["mask_qk"][:, :], in_=c["mask_qk"][:, :], compare_op=ALU.is_ge, fill=MASKED,
                               base=0, pattern=[[-1, P]], channel_multiplier=1).then_inc(made, 1)
            pool.affine_select(out=c["mask_kq"][:, :], in_=c["mask_kq"][:, :], compare_op=ALU.is_ge, fill=MASKED,
                               base=0, pattern=[[1, P]], channel_multiplier=-1).then_inc(made, 1)
            pool.wait_ge(made, 6)
    return c


def clear_guard(nc, stack, guard, flag_i):
    cleared = stack.enter_context(nc.semaphore("guard_cleared"))
    with nc.Block() as block:
        @block.gpsimd
        def _(pool):
            for n in ("highest", "lowest", "nan"):
                pool.memset(guard[n][:, :], 0.0).then_inc(cleared, 1)
            pool.memset(flag_i[:, :], 0).then_inc(cleared, 1)
            pool.wait_ge(cleared, 4)


def raise_flag(nc, guard, flag_i, consts, which):
    with ExitStack() as s:
        steps, summed = (s.enter_context(nc.semaphore(f"flag{which}_{n}")) for n in ("steps", "summed"))
        cell = s.enter_context(nc.sbuf_tensor(f"flag{which}_cell", [P, 3, 16], F32))
        total = s.enter_context(nc.sbuf_tensor(f"flag{which}_total", [P, 1], F32))
        flag_ps = s.enter_context(nc.psum_tensor(f"flag{which}_ps", [P, 512], F32))
        with nc.Block() as block:
            @block.vector
            def _(dve):
                dve.tensor_scalar(cell[:, 0, :], guard["highest"][:, :], 4.0 * CLAMP, None, ALU.is_gt).then_inc(steps, 1)
                dve.tensor_scalar(cell[:, 1, :], guard["lowest"][:, :], -4.0 * (CLAMP - 110.0), None, ALU.is_lt).then_inc(steps, 1)
                dve.tensor_copy(cell[:, 2, :], guard["nan"][:, :]).then_inc(steps, 1)
                dve.wait_ge(steps, 3)
                dve.tensor_reduce(total[:, :], cell[:, 2 * which:, :].rearrange("p a b -> p (a b)"), AX.X, ALU.max).then_inc(steps, 1)
                dve.memset(guard["nan"][:, :], 0.0).then_inc(steps, 1)
                dve.wait_ge(summed, 1)
                dve.tensor_copy(flag_i[:, which:which + 1], flag_ps[:, 0:1]).then_inc(steps, 1)
                dve.wait_ge(steps, 6)

            @block.tensor
            def _(pe):
                pe.wait_ge(steps, 4)
                pe.matmul(flag_ps[:, 0:1], consts["ones"][:, :], total[:, :], start=True, stop=True).then_inc(summed, 1)


def restore(nc, name, x, kept):
    with ExitStack() as s:
        loaded = s.enter_context(nc.semaphore(f"{name}_x_loaded"))
        with nc.Block() as block:
            @block.sync
            def _(sp):
                for b in range(x.shape[1]):
                    sp.dma_start(x[:, b, :, :], kept[b].rearrange("(t p) c -> p t c", p=P)).then_inc(loaded, 16)
                sp.wait_ge(loaded, 16 * x.shape[1])


def decoder_block(nc, a, out, until=3):
    B, N, C = a["x"].shape
    with ExitStack() as whole:
        x = whole.enter_context(nc.sbuf_tensor("x_sb", [P, B, N // P, C], F32))
        flag_i = whole.enter_context(nc.sbuf_tensor("flag_i", [P, 2], I32))
        with ExitStack() as s:
            consts = make_consts(nc, s)
            with ExitStack() as phase:
                attention(nc, phase, "self", False, x, a["x"], {n: a["L0_attn_" + n] for n in ("Wq", "Wk", "Wv", "Wo")}, consts)
            if until >= 2:
                ctx = a["ctx_768"]
                w = {n: a["L0_xattn_" + n] for n in ("Wq", "Wk", "Wv", "Wo", "bq", "bk", "bv", "bo")}
                kept = nc.dram_tensor("x_kept", [B, N, C], F32).ap()
                guard = {n: s.enter_context(nc.sbuf_tensor("guard_" + n, [P, 16], F32)) for n in ("highest", "lowest", "nan")}
                clear_guard(nc, s, guard, flag_i)
                with ExitStack() as phase:
                    attention(nc, phase, "cross", True, x, ctx, w, consts, guard, "plain", kept)
                raise_flag(nc, guard, flag_i, consts, 0)
                flag = nc.values_load(flag_i[0:1, 0:1], min_val=0, max_val=P)
                with nc.If(flag > 0):
                    nc.all_engine_barrier()
                    restore(nc, "clip", x, kept)
                    with ExitStack() as phase:
                        attention(nc, phase, "clip", True, x, ctx, w, consts, guard, "clip")
                    raise_flag(nc, guard, flag_i, consts, 1)
                flag = nc.values_load(flag_i[0:1, 1:2], min_val=0, max_val=P)
                with nc.If(flag > 0):
                    nc.all_engine_barrier()
                    restore(nc, "uniform", x, kept)
                    with ExitStack() as phase:
                        attention(nc, phase, "uniform", True, x, ctx, w, consts, guard, "uniform")
        if until < 3:
            st = whole.enter_context(nc.semaphore("st"))
            with nc.Block() as block:
                @block.sync
                def _(sp):
                    for b in range(B):
                        sp.dma_start(out[b].rearrange("(t p) c -> p t c", p=P), x[:, b, :, :]).then_inc(st, 16)
                    sp.wait_ge(st, 16 * B)
        else:
            expert_choice(nc, whole, x, a, out)


_INS = ["x", "ctx_768", "L0_attn_Wq", "L0_attn_Wk", "L0_attn_Wv", "L0_attn_Wo", "L0_xattn_Wq", "L0_xattn_bq",
        "L0_xattn_Wk", "L0_xattn_bk", "L0_xattn_Wv", "L0_xattn_bv", "L0_xattn_Wo", "L0_xattn_bo", "L0_ffn_Wr",
        "L0_ffn_br", "L0_ffn_W_up", "L0_ffn_b_up", "L0_ffn_W_down", "L0_ffn_b_down"]
_OUTS = [((8, 512, 256), "float32")]


def kernel(**inputs):
    import numpy as _np
    import concourse.bacc as _bacc
    from concourse import mybir as _mybir
    from concourse.bass_utils import run_bass_kernel_spmd as _run

    nc = _bacc.Bacc("TRN2", target_bir_lowering=False, num_devices=1)
    arrays, args = {}, {}
    for name in _INS:
        v = _np.ascontiguousarray(inputs[name])
        arrays[f"in_{name}_dram"] = v
        args[name] = nc.dram_tensor(f"in_{name}_dram", v.shape, _mybir.dt.from_np(v.dtype), kind="ExternalInput").ap()
    (shape, dtype), = _OUTS
    out = nc.dram_tensor("out_0_dram", shape, _mybir.dt.from_np(_np.dtype(dtype)), kind="ExternalOutput").ap()
    decoder_block(nc, args, out)
    r = _run(nc, [arrays], core_ids=[0])
    return r.results[0]["out_0_dram"]
```
